# Optimizing a Trainium2 kernel written in Bass

```python
import numpy as np
import jax
import jax.numpy as jnp

def _softmax(x, axis=-1):
    return jax.nn.softmax(x, axis=axis)

def _gelu(x):
    return jax.nn.gelu(x, approximate=True)

def _silu(x):
    return jax.nn.silu(x)

def _sigmoid(x):
    return jax.nn.sigmoid(x)

def _layernorm(x, axis=-1, eps=1e-05):
    m = jnp.mean(x, axis=axis, keepdims=True)
    v = jnp.var(x, axis=axis, keepdims=True)
    return (x - m) / jnp.sqrt(v + eps)

def _scatter_add(tgt, idx, src, axis=0):
    return tgt.at[idx].add(src)

def _segment_sum(src, seg, n):
    return jax.ops.segment_sum(src, seg, n)
kernel_name = 'mk_seq_preln_d2_jaxref_r8_10a7f3'

def setup_inputs(seed: int=0):
    np.random.seed(seed)
    _w = jnp.asarray

    def _L0_attn_setup():
        import jax, jax.numpy as jnp
        import numpy as np
        NH = 16
        key = jax.random.key(seed)
        ks = jax.random.split(key, 5)
        B, T, D = (2, 256, 256)
        scale = 0.02
        return {'x': jax.random.normal(ks[0], (B, T, D), dtype=jnp.float32), 'Wq': jax.random.normal(ks[1], (D, D), dtype=jnp.float32) * scale, 'Wk': jax.random.normal(ks[2], (D, D), dtype=jnp.float32) * scale, 'Wv': jax.random.normal(ks[3], (D, D), dtype=jnp.float32) * scale, 'Wo': jax.random.normal(ks[4], (D, D), dtype=jnp.float32) * scale}
    _L0_attn_in = _L0_attn_setup()

    def _L0_ffn_setup():
        import jax, jax.numpy as jnp
        import numpy as np
        D_MODEL = 256
        D_EXPERT = 1024
        EPS = 1e-08

        def ternary_quant(w):
            scale = jnp.mean(jnp.abs(w)) + EPS
            q = jnp.clip(jnp.round(w / scale), -1.0, 1.0) * scale
            return w + jax.lax.stop_gradient(q - w)
        key = jax.random.key(seed)
        k_x, k_up, k_gate, k_down = jax.random.split(key, 4)
        std_in = 1.0 / np.sqrt(D_MODEL)
        std_exp = 1.0 / np.sqrt(D_EXPERT)
        return {'x': jax.random.normal(k_x, (4, 256, D_MODEL), dtype=jnp.float32), 'W_up': jax.random.normal(k_up, (D_EXPERT, D_MODEL), dtype=jnp.float32) * std_in, 'W_gate': jax.random.normal(k_gate, (D_EXPERT, D_MODEL), dtype=jnp.float32) * std_in, 'W_down': jax.random.normal(k_down, (D_MODEL, D_EXPERT), dtype=jnp.float32) * std_exp}
    _L0_ffn_in = _L0_ffn_setup()

    def _L1_attn_setup():
        import jax, jax.numpy as jnp
        import numpy as np
        B, S, H = (4, 256, 256)
        key = jax.random.key(seed)
        k1, k2, k3 = jax.random.split(key, 3)
        xav_qkv = float(np.sqrt(6.0 / (H + 3 * H)))
        xav_out = float(np.sqrt(6.0 / (H + H)))
        return {'hidden_states': jax.random.normal(k1, (B, S, H), dtype=jnp.float32), 'w_qkv': jax.random.uniform(k2, (3 * H, H), minval=-xav_qkv, maxval=xav_qkv, dtype=jnp.float32), 'b_qkv': jnp.zeros((3 * H,), dtype=jnp.float32), 'w_out': jax.random.uniform(k3, (H, H), minval=-xav_out, maxval=xav_out, dtype=jnp.float32), 'b_out': jnp.zeros((H,), dtype=jnp.float32)}
    _L1_attn_in = _L1_attn_setup()

    def _L1_ffn_setup():
        import jax, jax.numpy as jnp
        import numpy as np
        TOP_K = 4
        key = jax.random.key(seed)
        ks = jax.random.split(key, 9)
        B, T, D, H, NE = (2, 128, 256, 176, 16)
        s = 0.02
        return {'x': jax.random.normal(ks[0], (B, T, D), jnp.float32), 'gate_w': jax.random.normal(ks[1], (NE, D), jnp.float32) * s, 'gate_b': jax.random.normal(ks[2], (NE,), jnp.float32) * s, 'w1_shared': jax.random.normal(ks[3], (D, H), jnp.float32) * s, 'w2_shared': jax.random.normal(ks[4], (H, D), jnp.float32) * s, 'w3_shared': jax.random.normal(ks[5], (D, H), jnp.float32) * s, 'w1_routed': jax.random.normal(ks[6], (NE, D, H), jnp.float32) * s, 'w2_routed': jax.random.normal(ks[7], (NE, H, D), jnp.float32) * s, 'w3_routed': jax.random.normal(ks[8], (NE, D, H), jnp.float32) * s}
    _L1_ffn_in = _L1_ffn_setup()
    _d = {'L0_attn_x': _L0_attn_in['x'], 'L0_attn_Wq': _L0_attn_in['Wq'], 'L0_attn_Wk': _L0_attn_in['Wk'], 'L0_attn_Wv': _L0_attn_in['Wv'], 'L0_attn_Wo': _L0_attn_in['Wo'], 'L0_ffn_W_up': _L0_ffn_in['W_up'], 'L0_ffn_W_gate': _L0_ffn_in['W_gate'], 'L0_ffn_W_down': _L0_ffn_in['W_down'], 'L1_attn_w_qkv': _L1_attn_in['w_qkv'], 'L1_attn_b_qkv': _L1_attn_in['b_qkv'], 'L1_attn_w_out': _L1_attn_in['w_out'], 'L1_attn_b_out': _L1_attn_in['b_out'], 'L1_ffn_gate_w': _L1_ffn_in['gate_w'], 'L1_ffn_gate_b': _L1_ffn_in['gate_b'], 'L1_ffn_w1_shared': _L1_ffn_in['w1_shared'], 'L1_ffn_w2_shared': _L1_ffn_in['w2_shared'], 'L1_ffn_w3_shared': _L1_ffn_in['w3_shared'], 'L1_ffn_w1_routed': _L1_ffn_in['w1_routed'], 'L1_ffn_w2_routed': _L1_ffn_in['w2_routed'], 'L1_ffn_w3_routed': _L1_ffn_in['w3_routed']}
    _x0 = _d['L0_attn_x']
    _d['L0_attn_x'] = jax.random.normal(jax.random.fold_in(jax.random.key(seed), 1), (4, 512, 256), dtype=_x0.dtype)
    del _x0
    return _d

def reference(L0_attn_x, L0_attn_Wq, L0_attn_Wk, L0_attn_Wv, L0_attn_Wo, L0_ffn_W_up, L0_ffn_W_gate, L0_ffn_W_down, L1_attn_w_qkv, L1_attn_b_qkv, L1_attn_w_out, L1_attn_b_out, L1_ffn_gate_w, L1_ffn_gate_b, L1_ffn_w1_shared, L1_ffn_w2_shared, L1_ffn_w3_shared, L1_ffn_w1_routed, L1_ffn_w2_routed, L1_ffn_w3_routed):

    def _L0_attn_ref(x, Wq, Wk, Wv, Wo):
        import jax, jax.numpy as jnp
        import numpy as np
        NH = 16
        B, T, D = x.shape
        hd = D // NH
        q = (x @ Wq.T).reshape(B, T, NH, hd).transpose(0, 2, 1, 3)
        k = (x @ Wk.T).reshape(B, T, NH, hd).transpose(0, 2, 1, 3)
        v = (x @ Wv.T).reshape(B, T, NH, hd).transpose(0, 2, 1, 3)
        att = jnp.einsum('bhtd,bhsd->bhts', q, k) / jnp.sqrt(jnp.asarray(hd, x.dtype))
        neg = jnp.finfo(att.dtype).min
        mask = jnp.triu(jnp.full((T, T), neg, dtype=att.dtype), k=1)
        att = att + mask
        w = jax.nn.softmax(att, axis=-1)
        z = jnp.einsum('bhts,bhsd->bhtd', w, v)
        z = z.transpose(0, 2, 1, 3).reshape(B, T, D)
        return z @ Wo.T

    def _L0_ffn_ref(x, W_up, W_gate, W_down):
        import jax, jax.numpy as jnp
        import numpy as np
        D_MODEL = 256
        D_EXPERT = 1024
        EPS = 1e-08

        def ternary_quant(w):
            scale = jnp.mean(jnp.abs(w)) + EPS
            q = jnp.clip(jnp.round(w / scale), -1.0, 1.0) * scale
            return w + jax.lax.stop_gradient(q - w)
        wu = ternary_quant(W_up)
        wg = ternary_quant(W_gate)
        wd = ternary_quant(W_down)
        up = jnp.einsum('bsd,ed->bse', x, wu)
        gate = jnp.einsum('bsd,ed->bse', x, wg)
        hidden = jax.nn.silu(up) * gate
        return jnp.einsum('bse,de->bsd', hidden, wd)

    def _L1_attn_ref(hidden_states, w_qkv, b_qkv, w_out, b_out):
        import jax, jax.numpy as jnp
        import numpy as np
        B, S, H = (4, 256, 256)
        Bc, Sc, Hc = hidden_states.shape
        scaling = jnp.sqrt(jnp.asarray(Hc, hidden_states.dtype))
        qkv = jnp.einsum('bsh,oh->bso', hidden_states, w_qkv) + b_qkv
        q, k, v = jnp.split(qkv, 3, axis=-1)
        scores = jnp.einsum('bqh,bkh->bqk', q, k) / scaling
        probs = jax.nn.softmax(scores, axis=-1)
        context = jnp.einsum('bqk,bkh->bqh', probs, v)
        out = jnp.einsum('bsh,oh->bso', context, w_out) + b_out
        return out

    def _L1_ffn_ref(x, gate_w, gate_b, w1_shared, w2_shared, w3_shared, w1_routed, w2_routed, w3_routed):
        import jax, jax.numpy as jnp
        import numpy as np
        TOP_K = 4
        n_experts = w1_routed.shape[0]
        logits = jnp.einsum('ed,btd->bte', gate_w, x)
        scores = jax.nn.sigmoid(logits) + gate_b
        weights, indices = jax.lax.top_k(scores, TOP_K)
        weights = weights / weights.sum(-1, keepdims=True)
        shared_out = jax.nn.silu(x @ w1_shared) * (x @ w3_shared) @ w2_shared
        one_hot = jax.nn.one_hot(indices, n_experts, dtype=x.dtype)
        router_probs = (weights[..., None] * one_hot).sum(-2)
        h1 = jnp.einsum('btd,edc->btec', x, w1_routed)
        h2 = jnp.einsum('btd,edc->btec', x, w3_routed)
        h3 = jax.nn.silu(h1 * h2)
        experts_out = jnp.einsum('btec,ecd->bted', h3, w2_routed)
        routed_out = jnp.einsum('bted,bte->btd', experts_out, router_probs)
        return shared_out + routed_out
    x = L0_attn_x
    x = x + _L0_attn_ref(_layernorm(x, axis=-1), L0_attn_Wq, L0_attn_Wk, L0_attn_Wv, L0_attn_Wo)
    x = x + _L0_ffn_ref(_layernorm(x, axis=-1), L0_ffn_W_up, L0_ffn_W_gate, L0_ffn_W_down)
    x = x + _L1_attn_ref(_layernorm(x, axis=-1), L1_attn_w_qkv, L1_attn_b_qkv, L1_attn_w_out, L1_attn_b_out)
    x = x + _L1_ffn_ref(_layernorm(x, axis=-1), L1_ffn_gate_w, L1_ffn_gate_b, L1_ffn_w1_shared, L1_ffn_w2_shared, L1_ffn_w3_shared, L1_ffn_w1_routed, L1_ffn_w2_routed, L1_ffn_w3_routed)
    return x

_drawn_inputs = setup_inputs


def setup_inputs(seed=0):
    import zlib

    import numpy as np

    out = dict(_drawn_inputs(seed))
    spreads = {'L1_attn_b_qkv': (0.0, 0.1), 'L1_attn_b_out': (0.0, 0.1)}
    factors = {'L0_attn_Wq': 8.0,
     'L0_attn_Wk': 8.0,
     'L0_attn_Wv': 4.538,
     'L0_attn_Wo': 4.68,
     'L1_ffn_gate_w': 8.0,
     'L1_ffn_gate_b': 8.0,
     'L1_ffn_w1_shared': 4.251,
     'L1_ffn_w2_shared': 4.196,
     'L1_ffn_w3_shared': 4.171,
     'L1_ffn_w1_routed': 8.0,
     'L1_ffn_w2_routed': 8.0,
     'L1_ffn_w3_routed': 8.0}
    for name, (base, spread) in spreads.items():
        noise = np.random.default_rng([zlib.crc32(name.encode()), seed]).standard_normal(out[name].shape)
        drawn = base * np.exp(spread * noise) if base else spread * noise
        out[name] = jnp.asarray(drawn.astype(out[name].dtype))
    for name, factor in factors.items():
        out[name] = (out[name] * factor).astype(out[name].dtype)
    return out
```

```python
from contextlib import ExitStack

import concourse.bass as bass
from concourse import mybir

ALU = mybir.AluOpType
ACT = mybir.ActivationFunctionType
F32 = mybir.dt.float32
F32R = mybir.dt.float32r
BF16 = mybir.dt.bfloat16
X = mybir.AxisListType.X

P = 128
D = 256
KH = D // P
B, T = 4, 512
TJ = T // P
NTOK = B * T
NH, HD = 16, 16
NP = NH // 2
HS = 64
Q_LO, K_LO, AUX = 16, 32, 48
FF = 1024
FM = FF // P
NE, EH = 16, 176
HID = NE * EH
TOP_K = 4
PAIR = 2 * P
NPAIRS = 1 + HID // PAIR
NEG = -1.0e30
EPS = 1e-5
TEPS = 1e-8
LOGIT_PAD = 20

XT_LN0, XT_Z, XT_LN1, XT_LN2, XT_CTX, XT_LN3 = range(6)
LAG = 2
T_BANK, PO_BANK = 6, 7


def attention_order():
    order = []
    for s in range(-1, NP + LAG + 1):
        done = s - LAG - 1
        if done >= 0 and done % 2:
            order.append(("copy_out", done // 2, 0))
        if s + 1 < NP:
            order.append(("turn_k", s + 1, 0))
        for u in range(TJ):
            if 0 <= s < NP:
                order.append(("score", s, u))
            if u == 0 and s + 1 < NP:
                order.append(("turn_q", s + 1, 0))
            if u == 1 and 0 <= s - 1 < NP:
                order.append(("turn_shifted_q", s - 1, 0))
            if 0 <= s - LAG < NP:
                order.append(("scoreT", s - LAG, u))
                if u:
                    order.append(("value", s - LAG, u - 1))
            if u == 2 and done >= 0 and done % 2:
                order.append(("turn_out", done // 2, 0))
        if 0 <= s - LAG < NP:
            order.append(("value", s - LAG, TJ - 1))
    return order


ORDER = attention_order()
UNITS = [x for x in ORDER if x[0] in ("score", "scoreT")]
TURNS = [x for x in ORDER if x[0].startswith("turn")]
TURN_READS = {"turn_k": 2, "turn_q": 1, "turn_shifted_q": 1, "turn_out": 1}
N_TURN_READS = sum(TURN_READS[k] for k, _, _ in TURNS)


def turn_reads(event):
    n = TURNS.index(event)
    return sum(TURN_READS[k] for k, _, _ in TURNS[: n + 1])


def unit_slot(unit):
    return UNITS.index(unit) % 3


def layers(nc, x, wqkv0, wo0, w_up, w_gate, w_down, wqkv1, bqk1, bv1, wo1, bo1, gate_w, gate_b,
           x3_d, xt4_d, probs_d):
    with ExitStack() as ctx:
        def sb(name, shape, dt=F32):
            return ctx.enter_context(nc.sbuf_tensor(name, shape, dt))

        def sem(name):
            return ctx.enter_context(nc.semaphore(name))

        ps = ctx.enter_context(nc.psum_tensor("ps", [P, 8, 512], F32))

        wq0 = sb("wq0", [P, 2, KH, 3 * D], F32R)
        wo0s = sb("wo0s", [P, 2, KH, D], F32R)
        wq1 = sb("wq1", [P, 2, KH, 3 * D], F32R)
        wo1s = sb("wo1s", [P, 2, KH, D], F32R)
        gws = sb("gws", [P, 2, KH, NE], F32R)
        tup = sb("tup", [P, KH, FF], F32R)
        tgate = sb("tgate", [P, KH, FF], F32R)
        tdown = sb("tdown", [P, FM, D], F32R)
        stage = sb("stage", [P, 2, 2048])
        below = sb("below", [P, 1024])
        absout = sb("absout", [P, 2048], BF16)
        abssum = sb("abssum", [P, 3])
        abstot = sb("abstot", [P, 3])
        meaneps = sb("meaneps", [P, 3])
        tscale = sb("tscale", [P, 3])
        thalf = sb("thalf", [P, 3])
        tnhalf = sb("tnhalf", [P, 3])
        tsgd = sb("tsgd", [P, 1])
        bqk = sb("bqk", [P, 4])
        bv = sb("bv", [P, 2])
        bo = sb("bo", [P, D])
        gb = sb("gb", [P, NE])

        ident = sb("ident", [P, P])
        identb = sb("identb", [P, P], BF16)
        mask_q = sb("mask_q", [P, P], BF16)
        mask_k = sb("mask_k", [P, P], BF16)
        epsc = sb("epsc", [P, TJ])
        halfc = sb("halfc", [P, TJ])

        xin = sb("xin", [P, TJ, D])
        xres = sb("xres", [P, TJ, D])
        xn = sb("xn", [P, TJ, D])
        xt = sb("xt", [P, 2, KH, T], F32R)
        big = sb("big", [P, 8192], F32R)
        vh = sb("vh", [P, TJ, NH, 32])
        ka = sb("ka", [P, 4, T], F32R)
        kb = sb("kb", [P, 4, T], F32R)
        q1 = sb("q1", [P, 2, T], F32R)
        q2 = sb("q2", [P, 2, T], F32R)
        pt = sb("pt", [P, 3, 2, T])
        ot = sb("ot", [P, 2, T])
        v1 = sb("v1", [P, 2, TJ, D], F32R)

        fence = sb("fence", [P, 1])
        pfence = sb("pfence", [P, 1])
        stats = sb("stats", [P, TJ, 6])
        mv = sb("mv", [P, TJ, 2])
        vareps = sb("vareps", [P, TJ])
        rstd = sb("rstd", [P, TJ])
        negm = sb("negm", [P, 2, TJ, 2])
        zinv = sb("zinv", [P, TJ, 4])
        nm1 = sb("nm1", [P, TJ])
        nm1s = sb("nm1s", [P, TJ])
        rs1 = sb("rs1", [P, TJ])
        ri1 = sb("ri1", [P, TJ])
        elog = sb("elog", [P, TJ, NE])
        score = sb("score", [P, TJ, LOGIT_PAD])
        top8 = sb("top8", [P, TJ, 8])
        top4 = sb("top4", [P, TJ, 8])
        topsum = sb("topsum", [P, TJ])
        topinv = sb("topinv", [P, TJ])
        rest = sb("rest", [P, TJ, LOGIT_PAD])
        prob = sb("prob", [P, TJ, NE])
        probs = sb("probs", [P, TJ, P], F32R)
        probt = sb("probt", [P, T], F32R)

        qkt = big[:, :].rearrange("p (j h c) -> p j h c", j=TJ, h=2 * NH)
        hs = big[:, :].rearrange("p (l m t) -> p l m t", l=2, m=FM)
        qk1 = big[:, 0:4096].rearrange("p (l m t) -> p l m t", l=2, m=4)
        ptr = big[:, 4096:8192].rearrange("p (l m t) -> p l m t", l=2, m=TJ)
        gated = pt[:, 0]
        hid = pt[:, 1]
        p1 = pt[:, 0:2].rearrange("p a h t -> p (a h) t")

        w_loaded = [sem("w_loaded_even"), sem("w_loaded_odd")]
        bias_loaded = sem("bias_loaded")
        qkv0_split = sem("qkv0_split")
        split = sem("split")
        split_end = sem("split_end")
        abs_summed = sem("abs_summed")
        scale_step = sem("scale_step")
        tern_step = sem("tern_step")
        ternary = sem("ternary")
        const_zero = sem("const_zero")
        consts = sem("consts")
        x_loaded = sem("x_loaded")
        stats_done = sem("stats_done")
        aggr_done = sem("aggr_done")
        vareps_done = sem("vareps_done")
        rstd_done = sem("rstd_done")
        xn_ready = sem("xn_ready")
        xt_psum = sem("xt_psum")
        xt_hi = sem("xt_hi")
        xt_lo = sem("xt_lo")
        pads_ready = sem("pads_ready")
        qkv_psum = sem("qkv_psum")
        qk_hi = sem("qk_hi")
        qk_lo = sem("qk_lo")
        v_ready = sem("v_ready")
        turned = sem("turned")
        turn_read = sem("turn_read")
        scored = sem("scored")
        max_done = sem("max_done")
        m_part = sem("m_part")
        m_ready = sem("m_ready")
        scored_t = sem("scored_t")
        exp_done = sem("exp_done")
        pv_done = sem("pv_done")
        out_copied = sem("out_copied")
        zinv_done = sem("zinv_done")
        attn_psum = sem("attn_psum")
        x1_ready = sem("x1_ready")
        up_psum = sem("up_psum")
        silu_done = sem("silu_done")
        hid_done = sem("hid_done")
        h_hi = sem("h_hi")
        h_lo = sem("h_lo")
        down_psum = sem("down_psum")
        x2_ready = sem("x2_ready")
        qk1_psum = sem("qk1_psum")
        qk1_hi = sem("qk1_hi")
        qk1_lo = sem("qk1_lo")
        v1_psum = sem("v1_psum")
        v1_hi = sem("v1_hi")
        v1_lo = sem("v1_lo")
        s1_psum = sem("s1_psum")
        nm1_part = sem("nm1_part")
        nm1_ready = sem("nm1_ready")
        exp1_done = sem("exp1_done")
        ri1_done = sem("ri1_done")
        p1_ready = sem("p1_ready")
        pt1_psum = sem("pt1_psum")
        pt1_hi = sem("pt1_hi")
        pt1_lo = sem("pt1_lo")
        out1_psum = sem("out1_psum")
        bias_added = sem("bias_added")
        x3_ready = sem("x3_ready")
        x3_stored = sem("x3_stored")
        xt_stored = sem("xt_stored")
        logits_psum = sem("logits_psum")
        elog_done = sem("elog_done")
        route = sem("route")
        probs_ready = sem("probs_ready")
        probt_psum = sem("probt_psum")
        probt_ready = sem("probt_ready")
        probt_stored = sem("probt_stored")

        N_CONSTS = 13
        N_ROUTE = 3 + 1 + TJ + 2 + TJ + 3

        block = ctx.enter_context(nc.Block())

        loads = [wqkv0, wo0, wqkv1, wo1, gate_w, w_up, w_gate, w_down]
        UP, DOWN = 5, 7

        def staged(n):
            rows, cols = loads[n].shape
            c = rows // P
            return stage[:, n % 2, 0:c * cols].rearrange("p (c n) -> p c n", c=c)

        def loaded(eng, n):
            eng.wait_ge(w_loaded[n % 2], 16 * (n // 2 + 1))

        @block.sync
        def _(sp):
            def load_weights(n):
                sp.dma_start(staged(n), loads[n].rearrange("(c p) n -> p c n", p=P)).then_inc(
                    w_loaded[n % 2], 16)

            sp.dma_start(xin[:], x[0:T, :].rearrange("(j p) n -> p j n", p=P)).then_inc(x_loaded, 16)
            load_weights(0)
            load_weights(1)
            sp.dma_start(bqk[:], bqk1).then_inc(bias_loaded, 16)
            sp.dma_start(bv[:], bv1).then_inc(bias_loaded, 16)
            sp.dma_start(bo[:], bo1.to_broadcast([P, D])).then_inc(bias_loaded, 16)
            sp.dma_start(gb[:], gate_b.to_broadcast([P, NE])).then_inc(bias_loaded, 16)
            sp.wait_ge(qkv0_split, 2)
            load_weights(2)
            for n in range(3, len(loads)):
                sp.wait_ge(split_end, n - 2)
                load_weights(n)

            def batch(b, more):
                x3_rows = x3_d[bass.ts(b, T), :].rearrange("(j p) n -> p j n", p=P)
                if more:
                    x_rows = x[bass.ts(b + 1, T), :].rearrange("(j p) n -> p j n", p=P)
                    sp.wait_ge(x1_ready, b * TJ + TJ)
                    sp.dma_start(xin[:], x_rows).then_inc(x_loaded, 16)
                sp.wait_ge(x3_ready, b * TJ + TJ)
                sp.dma_start(x3_rows, xres[:]).then_inc(x3_stored, 16)

            with sp.Fori(0, B - 1) as b:
                batch(b, True)
            batch(B - 1, False)
            sp.wait_ge(x3_stored, 16 * B)
            sp.wait_ge(xt_stored, 16 * B)
            sp.wait_ge(probt_stored, 16 * B)

        @block.gpsimd
        def _(pool):
            pool.memset(ident[:], 0.0).then_inc(const_zero, 1)
            pool.memset(identb[:], 0.0).then_inc(const_zero, 1)
            pool.memset(mask_q[:], 0.0).then_inc(const_zero, 1)
            pool.memset(mask_k[:], 0.0).then_inc(const_zero, 1)
            pool.memset(epsc[:], EPS).then_inc(consts, 1)
            pool.memset(halfc[:], -0.5).then_inc(consts, 1)
            pool.wait_ge(const_zero, 4)
            for m in (ident, identb):
                pool.affine_select(out=m[:], in_=m[:], compare_op=ALU.not_equal, fill=1.0, base=0,
                                   pattern=[[-1, P]], channel_multiplier=1).then_inc(consts, 1)
            pool.affine_select(out=mask_q[:], in_=mask_q[:], compare_op=ALU.is_ge, fill=NEG, base=0,
                               pattern=[[-1, P]], channel_multiplier=1).then_inc(consts, 1)
            pool.affine_select(out=mask_k[:], in_=mask_k[:], compare_op=ALU.is_ge, fill=NEG, base=0,
                               pattern=[[1, P]], channel_multiplier=-1).then_inc(consts, 1)
            pool.memset(vh[:, :, :, HD:HD + 1], 1.0).then_inc(consts, 1)
            pool.memset(vh[:, :, :, HD + 1:32], 0.0).then_inc(consts, 1)
            pool.wait_ge(consts, 8)
            pool.memset(ka[P // 2:P, :, :].bitcast(F32), 0.0).then_inc(consts, 1)
            pool.wait_ge(consts, 9)
            pool.memset(kb[0:P // 2, :, :].bitcast(F32), 0.0).then_inc(consts, 1)
            pool.wait_ge(consts, 10)
            pool.memset(score[:, :, NE:LOGIT_PAD], NEG).then_inc(consts, 1)
            pool.memset(top4[:, :, TOP_K:8], NEG).then_inc(consts, 1)
            pool.memset(probs[:].bitcast(F32), 0.0).then_inc(consts, 1)

            def rstd_of(b, n):
                pool.wait_ge(aggr_done, b * 16 + TJ * (n + 1))
                pool.tensor_tensor(vareps[:], mv[:, :, 1], epsc[:], ALU.add).then_inc(vareps_done, 1)
                pool.wait_ge(vareps_done, b * 4 + n + 1)
                pool.tensor_tensor(rstd[:], vareps[:], halfc[:], ALU.pow).then_inc(rstd_done, 1)

            def prepare_weights():
                parts = {1: wo0s, 2: wq1, 3: wo1s, 4: gws}
                for n, w in parts.items():
                    loaded(pool, n)
                    pool.tensor_copy(w[:, 0], staged(n)).then_inc(split, 1)
                    pool.wait_ge(split, n)
                    pool.tensor_tensor(w[:, 1], staged(n), w[:, 0].bitcast(F32), ALU.subtract).then_inc(split_end, 1)
                for k, w in enumerate((tup, tgate, tdown)):
                    pool.wait_ge(abs_summed, k + 1)
                    pool.partition_all_reduce(abstot[:, k:k + 1], abssum[:, k:k + 1], P,
                                              bass.bass_isa.ReduceOp.add).then_inc(scale_step, 1)
                    pool.wait_ge(scale_step, 4 * k + 1)
                    pool.tensor_scalar(tscale[:, k:k + 1], abstot[:, k:k + 1], 1.0 / (FF * D), TEPS,
                                       ALU.mult, ALU.add).then_inc(scale_step, 1)
                    pool.wait_ge(scale_step, 4 * k + 2)
                    pool.tensor_scalar(thalf[:, k:k + 1], tscale[:, k:k + 1], 0.5, 0.0,
                                       ALU.mult, ALU.add).then_inc(scale_step, 1)
                    pool.tensor_scalar(tnhalf[:, k:k + 1], tscale[:, k:k + 1], -0.5, 0.0,
                                       ALU.mult, ALU.add).then_inc(scale_step, 1)
                    pool.wait_ge(scale_step, 4 * k + 4)
                    flat = w[:, :, :].rearrange("p c n -> p (c n)")
                    for h in range(2):
                        part = slice(1024 * h, 1024 * h + 1024)
                        src = stage[:, (UP + k) % 2, part]
                        steps = 5 * k + 3 * h
                        pool.tensor_scalar(below[:], src, tnhalf[:, k:k + 1], 1.0, ALU.is_lt, ALU.mult)\
                            .then_inc(tern_step, 1)
                        pool.wait_ge(tern_step, steps + 1)
                        pool.tensor_scalar(src, src, thalf[:, k:k + 1], 1.0, ALU.is_gt, ALU.mult)\
                            .then_inc(tern_step, 1)
                        pool.wait_ge(tern_step, steps + 2)
                        pool.tensor_tensor(flat[:, part], src, below[:], ALU.subtract)\
                            .then_inc(tern_step if h == 0 else split_end, 1)
                        if h == 0:
                            pool.wait_ge(tern_step, steps + 3)
                        else:
                            pool.wait_ge(split_end, 5 + k)
                pool.tensor_tensor(tsgd[:], tscale[:, 1:2], tscale[:, 2:3], ALU.mult).then_inc(ternary, 1)

            def batch(b, first):
                if not first:
                    pool.wait_ge(xt_psum, b * 12)
                    pool.tensor_tensor(pfence[:], epsc[:, 0:1], epsc[:, 0:1], ALU.add)
                pool.memset(qkt[:, :, 0:NH, AUX:HS].bitcast(F32), 0.0).then_inc(pads_ready, 1)
                pool.memset(qkt[:, :, NH:2 * NH, AUX:AUX + 2].bitcast(F32), 1.0).then_inc(pads_ready, 1)
                pool.memset(qkt[:, :, NH:2 * NH, AUX + 2:HS].bitcast(F32), 0.0).then_inc(pads_ready, 1)
                rstd_of(b, 0)
                if first:
                    prepare_weights()
                rstd_of(b, 1)
                for m in range(FM):
                    pool.wait_ge(hid_done, b * FM + m + 1)
                    pool.wait_ge(h_hi, b * FM + m + 1)
                    pool.tensor_tensor(hs[:, 1, m], hid[:, m % 2], hs[:, 0, m].bitcast(F32), ALU.subtract)\
                        .then_inc(h_lo, 1)
                rstd_of(b, 2)
                if first:
                    pool.wait_ge(bias_loaded, 64)
                pool.wait_ge(xn_ready, b * 16 + 3 * TJ)
                pool.tensor_tensor(xres[:], xres[:], bo[:].rearrange("p (a n) -> p a n", a=1).to_broadcast([P, TJ, D]),
                                   ALU.add).then_inc(bias_added, 1)
                rstd_of(b, 3)

            batch(0, True)
            with pool.Fori(1, B) as b:
                batch(b, False)

        @block.vector
        def _(dve):
            def layernorm(b, n, src, ready):
                for j in range(TJ):
                    dve.wait_ge(*ready(j))
                    dve.bn_stats(stats[:, j], src[:, j]).then_inc(stats_done, 1)
                dve.wait_ge(stats_done, b * 16 + TJ * (n + 1))
                dve.memset(fence[:], 0.0)
                for j in range(TJ):
                    dve.bn_aggr(mv[:, j], stats[:, j]).then_inc(aggr_done, 1)
                dve.wait_ge(rstd_done, b * 4 + n + 1)
                for j in range(TJ):
                    dve.tensor_scalar(xn[:, j], src[:, j], mv[:, j, 0:1], rstd[:, j:j + 1],
                                      ALU.subtract, ALU.mult).then_inc(xn_ready, 1)

            def low_half(b, t, kh, bias=None):
                dve.wait_ge(xt_hi, b * 12 + 2 * t + kh + 1)
                if bias is None:
                    dve.tensor_tensor(xt[:, 1, kh], ps[:, kh], xt[:, 0, kh].bitcast(F32), ALU.subtract)\
                        .then_inc(xt_lo, 1)
                else:
                    dve.scalar_tensor_tensor(xt[:, 1, kh], ps[:, kh], bias, xt[:, 0, kh].bitcast(F32),
                                             ALU.add, ALU.subtract).then_inc(xt_lo, 1)

            def attention(b):
                for j in range(TJ):
                    dve.wait_ge(qk_hi, b * 8 + 2 * j + 2)
                    bank = ps[:, 2 * (j % 2)].rearrange("p (h c) -> p h c", h=2 * NH)
                    dve.tensor_tensor(qkt[:, j, 0:NH, Q_LO:Q_LO + HD], bank[:, 0:NH],
                                      qkt[:, j, 0:NH, 0:HD].bitcast(F32), ALU.subtract).then_inc(qk_lo, 1)
                    dve.tensor_tensor(qkt[:, j, NH:2 * NH, K_LO:K_LO + HD], bank[:, NH:2 * NH],
                                      qkt[:, j, NH:2 * NH, 0:HD].bitcast(F32), ALU.subtract).then_inc(qk_lo, 1)
                for event in ORDER:
                    kind, p, u = event
                    if kind == "turn_k":
                        dve.wait_ge(turned, b * len(TURNS) + TURNS.index(event) + 1)
                        if p >= 4:
                            dve.wait_ge(scored_t, b * 32 + TJ * (p - 3))
                        dve.tensor_copy(kb[P // 2:P, p % 4], ps[P // 2:P, T_BANK]).then_inc(turn_read, 1)
                    elif kind == "score":
                        n = TJ * p + u
                        s = unit_slot(event)
                        dve.wait_ge(scored, b * 32 + n + 1)
                        dve.tensor_reduce(negm[:, p % 2, u], ps[:, 2 * s:2 * s + 2, 0:P * (u + 1)], X, ALU.max,
                                          negate=True).then_inc(max_done, 1)
                        if u == TJ - 1:
                            dve.wait_ge(max_done, b * 32 + n + 1)
                            aux = qkt[:, :, 2 * p:2 * p + 2, AUX]
                            dve.tensor_copy(aux, negm[:, p % 2]).then_inc(m_part, 1)
                            dve.wait_ge(m_part, b * NP + p + 1)
                            dve.tensor_tensor(qkt[:, :, 2 * p:2 * p + 2, AUX + 1], negm[:, p % 2],
                                              aux.bitcast(F32), ALU.subtract).then_inc(m_ready, 1)
                    elif kind == "turn_out":
                        g = p
                        dve.wait_ge(turned, b * len(TURNS) + TURNS.index(event) + 1)
                        rows = ps[:, T_BANK].rearrange("p (j h c) -> p j h c", j=TJ, h=4)
                        dve.reciprocal(zinv[:], rows[:, :, :, HD]).then_inc(zinv_done, 1)
                        dve.wait_ge(zinv_done, b * 4 + g + 1)
                        dve.tensor_tensor(xn[:, :, 4 * HD * g:4 * HD * (g + 1)].rearrange("p j (h c) -> p j h c", h=4),
                                          rows[:, :, :, 0:HD],
                                          zinv[:].rearrange("p j (h a) -> p j h a", a=1).to_broadcast([P, TJ, 4, HD]),
                                          ALU.mult).then_inc(turn_read, 1)
                for kh in range(KH):
                    low_half(b, XT_Z, kh)
                for j in range(TJ):
                    dve.wait_ge(attn_psum, b * TJ + j + 1)
                    dve.tensor_tensor(xres[:, j], ps[:, 2 + j, 0:D], xin[:, j], ALU.add).then_inc(x1_ready, 1)

            def feed_forward(b):
                for m in range(FM):
                    r = m % 2
                    dve.wait_ge(up_psum, b * 2 * FM + 2 * m + 2)
                    dve.wait_ge(silu_done, b * FM + m + 1)
                    if m >= 2:
                        dve.wait_ge(h_lo, b * FM + m - 1)
                    dve.tensor_tensor(hid[:, r], ps[:, 2 * r + 1], gated[:, r], ALU.mult).then_inc(hid_done, 1)
                for j in range(TJ):
                    dve.wait_ge(down_psum, b * TJ + j + 1)
                    if j == 0:
                        dve.wait_ge(ternary, 1)
                    dve.scalar_tensor_tensor(xres[:, j], ps[:, 4 + j, 0:D], tsgd[:, 0:1], xres[:, j],
                                             ALU.mult, ALU.add).then_inc(x2_ready, 1)

            def second_attention(b):
                for m in range(4):
                    dve.wait_ge(qk1_hi, b * 4 + m + 1)
                    dve.scalar_tensor_tensor(qk1[:, 1, m], ps[:, m], bqk[:, m:m + 1], qk1[:, 0, m].bitcast(F32),
                                             ALU.add, ALU.subtract).then_inc(qk1_lo, 1)
                for j in range(TJ):
                    dve.wait_ge(v1_hi, b * TJ + j + 1)
                    dve.tensor_tensor(v1[:, 1, j], ps[:, 4 + j, 0:D], v1[:, 0, j].bitcast(F32), ALU.subtract)\
                        .then_inc(v1_lo, 1)

                def maximum(j):
                    dve.wait_ge(s1_psum, b * TJ + j + 1)
                    dve.tensor_reduce(nm1[:, j:j + 1], ps[:, j], X, ALU.max, negate=True).then_inc(nm1_part, 1)
                    dve.wait_ge(nm1_part, b * TJ + j + 1)
                    dve.tensor_scalar(nm1s[:, j:j + 1], nm1[:, j:j + 1], 1.0 / 16, None, ALU.mult)\
                        .then_inc(nm1_ready, 1)

                def normalise(j):
                    dve.wait_ge(exp1_done, b * TJ + j + 1)
                    dve.reciprocal(ri1[:, j:j + 1], rs1[:, j:j + 1]).then_inc(ri1_done, 1)
                    dve.wait_ge(ri1_done, b * TJ + j + 1)
                    dve.tensor_scalar(p1[:, j], p1[:, j], ri1[:, j:j + 1], None, ALU.mult).then_inc(p1_ready, 1)

                for j in range(TJ):
                    maximum(j)
                    if j:
                        normalise(j - 1)
                normalise(TJ - 1)
                for i in range(TJ):
                    dve.wait_ge(pt1_hi, b * TJ + i + 1)
                    dve.tensor_tensor(ptr[:, 1, i], ps[:, 4 + i], ptr[:, 0, i].bitcast(F32), ALU.subtract)\
                        .then_inc(pt1_lo, 1)
                for kh in range(KH):
                    low_half(b, XT_CTX, kh, bv[:, kh:kh + 1])
                for j in range(TJ):
                    dve.wait_ge(out1_psum, b * TJ + j + 1)
                    if j == 0:
                        dve.wait_ge(bias_added, b + 1)
                    dve.tensor_tensor(xres[:, j], ps[:, 4 + j, 0:D], xres[:, j], ALU.add).then_inc(x3_ready, 1)

            def router(b):
                n = [0]

                def link(ins):
                    n[0] += 1
                    ins.then_inc(route, 1)
                    return b * N_ROUTE + n[0]

                s = score[:, :, 0:NE]
                dve.wait_ge(elog_done, b + 1)
                done = link(dve.tensor_scalar(prob[:], elog[:], 1.0, None, ALU.add))
                dve.wait_ge(route, done)
                done = link(dve.reciprocal(elog[:], prob[:]))
                dve.wait_ge(route, done)
                done = link(dve.tensor_tensor(s, elog[:], gb[:].rearrange("p (a e) -> p a e", a=1).to_broadcast(
                    [P, TJ, NE]), ALU.add))
                dve.wait_ge(route, done)
                dve.memset(fence[:], 0.0)
                for j in range(TJ):
                    done = link(dve.max(top8[:, j], score[:, j]))
                dve.wait_ge(route, done)
                link(dve.tensor_reduce(topsum[:], top8[:, :, 0:TOP_K], X, ALU.add))
                done = link(dve.tensor_copy(top4[:, :, 0:TOP_K], top8[:, :, 0:TOP_K]))
                dve.wait_ge(route, done)
                link(dve.reciprocal(topinv[:], topsum[:]))
                for j in range(TJ):
                    done = link(dve.match_replace(rest[:, j], top4[:, j], score[:, j], -3.0e38))
                dve.wait_ge(route, done)
                done = link(dve.tensor_tensor(prob[:], rest[:, :, 0:NE], s, ALU.not_equal))
                dve.wait_ge(route, done)
                done = link(dve.tensor_tensor(prob[:], prob[:], s, ALU.mult))
                dve.wait_ge(route, done)
                done = link(dve.tensor_tensor(elog[:], prob[:], topinv[:].rearrange(
                    "p (j a) -> p j a", a=1).to_broadcast([P, TJ, NE]), ALU.mult))
                assert n[0] == N_ROUTE, n
                dve.wait_ge(route, done)
                dve.tensor_copy(probs[:, :, 0:NE], elog[:]).then_inc(probs_ready, 1)
                dve.wait_ge(probs_ready, b * 2 + 1)
                dve.tensor_tensor(probs[:, :, NE:2 * NE], elog[:], probs[:, :, 0:NE].bitcast(F32), ALU.subtract)\
                    .then_inc(probs_ready, 1)
                dve.wait_ge(x3_stored, b * 16 + 16)

            dve.wait_ge(qkv0_split, 1)
            dve.tensor_tensor(wq0[:, 1], staged(0), wq0[:, 0].bitcast(F32), ALU.subtract).then_inc(qkv0_split, 1)
            dve.wait_ge(bias_loaded, 64)
            with dve.Fori(0, B) as b:
                layernorm(b, 0, xin, lambda j: (x_loaded, b * 16 + 16))
                for kh in range(KH):
                    low_half(b, XT_LN0, kh)
                attention(b)
                layernorm(b, 1, xres, lambda j: (x1_ready, b * TJ + j + 1))
                for kh in range(KH):
                    low_half(b, XT_LN1, kh)
                feed_forward(b)
                layernorm(b, 2, xres, lambda j: (x2_ready, b * TJ + j + 1))
                for kh in range(KH):
                    low_half(b, XT_LN2, kh)
                second_attention(b)
                layernorm(b, 3, xres, lambda j: (x3_ready, b * TJ + j + 1))
                for kh in range(KH):
                    low_half(b, XT_LN3, kh)
                router(b)

        @block.scalar
        def _(act):
            def high_half(b, t, kh, bias=None):
                act.wait_ge(xt_psum, b * 12 + 2 * t + kh + 1)
                if bias is None:
                    act.activation(xt[:, 0, kh], ps[:, kh], ACT.Copy).then_inc(xt_hi, 1)
                else:
                    act.activation(xt[:, 0, kh], ps[:, kh], ACT.Identity, bias=bias).then_inc(xt_hi, 1)

            def attention(b, first):
                for j in range(TJ):
                    act.wait_ge(qkv_psum, b * TJ + j + 1)
                    bank = ps[:, 2 * (j % 2)].rearrange("p (h a c) -> p h a c", h=2 * NH, a=1)
                    act.activation(qkt[:, j, 0:NH, 0:AUX].rearrange("p h (a c) -> p h a c", c=HD)[:, :, 0:3:2],
                                   bank[:, 0:NH].to_broadcast([P, NH, 2, HD]), ACT.Copy).then_inc(qk_hi, 1)
                    act.activation(qkt[:, j, NH:2 * NH, 0:AUX].rearrange("p h (a c) -> p h a c", c=HD)[:, :, 0:2],
                                   bank[:, NH:2 * NH].to_broadcast([P, NH, 2, HD]), ACT.Copy).then_inc(qk_hi, 1)
                    act.activation(vh[:, j, :, 0:HD], ps[:, 2 * (j % 2) + 1, 0:D].rearrange("p (h c) -> p h c", h=NH),
                                   ACT.Copy).then_inc(v_ready, 1)
                for event in ORDER:
                    kind, p, u = event
                    if kind in ("turn_k", "turn_q", "turn_shifted_q"):
                        if kind == "turn_k":
                            to = ka[0:P // 2, p % 4]
                            if p >= 4:
                                act.wait_ge(scored_t, b * 32 + TJ * (p - 3))
                        elif kind == "turn_q":
                            to = q1[:, p % 2]
                            if p >= 2:
                                act.wait_ge(scored, b * 32 + TJ * (p - 1))
                        else:
                            to = q2[:, p % 2]
                            if p >= 2:
                                act.wait_ge(scored_t, b * 32 + TJ * (p - 1))
                        act.wait_ge(turned, b * len(TURNS) + TURNS.index(event) + 1)
                        rows = P // 2 if kind == "turn_k" else P
                        act.activation(to, ps[0:rows, T_BANK], ACT.Copy).then_inc(turn_read, 1)
                    elif kind == "scoreT":
                        n = TJ * p + u
                        s = unit_slot(event)
                        w = T - P * u
                        act.wait_ge(scored_t, b * 32 + n + 1)
                        if n >= 3:
                            act.wait_ge(pv_done, b * 32 + n - 2)
                        act.activation(pt[:, n % 3, :, 0:w], ps[:, 2 * s:2 * s + 2, 0:w], ACT.Exp,
                                       scale=0.25).then_inc(exp_done, 1)
                    elif kind == "copy_out":
                        act.wait_ge(pv_done, b * 32 + 8 * (p + 1))
                        if p >= 2:
                            act.wait_ge(turned, b * len(TURNS) + TURNS.index(("turn_out", p - 2, 0)) + 1)
                        act.activation(ot[:, p % 2], ps[:, PO_BANK], ACT.Copy).then_inc(out_copied, 1)
                    if first and event in (("scoreT", 1, 0), ("scoreT", 3, 0), ("scoreT", 5, 0)):
                        k = p // 2
                        loaded(act, UP + k)
                        act.activation(absout[:], stage[:, (UP + k) % 2, :], ACT.Abs,
                                       accum_out=abssum[:, k:k + 1]).then_inc(abs_summed, 1)
                for kh in range(KH):
                    high_half(b, XT_Z, kh)

            def feed_forward(b):
                def high(m):
                    act.wait_ge(hid_done, b * FM + m + 1)
                    act.activation(hs[:, 0, m], hid[:, m % 2], ACT.Copy).then_inc(h_hi, 1)

                for m in range(FM):
                    r = m % 2
                    act.wait_ge(up_psum, b * 2 * FM + 2 * m + 1)
                    if m >= 2:
                        act.wait_ge(hid_done, b * FM + m - 1)
                    act.activation(gated[:, r], ps[:, 2 * r], ACT.Silu, scale=tscale[:, 0:1]).then_inc(silu_done, 1)
                    if m:
                        high(m - 1)
                high(FM - 1)

            def second_attention(b):
                for m in range(4):
                    act.wait_ge(qk1_psum, b * 4 + m + 1)
                    act.activation(qk1[:, 0, m], ps[:, m], ACT.Identity, bias=bqk[:, m:m + 1]).then_inc(qk1_hi, 1)
                for j in range(TJ):
                    act.wait_ge(v1_psum, b * TJ + j + 1)
                    act.activation(v1[:, 0, j], ps[:, 4 + j, 0:D], ACT.Copy).then_inc(v1_hi, 1)
                for j in range(TJ):
                    act.wait_ge(nm1_ready, b * TJ + j + 1)
                    act.activation(p1[:, j], ps[:, j], ACT.Exp, bias=nm1s[:, j:j + 1], scale=1.0 / 16,
                                   accum_out=rs1[:, j:j + 1]).then_inc(exp1_done, 1)
                act.wait_ge(pt1_psum, b * TJ + TJ)
                for i in range(TJ):
                    act.activation(ptr[:, 0, i], ps[:, 4 + i], ACT.Copy).then_inc(pt1_hi, 1)
                for kh in range(KH):
                    high_half(b, XT_CTX, kh, bv[:, kh:kh + 1])

            def batch(b, first):
                if not first:
                    act.wait_ge(xt_stored, b * 16)
                for kh in range(KH):
                    high_half(b, XT_LN0, kh)
                attention(b, first)
                for kh in range(KH):
                    high_half(b, XT_LN1, kh)
                feed_forward(b)
                for kh in range(KH):
                    high_half(b, XT_LN2, kh)
                second_attention(b)
                for kh in range(KH):
                    high_half(b, XT_LN3, kh)
                act.wait_ge(xt_lo, b * 12 + 12)
                act.dma_start(xt4_d[:, :, :, bass.ts(b, T)], xt[:].bitcast(F32)).then_inc(xt_stored, 16)
                act.wait_ge(logits_psum, b + 1)
                act.activation(elog[:], ps[:, 2, 0:TJ * NE].rearrange("p (j e) -> p j e", j=TJ), ACT.Exp,
                               scale=-1.0).then_inc(elog_done, 1)
                if not first:
                    act.wait_ge(probt_stored, b * 16)
                act.wait_ge(probt_psum, b + 1)
                act.activation(probt[:], ps[:, 3], ACT.Copy).then_inc(probt_ready, 1)
                act.wait_ge(probt_ready, b + 1)
                act.dma_start(probs_d[:, bass.ts(b, T)], probt[:].bitcast(F32)).then_inc(probt_stored, 16)

            loaded(act, 0)
            act.activation(wq0[:, 0], staged(0), ACT.Copy).then_inc(qkv0_split, 1)
            act.wait_ge(bias_loaded, 64)
            batch(0, True)
            with act.Fori(1, B) as b:
                batch(b, False)

        @block.tensor
        def _(pe):
            def turn_halves(b, t, src, ready):
                for kh in range(KH):
                    for j in range(TJ):
                        if kh == 0:
                            ready(j)
                        mm = pe.transpose(ps[:, kh, P * j:P * (j + 1)], src[:, j, P * kh:P * (kh + 1)], ident[:])
                    mm.then_inc(xt_psum, 1)

            def halves_ready(b, t):
                for kh in range(KH):
                    pe.wait_ge(xt_lo, b * 12 + 2 * t + kh + 1)

            def product(out, left, right, start=True, stop=True):
                terms = [(l, r, kh) for kh in range(KH) for l, r in ((0, 0), (1, 0), (0, 1))]
                for n, (l, r, kh) in enumerate(terms):
                    mm = pe.matmul(out, left(l, kh), right(r, kh), start=start and n == 0,
                                   stop=stop and n == len(terms) - 1)
                return mm

            def x_tile(j):
                return lambda part, kh: xt[:, part, kh, P * j:P * (j + 1)]

            def attention(b):
                halves_ready(b, XT_LN0)
                pe.wait_ge(qkv0_split, 2)
                for j in range(TJ):
                    r = j % 2
                    if j >= 2:
                        pe.wait_ge(qk_lo, b * 8 + 2 * (j - 1))
                        pe.wait_ge(v_ready, b * TJ + j - 1)
                    product(ps[:, 2 * r], x_tile(j), lambda part, kh: wq0[:, part, kh, 0:2 * D])
                    product(ps[:, 2 * r + 1, 0:D], x_tile(j), lambda part, kh: wq0[:, part, kh, 2 * D:3 * D])\
                        .then_inc(qkv_psum, 1)
                pe.wait_ge(qk_lo, b * 8 + 8)
                pe.wait_ge(pads_ready, b * 3 + 3)
                for event in ORDER:
                    kind, p, u = event
                    if kind.startswith("turn"):
                        n = TURNS.index(event)
                        if n:
                            pe.wait_ge(turn_read, b * N_TURN_READS + turn_reads(TURNS[n - 1]))
                        if kind == "turn_shifted_q":
                            pe.wait_ge(m_ready, b * NP + p + 1)
                        if kind == "turn_out":
                            pe.wait_ge(out_copied, b * 4 + p + 1)
                        for j in range(TJ):
                            if kind == "turn_out":
                                src = ot[:, p % 2, P * j:P * (j + 1)]
                            else:
                                h = 2 * p + (NH if kind == "turn_k" else 0)
                                src = qkt[:, j, h:h + 2].rearrange("p h c -> p (h c)").bitcast(F32)
                            mm = pe.transpose(ps[:, T_BANK, P * j:P * (j + 1)], src, ident[:])
                        mm.then_inc(turned, 1)
                    elif kind in ("score", "scoreT"):
                        n = UNITS.index(event)
                        s = unit_slot(event)
                        if n >= 3:
                            before, bp, bu = UNITS[n - 3]
                            pe.wait_ge(max_done if before == "score" else exp_done, b * 32 + TJ * bp + bu + 1)
                        if event == UNITS[0]:
                            pe.wait_ge(v_ready, b * TJ + TJ)
                        if u == 0:
                            q = ("turn_q" if kind == "score" else "turn_shifted_q", p, 0)
                            pe.wait_ge(turn_read, b * N_TURN_READS + turn_reads(q))
                        for h, keys in enumerate((ka, kb)):
                            if kind == "score":
                                w, d = P * (u + 1), P * u
                                pe.matmul(ps[:, 2 * s + h, 0:w], q1[:, p % 2, P * u:P * (u + 1)],
                                          keys[:, p % 4, 0:w], start=True, stop=False)
                                mm = pe.matmul(ps[:, 2 * s + h, d:d + P], identb[:], mask_q[:],
                                               start=False, stop=True)
                            else:
                                w = T - P * u
                                pe.matmul(ps[:, 2 * s + h, 0:w], keys[:, p % 4, P * u:P * (u + 1)],
                                          q2[:, p % 2, P * u:T], start=True, stop=False)
                                mm = pe.matmul(ps[:, 2 * s + h, 0:P], identb[:], mask_k[:],
                                               start=False, stop=True)
                        mm.then_inc(scored if kind == "score" else scored_t, 1)
                    elif kind == "value":
                        n = TJ * p + u
                        w = T - P * u
                        pe.wait_ge(exp_done, b * 32 + n + 1)
                        if p % 2 == 0 and u == 0 and p:
                            pe.wait_ge(out_copied, b * 4 + p // 2)
                        for h in range(2):
                            at = 32 * (2 * (p % 2) + h)
                            mm = pe.matmul(ps[at:at + 32, PO_BANK, P * u:T], vh[:, u, 2 * p + h],
                                           pt[:, n % 3, h, 0:w], start=u == 0, stop=u == TJ - 1)
                        mm.then_inc(pv_done, 1)
                turn_halves(b, XT_Z, xn, lambda j: pe.wait_ge(turn_read, b * N_TURN_READS + N_TURN_READS))
                halves_ready(b, XT_Z)
                pe.wait_ge(split_end, 1)
                for j in range(TJ):
                    product(ps[:, 2 + j, 0:D], x_tile(j), lambda part, kh: wo0s[:, part, kh]).then_inc(attn_psum, 1)

            def feed_forward(b):
                halves_ready(b, XT_LN1)
                pe.wait_ge(ternary, 1)

                def down(m):
                    pe.wait_ge(h_lo, b * FM + m + 1)
                    for j in range(TJ):
                        for part in range(2):
                            mm = pe.matmul(ps[:, 4 + j, 0:D], hs[:, part, m, P * j:P * (j + 1)], tdown[:, m],
                                           start=m == 0 and part == 0, stop=m == FM - 1 and part == 1)
                        if m == FM - 1:
                            mm.then_inc(down_psum, 1)

                for m in range(FM + 2):
                    if m < FM:
                        r = m % 2
                        if m >= 2:
                            pe.wait_ge(hid_done, b * FM + m - 1)
                        for w, bank in ((tup, 2 * r), (tgate, 2 * r + 1)):
                            for kh in range(KH):
                                for part in range(2):
                                    mm = pe.matmul(ps[:, bank], w[:, kh, P * m:P * (m + 1)], xt[:, part, kh],
                                                   start=kh == 0 and part == 0, stop=kh == 1 and part == 1)
                            mm.then_inc(up_psum, 1)
                    if m >= 2:
                        down(m - 2)

            def second_attention(b):
                halves_ready(b, XT_LN2)
                pe.wait_ge(split_end, 2)
                for m in range(4):
                    product(ps[:, m], lambda part, kh: wq1[:, part, kh, P * m:P * (m + 1)],
                            lambda part, kh: xt[:, part, kh]).then_inc(qk1_psum, 1)
                for j in range(TJ):
                    product(ps[:, 4 + j, 0:D], x_tile(j), lambda part, kh: wq1[:, part, kh, 2 * D:3 * D])\
                        .then_inc(v1_psum, 1)
                pe.wait_ge(qk1_lo, b * 4 + 4)
                for j in range(TJ):
                    product(ps[:, j], lambda part, kh: qk1[:, part, kh, P * j:P * (j + 1)],
                            lambda part, kh: qk1[:, part, 2 + kh]).then_inc(s1_psum, 1)
                pe.wait_ge(v1_lo, b * TJ + TJ)
                for j in range(TJ):
                    pe.wait_ge(p1_ready, b * TJ + j + 1)
                    for i in range(TJ):
                        mm = pe.transpose(ps[:, 4 + i, P * j:P * (j + 1)], p1[:, j, P * i:P * (i + 1)], ident[:])
                    mm.then_inc(pt1_psum, 1)
                for hh in range(KH):
                    for i in range(TJ):
                        if hh == 0:
                            pe.wait_ge(pt1_lo, b * TJ + i + 1)
                        for l, r in ((0, 0), (1, 0), (0, 1)):
                            mm = pe.matmul(ps[:, hh], v1[:, l, i, P * hh:P * (hh + 1)], ptr[:, r, i],
                                           start=i == 0 and l == 0 and r == 0, stop=i == TJ - 1 and r == 1)
                    mm.then_inc(xt_psum, 1)
                halves_ready(b, XT_CTX)
                pe.wait_ge(split_end, 3)
                for j in range(TJ):
                    product(ps[:, 4 + j, 0:D], x_tile(j), lambda part, kh: wo1s[:, part, kh]).then_inc(out1_psum, 1)

            def router(b):
                halves_ready(b, XT_LN3)
                pe.wait_ge(split_end, 4)
                for j in range(TJ):
                    mm = product(ps[:, 2, NE * j:NE * (j + 1)], x_tile(j), lambda part, kh: gws[:, part, kh])
                mm.then_inc(logits_psum, 1)
                pe.wait_ge(probs_ready, b * 2 + 2)
                for j in range(TJ):
                    mm = pe.transpose(ps[:, 3, P * j:P * (j + 1)], probs[:, j].bitcast(F32), ident[:])
                mm.then_inc(probt_psum, 1)
                pe.wait_ge(probt_ready, b + 1)

            pe.wait_ge(consts, N_CONSTS)
            with pe.Fori(0, B) as b:
                turn_halves(b, XT_LN0, xn, lambda j: pe.wait_ge(xn_ready, b * 16 + j + 1))
                attention(b)
                turn_halves(b, XT_LN1, xn, lambda j: pe.wait_ge(xn_ready, b * 16 + TJ + j + 1))
                feed_forward(b)
                turn_halves(b, XT_LN2, xn, lambda j: pe.wait_ge(xn_ready, b * 16 + 2 * TJ + j + 1))
                second_attention(b)
                turn_halves(b, XT_LN3, xn, lambda j: pe.wait_ge(xn_ready, b * 16 + 3 * TJ + j + 1))
                router(b)


def experts(nc, w1, w3, w2, sel, x3_d, xt4_d, probs_d, out):
    with ExitStack() as ctx:
        def sb(name, shape, dt=F32):
            return ctx.enter_context(nc.sbuf_tensor(name, shape, dt))

        def sem(name):
            return ctx.enter_context(nc.semaphore(name))

        ps = ctx.enter_context(nc.psum_tensor("eps", [P, 8, 512], F32))
        xt4 = sb("xt4", [P, 2, KH, NTOK], F32R)
        prt = sb("prt", [P, NTOK], F32R)
        x3 = sb("x3", [P, NTOK // P, D])
        acc = sb("acc", [P, KH, NTOK])
        ident = sb("eident", [P, P])
        st13 = sb("st13", [P, 2, 2, KH, PAIR])
        st2 = sb("st2", [P, 2, 2, D])
        stsel = sb("stsel", [P, 2, PAIR])
        w13s = sb("w13s", [P, 2, 2, 2, KH, PAIR], F32R)
        w2s = sb("w2s", [P, 2, 2, 2, D], F32R)
        sels = sb("sels", [P, 2, PAIR], F32R)
        h1 = sb("h1", [P, 2, T])
        gate = sb("gate", [P, 2, T])
        act_h = sb("act_h", [P, 2, T])
        y = sb("y", [P, 2, T])
        ys = sb("ys", [P, 4, 2, T], F32R)

        zeroed = sem("e_zeroed")
        ident_ready = sem("e_ident_ready")
        xt4_loaded = sem("xt4_loaded")
        prt_loaded = sem("prt_loaded")
        x3_loaded = sem("x3_loaded")
        w_loaded = [sem("e_w_loaded_even"), sem("e_w_loaded_odd")]
        w_hi = sem("e_w_hi")
        w_lo = sem("e_w_lo")
        up_psum = sem("e_up_psum")
        spread_psum = sem("e_spread_psum")
        h1_copied = sem("h1_copied")
        gate_done = sem("gate_done")
        silu_done = sem("e_silu_done")
        y_ready = sem("y_ready")
        y_hi = sem("y_hi")
        y_lo = sem("y_lo")
        y_used = sem("y_used")
        half_psum = sem("half_psum")
        acc_zeroed = sem("acc_zeroed")
        acc_done = sem("acc_done")
        acc_turned = sem("acc_turned")
        summed = sem("summed")
        stored = sem("stored")

        block = ctx.enter_context(nc.Block())
        NU = 2 * B
        LOOPS = (NPAIRS - 2) // 2

        def steps(eng, step):
            step(0, 0)
            with eng.Fori(0, LOOPS) as k:
                step(2 * k + 1, 1)
                step(2 * k + 2, 0)
            step(NPAIRS - 1, 1)

        @block.sync
        def _(sp):
            def load(u, slot):
                cols = bass.ts(u, PAIR)
                w1_at = w1[:, cols].rearrange("(c p) n -> p c n", p=P)
                w3_at = w3[:, cols].rearrange("(c p) n -> p c n", p=P)
                w2_at = w2[cols, :].rearrange("(c p) n -> p c n", p=P)
                sel_at = sel[:, cols]
                if not isinstance(u, int):
                    sp.wait_ge(w_lo, 2 * (u - 1))
                sp.dma_start(st13[:, slot, 0], w1_at).then_inc(w_loaded[slot], 16)
                sp.dma_start(st13[:, slot, 1], w3_at).then_inc(w_loaded[slot], 16)
                sp.dma_start(st2[:, slot], w2_at).then_inc(w_loaded[slot], 16)
                sp.dma_start(stsel[:, slot], sel_at).then_inc(w_loaded[slot], 16)

            load(0, 0)
            for c in range(B):
                sp.dma_start(xt4[:, :, :, bass.ts(c, T)].bitcast(F32), xt4_d[:, :, :, bass.ts(c, T)]).then_inc(xt4_loaded, 16)
            load(1, 1)
            sp.dma_start(prt[:].bitcast(F32), probs_d).then_inc(prt_loaded, 16)
            sp.dma_start(x3[:], x3_d.rearrange("(j p) n -> p j n", p=P)).then_inc(x3_loaded, 16)
            with sp.Fori(1, LOOPS + 1) as k:
                load(2 * k, 0)
                load(2 * k + 1, 1)
            for c in range(B):
                sp.wait_ge(summed, c + 1)
                sp.dma_start(out[bass.ts(c, T), :].rearrange("(j p) n -> p j n", p=P),
                             x3[:, TJ * c:TJ * (c + 1)]).then_inc(stored, 16)
            sp.wait_ge(stored, 16 * B)

        @block.gpsimd
        def _(pool):
            pool.memset(ident[:], 0.0).then_inc(zeroed, 1)
            pool.wait_ge(zeroed, 1)
            pool.affine_select(out=ident[:], in_=ident[:], compare_op=ALU.not_equal, fill=1.0, base=0,
                               pattern=[[-1, P]], channel_multiplier=1).then_inc(ident_ready, 1)

            def split_low(u, slot):
                pool.wait_ge(w_hi, 3 * u + 3)
                pool.tensor_tensor(w13s[:, slot, 1], st13[:, slot], w13s[:, slot, 0].bitcast(F32), ALU.subtract)\
                    .then_inc(w_lo, 1)
                pool.tensor_tensor(w2s[:, slot, 1], st2[:, slot], w2s[:, slot, 0].bitcast(F32), ALU.subtract)\
                    .then_inc(w_lo, 1)

            def step(u, slot):
                for n in range(NU):
                    pool.wait_ge(y_hi, NU * u + n + 1)
                    pool.tensor_tensor(ys[:, n % 4, 1], y[:, n % 2], ys[:, n % 4, 0].bitcast(F32), ALU.subtract)\
                        .then_inc(y_lo, 1)
                    if n == 3 and not (isinstance(u, int) and u == NPAIRS - 1):
                        split_low(u + 1, 1 - slot)

            pool.memset(acc[:], 0.0).then_inc(acc_zeroed, 1)
            split_low(0, 0)
            steps(pool, step)

        @block.scalar
        def _(act):
            def split(u, slot, round_):
                act.wait_ge(w_loaded[slot], 64 * round_ + 64)
                act.activation(w13s[:, slot, 0], st13[:, slot], ACT.Copy).then_inc(w_hi, 1)
                act.activation(w2s[:, slot, 0], st2[:, slot], ACT.Copy).then_inc(w_hi, 1)
                act.activation(sels[:, slot], stsel[:, slot], ACT.Copy).then_inc(w_hi, 1)

            def step(u, slot, next_round, shared=False, last=False):
                for n in range(NU):
                    r = n % 2
                    act.wait_ge(up_psum, NU * u + n + 1)
                    if shared:
                        if n >= 2:
                            act.wait_ge(y_ready, n - 1)
                        act.activation(h1[:, r], ps[:, 3 * r], ACT.Silu).then_inc(h1_copied, 1)
                    else:
                        act.activation(h1[:, r], ps[:, 3 * r], ACT.Copy).then_inc(h1_copied, 1)
                        act.wait_ge(gate_done, NU * (u - 1) + n + 1)
                        act.activation(act_h[:, r], gate[:, r], ACT.Silu).then_inc(silu_done, 1)
                    act.wait_ge(y_ready, NU * u + n + 1)
                    if not (shared and n < 4):
                        act.wait_ge(y_used, NU * u + n - 3)
                    act.activation(ys[:, n % 4, 0], y[:, r], ACT.Copy).then_inc(y_hi, 1)
                    if n == 3 and not last:
                        if not shared:
                            act.wait_ge(y_used, NU * u)
                        split(u + 1, 1 - slot, next_round)

            split(0, 0, 0)
            step(0, 0, 0, shared=True)
            with act.Fori(0, LOOPS) as k:
                step(2 * k + 1, 1, k + 1)
                step(2 * k + 2, 0, k + 1)
            step(NPAIRS - 1, 1, 0, last=True)

        @block.vector
        def _(dve):
            def accumulate(c, chunk):
                dve.wait_ge(half_psum, c + 1)
                dve.tensor_tensor(acc[:, 0, bass.ts(chunk, T)], ps[:, 6], acc[:, 0, bass.ts(chunk, T)], ALU.add)\
                    .then_inc(acc_done, 1)
                dve.wait_ge(y_used, 2 * c + 2)
                dve.tensor_tensor(acc[:, 1, bass.ts(chunk, T)], ps[:, 7], acc[:, 1, bass.ts(chunk, T)], ALU.add)\
                    .then_inc(acc_done, 1)

            def step(u, slot):
                shared = isinstance(u, int) and u == 0
                for n in range(NU):
                    r = n % 2
                    dve.wait_ge(h1_copied, NU * u + n + 1)
                    if shared:
                        if n >= 2:
                            dve.wait_ge(y_lo, n - 1)
                        dve.tensor_tensor(y[:, r], ps[:, 3 * r + 1], h1[:, r], ALU.mult).then_inc(y_ready, 1)
                    else:
                        dve.tensor_tensor(gate[:, r], ps[:, 3 * r + 1], h1[:, r], ALU.mult).then_inc(gate_done, 1)
                        dve.wait_ge(spread_psum, NU * (u - 1) + n + 1)
                        dve.wait_ge(y_lo, NU * u + n - 1)
                        dve.wait_ge(silu_done, NU * (u - 1) + n + 1)
                        dve.tensor_tensor(y[:, r], ps[:, 3 * r + 2], act_h[:, r], ALU.mult).then_inc(y_ready, 1)
                    if n % 2 and not (shared and n == 1):
                        c = n // 2 - 1
                        if c < 0:
                            accumulate(B * u - 1, B - 1)
                        else:
                            accumulate(B * u + c, c)

            dve.wait_ge(acc_zeroed, 1)
            steps(dve, step)
            accumulate(B * NPAIRS - 1, B - 1)
            dve.wait_ge(x3_loaded, 16)
            for c in range(B):
                dve.wait_ge(acc_turned, c + 1)
                rows = x3[:, TJ * c:TJ * (c + 1)]
                at = 4 * (c % 2)
                dve.tensor_tensor(rows, ps[:, at:at + 2].rearrange("p a (j n) -> p (a j) n", j=2), rows, ALU.add)\
                    .then_inc(summed, 1)

        @block.tensor
        def _(pe):
            def up(u, slot, n):
                r, c, s = n % 2, n // 2, n % 2
                shared = isinstance(u, int) and u == 0
                if not (shared and n < 2):
                    pe.wait_ge(y_ready, NU * u + n - 1)
                if shared and s == 0:
                    pe.wait_ge(xt4_loaded, 64)
                if n == 0:
                    pe.wait_ge(w_hi, 3 * u + 3)
                    pe.wait_ge(w_lo, 2 * u + 2)
                for k in range(2):
                    terms = [(l, q, kh) for kh in range(KH) for l, q in ((0, 0), (1, 0), (0, 1))]
                    for i, (l, q, kh) in enumerate(terms):
                        mm = pe.matmul(ps[:, 3 * r + k], w13s[:, slot, l, k, kh, P * s:P * (s + 1)],
                                       xt4[:, q, kh, T * c:T * (c + 1)], start=i == 0, stop=i == len(terms) - 1)
                mm.then_inc(up_psum, 1)
                if not shared:
                    if n == 0:
                        pe.wait_ge(prt_loaded, 16)
                    pe.matmul(ps[:, 3 * r + 2], sels[:, slot, P * s:P * (s + 1)], prt[:, T * c:T * (c + 1)],
                              start=True, stop=True).then_inc(spread_psum, 1)

            def down(u, slot, n):
                c, s = n // 2, n % 2
                shared = isinstance(u, int) and u == 0
                if s == 0 and not (shared and n == 0):
                    pe.wait_ge(acc_done, 2 * (B * u + c))
                pe.wait_ge(y_lo, NU * u + n + 1)
                for half in range(KH):
                    for l, q in ((0, 0), (1, 0), (0, 1)):
                        mm = pe.matmul(ps[:, 6 + half], w2s[:, slot, l, s, P * half:P * (half + 1)], ys[:, n % 4, q],
                                       start=s == 0 and l == 0 and q == 0, stop=s == 1 and q == 1)
                    if s == 1 and half == 0:
                        mm.then_inc(half_psum, 1)
                mm.then_inc(y_used, 1)

            def step(u, slot):
                shared = isinstance(u, int) and u == 0
                for n in range(NU):
                    up(u, slot, n)
                    if n >= 2:
                        down(u, slot, n - 2)
                    elif not shared:
                        down(u - 1, 1 - slot, NU - 2 + n)

            steps(pe, step)
            down(NPAIRS - 1, 1, NU - 2)
            down(NPAIRS - 1, 1, NU - 1)
            pe.wait_ge(ident_ready, 1)
            for c in range(B):
                pe.wait_ge(acc_done, 2 * (B * (NPAIRS - 1) + c + 1))
                if c == 0:
                    pe.wait_ge(y_ready, NU * NPAIRS)
                if c >= 2:
                    pe.wait_ge(summed, c - 1)
                for j in range(TJ):
                    for half in range(KH):
                        at = D * (j % 2) + P * half
                        first = T * c + P * j
                        mm = pe.transpose(ps[:, 4 * (c % 2) + j // 2, at:at + P], acc[:, half, first:first + P],
                                          ident[:])
                mm.then_inc(acc_turned, 1)


def program(nc, t, out):
    x3_d = nc.dram_tensor("x3_kept", [NTOK, D], F32).ap()
    xt4_d = nc.dram_tensor("xt4_kept", [P, 2, KH, NTOK], F32).ap()
    probs_d = nc.dram_tensor("probs_kept", [P, NTOK], F32).ap()
    layers(nc, t["x"], t["wqkv0"], t["wo0"], t["w_up"], t["w_gate"], t["w_down"], t["wqkv1"], t["bqk1"], t["bv1"],
           t["wo1"], t["bo1"], t["gate_w"], t["gate_b"], x3_d, xt4_d, probs_d)
    experts(nc, t["w1"], t["w3"], t["w2"], t["sel"], x3_d, xt4_d, probs_d, out)


def kernel(**inputs):
    import numpy as np
    import concourse.bacc as bacc
    from concourse.bass_utils import run_bass_kernel_spmd as run

    a = {k: np.asarray(v) for k, v in inputs.items()}

    def padded(shared, axis):
        fill = [(0, 0), (0, 0)]
        fill[axis] = (0, PAIR - EH)
        return np.pad(shared, fill)

    def by_input(routed):
        return routed.transpose(1, 0, 2).reshape(D, HID)

    sel = np.zeros((P, PAIR + HID), np.float32)
    for e in range(NE):
        sel[e, PAIR + EH * e:PAIR + EH * (e + 1)] = 1.0
        sel[NE + e, PAIR + EH * e:PAIR + EH * (e + 1)] = 1.0

    wqkv1, bqkv1 = a["L1_attn_w_qkv"], a["L1_attn_b_qkv"]
    arrays = {
        "x": a["L0_attn_x"].reshape(NTOK, D),
        "wqkv0": np.concatenate([a["L0_attn_Wq"].T, a["L0_attn_Wk"].T, a["L0_attn_Wv"].T], 1),
        "wo0": a["L0_attn_Wo"].T,
        "w_up": a["L0_ffn_W_up"].T,
        "w_gate": a["L0_ffn_W_gate"].T,
        "w_down": a["L0_ffn_W_down"].T,
        "wqkv1": wqkv1.T,
        "bqk1": bqkv1[0:2 * D].reshape(4, P).T,
        "bv1": bqkv1[2 * D:3 * D].reshape(2, P).T,
        "wo1": a["L1_attn_w_out"].T,
        "bo1": a["L1_attn_b_out"].reshape(1, D),
        "gate_w": a["L1_ffn_gate_w"].T,
        "gate_b": a["L1_ffn_gate_b"].reshape(1, NE),
        "w1": np.concatenate([padded(a["L1_ffn_w1_shared"], 1), by_input(a["L1_ffn_w1_routed"])], 1),
        "w3": np.concatenate([padded(a["L1_ffn_w3_shared"], 1), by_input(a["L1_ffn_w3_routed"])], 1),
        "w2": np.concatenate([padded(a["L1_ffn_w2_shared"], 0), a["L1_ffn_w2_routed"].reshape(HID, D)], 0),
        "sel": sel,
    }
    arrays = {k: np.ascontiguousarray(v) for k, v in arrays.items()}
    nc = bacc.Bacc("TRN2", target_bir_lowering=False, num_devices=1)
    t = {k: nc.dram_tensor(k + "_in", v.shape, F32, kind="ExternalInput").ap() for k, v in arrays.items()}
    out = nc.dram_tensor("out", [NTOK, D], F32, kind="ExternalOutput").ap()
    program(nc, t, out)
    r = run(nc, [{k + "_in": v for k, v in arrays.items()}], core_ids=[0])
    return r.results[0]["out"].reshape(B, T, D)
```

```python
from contextlib import ExitStack

import concourse.bass as bass
from concourse import mybir

ALU = mybir.AluOpType
ACT = mybir.ActivationFunctionType
F32 = mybir.dt.float32
F32R = mybir.dt.float32r
BF16 = mybir.dt.bfloat16
X = mybir.AxisListType.X

P = 128
D = 256
KH = D // P
B, T = 4, 512
TJ = T // P
NTOK = B * T
NH, HD = 16, 16
NP = NH // 2
HS = 64
Q_LO, K_LO, AUX = 16, 32, 48
FF = 1024
FM = FF // P
NE, EH = 16, 176
HID = NE * EH
TOP_K = 4
PAIR = 2 * P
NPAIRS = 1 + HID // PAIR
NEG = -1.0e30
EPS = 1e-5
TEPS = 1e-8
LOGIT_PAD = 20

XT_Z, XT_LN1, XT_LN2, XT_CTX, XT_LN3 = range(5)
NXT = 5
XT_BANK = {XT_Z: 0, XT_LN1: 0, XT_LN2: 0, XT_CTX: 0, XT_LN3: 4}
XT0_BANK = 2
ROUTER_PARTS = 8
ROUTER_PAIR = 1
LN0_AGGR = 4
LAG = 2
T_BANK, PO_BANK = 6, 7
LOGIT_BANK = PO_BANK


TURN_AT = ((0, 0), (1, 1), (2, 1), (3, 1))


def attention_order():
    order = []
    for s in range(-1, NP + LAG + 1):
        done = s - LAG - 1
        turns = [("turn_k", s + 1, TURN_AT[0]), ("turn_q", s + 1, TURN_AT[1]), ("turn_shifted_q", s - 1, TURN_AT[2])]
        if done >= 0 and done % 2:
            order.append(("copy_out", done // 2, 0))
            turns.append(("turn_out", done // 2, TURN_AT[3]))
        for u in range(TJ):
            for place in range(3):
                for kind, p, at in turns:
                    if at == (u, place) and (kind == "turn_out" or 0 <= p < NP):
                        order.append((kind, p, 0))
                if place == 0 and 0 <= s < NP:
                    order.append(("score", s, u))
                if place == 1 and 0 <= s - LAG < NP:
                    order.append(("scoreT", s - LAG, u))
                    if u:
                        order.append(("value", s - LAG, u - 1))
        if 0 <= s - LAG < NP:
            order.append(("value", s - LAG, TJ - 1))
    return order


ORDER = attention_order()
UNITS = [x for x in ORDER if x[0] in ("score", "scoreT")]
TURNS = [x for x in ORDER if x[0].startswith("turn")]
TURN_READS = {"turn_k": 2, "turn_q": 1, "turn_shifted_q": 1, "turn_out": 1}
N_TURN_READS = sum(TURN_READS[k] for k, _, _ in TURNS)


def turn_reads(event):
    n = TURNS.index(event)
    return sum(TURN_READS[k] for k, _, _ in TURNS[: n + 1])


def unit_slot(unit):
    return UNITS.index(unit) % 3


def layers(nc, x, wqkv0, wo0, w_up, w_gate, w_down, wqkv1, bqk1, bv1, wo1, bo1, gate_w, gate_b,
           x3_d, xt4_d, probs_d):
    with ExitStack() as ctx:
        def sb(name, shape, dt=F32):
            return ctx.enter_context(nc.sbuf_tensor(name, shape, dt))

        def sem(name):
            return ctx.enter_context(nc.semaphore(name))

        ps = ctx.enter_context(nc.psum_tensor("ps", [P, 8, 512], F32))

        wq0 = sb("wq0", [P, 2, KH, 3 * D], F32R)
        wo0s = sb("wo0s", [P, 2, KH, D], F32R)
        wq1 = sb("wq1", [P, 2, KH, 3 * D], F32R)
        wo1s = sb("wo1s", [P, 2, KH, D], F32R)
        gws = sb("gws", [P, 2, KH, NE], F32R)
        tup = sb("tup", [P, KH, FF], F32R)
        tgate = sb("tgate", [P, KH, FF], F32R)
        tdown = sb("tdown", [P, FM, D], F32R)
        stage = sb("stage", [P, 2, 2048])
        below = sb("below", [P, 1024])
        absout = sb("absout", [P, 2048], BF16)
        abssum = sb("abssum", [P, 3])
        abstot = sb("abstot", [P, 3])
        meaneps = sb("meaneps", [P, 3])
        tscale = sb("tscale", [P, 3])
        thalf = sb("thalf", [P, 3])
        tnhalf = sb("tnhalf", [P, 3])
        tsgd = sb("tsgd", [P, 1])
        bqk = sb("bqk", [P, 4])
        bv = sb("bv", [P, 2])
        bo = sb("bo", [P, D])
        gb = sb("gb", [P, NE])

        ident = sb("ident", [P, P])
        identb = sb("identb", [P, P], BF16)
        mask_q = sb("mask_q", [P, P], BF16)
        mask_k = sb("mask_k", [P, P], BF16)
        epsc = sb("epsc", [P, TJ])
        halfc = sb("halfc", [P, TJ])

        xin = sb("xin", [P, TJ, D])
        xres = sb("xres", [P, TJ, D])
        xn = sb("xn", [P, TJ, D])
        xt = sb("xt", [P, 2, KH, T], F32R)
        xt0 = sb("xt0", [P, 2, KH, T], F32R)
        big = sb("big", [P, 8192], F32R)
        vh = sb("vh", [P, TJ, NH, 32])
        ka = sb("ka", [P, 4, T], F32R)
        kb = sb("kb", [P, 4, T], F32R)
        q1 = sb("q1", [P, 2, T], F32R)
        q2 = sb("q2", [P, 2, T], F32R)
        pt = sb("pt", [P, 3, 2, T])
        ot = sb("ot", [P, 2, T])
        v1 = sb("v1", [P, 2, TJ, D], F32R)

        fence = sb("fence", [P, 1])
        pfence = sb("pfence", [P, 1])
        stats = sb("stats", [P, 2, TJ, 6])
        mv = sb("mv", [P, 2, TJ, 2])
        vareps = sb("vareps", [P, 2, TJ])
        rstd = sb("rstd", [P, 2, TJ])
        negm = sb("negm", [P, 2, TJ, 2])
        zinv = sb("zinv", [P, TJ, 4])
        nm1 = sb("nm1", [P, TJ])
        nm1s = sb("nm1s", [P, TJ])
        rs1 = sb("rs1", [P, TJ])
        ri1 = sb("ri1", [P, TJ])
        elog = sb("elog", [P, TJ, NE])
        score = sb("score", [P, TJ, LOGIT_PAD])
        top8 = sb("top8", [P, TJ, 8])
        top4 = sb("top4", [P, TJ, 8])
        topsum = sb("topsum", [P, TJ])
        topinv = sb("topinv", [P, TJ])
        others = sb("others", [P, TJ, LOGIT_PAD])
        prob = sb("prob", [P, TJ, NE])
        probs = sb("probs", [P, TJ, P], F32R)
        probt = sb("probt", [P, T], F32R)

        qkt = big[:, :].rearrange("p (j h c) -> p j h c", j=TJ, h=2 * NH)
        hs = big[:, :].rearrange("p (l m t) -> p l m t", l=2, m=FM)
        qk1 = big[:, 0:4096].rearrange("p (l m t) -> p l m t", l=2, m=4)
        ptr = big[:, 4096:8192].rearrange("p (l m t) -> p l m t", l=2, m=TJ)
        gated = pt[:, 0]
        hid = pt[:, 1]
        p1 = pt[:, 0:2].rearrange("p a h t -> p (a h) t")

        w_loaded = [sem("w_loaded_even"), sem("w_loaded_odd")]
        bias_loaded = sem("bias_loaded")
        qkv0_split = sem("qkv0_split")
        split = sem("split")
        split_end = sem("split_end")
        abs_summed = sem("abs_summed")
        scale_step = sem("scale_step")
        tern_step = sem("tern_step")
        ternary = sem("ternary")
        const_zero = sem("const_zero")
        consts = sem("consts")
        x_loaded = sem("x_loaded")
        stats_done = [sem("stats0_done"), sem("stats_done")]
        aggr_done = [sem("aggr0_done"), sem("aggr_done")]
        vareps_done = [sem("vareps0_done"), sem("vareps_done")]
        rstd_done = [sem("rstd0_done"), sem("rstd_done")]
        xn_ready = [sem("xn0_ready"), sem("xn_ready")]
        xt0_psum = sem("xt0_psum")
        xt0_hi = sem("xt0_hi")
        xt0_lo = sem("xt0_lo")
        xt_psum = sem("xt_psum")
        xt_hi = sem("xt_hi")
        xt_lo = sem("xt_lo")
        pads_ready = sem("pads_ready")
        qkv_psum = sem("qkv_psum")
        qk_hi = sem("qk_hi")
        qk_lo = sem("qk_lo")
        v_ready = sem("v_ready")
        turned = sem("turned")
        turn_read = sem("turn_read")
        scored = sem("scored")
        max_done = sem("max_done")
        m_part = sem("m_part")
        m_ready = sem("m_ready")
        scored_t = sem("scored_t")
        exp_done = sem("exp_done")
        pv_done = sem("pv_done")
        out_copied = sem("out_copied")
        zinv_done = sem("zinv_done")
        attn_psum = sem("attn_psum")
        x1_ready = sem("x1_ready")
        up_psum = sem("up_psum")
        silu_done = sem("silu_done")
        hid_done = sem("hid_done")
        h_hi = sem("h_hi")
        h_lo = sem("h_lo")
        down_psum = sem("down_psum")
        x2_ready = sem("x2_ready")
        qk1_psum = sem("qk1_psum")
        qk1_hi = sem("qk1_hi")
        qk1_lo = sem("qk1_lo")
        v1_psum = sem("v1_psum")
        v1_hi = sem("v1_hi")
        v1_lo = sem("v1_lo")
        s1_psum = sem("s1_psum")
        nm1_part = sem("nm1_part")
        nm1_ready = sem("nm1_ready")
        exp1_done = sem("exp1_done")
        ri1_done = sem("ri1_done")
        p1_ready = sem("p1_ready")
        pt1_psum = sem("pt1_psum")
        pt1_hi = sem("pt1_hi")
        pt1_lo = sem("pt1_lo")
        out1_psum = sem("out1_psum")
        bias_added = sem("bias_added")
        x3_ready = sem("x3_ready")
        x3_stored = sem("x3_stored")
        kept = sem("kept")
        logits_psum = sem("logits_psum")
        elog_done = sem("elog_done")
        route = sem("route")
        probs_ready = sem("probs_ready")
        probt_psum = sem("probt_psum")
        probt_ready = sem("probt_ready")

        N_CONSTS = 13
        N_ROUTE = 9 + 2 * TJ

        block = ctx.enter_context(nc.Block())

        loads = [wqkv0, wo0, wqkv1, wo1, gate_w, w_up, w_gate, w_down]
        UP, DOWN = 5, 7

        def staged(n):
            rows, cols = loads[n].shape
            c = rows // P
            return stage[:, n % 2, 0:c * cols].rearrange("p (c n) -> p c n", c=c)

        def loaded(eng, n):
            eng.wait_ge(w_loaded[n % 2], 16 * (n // 2 + 1))

        @block.sync
        def _(sp):
            def load_weights(n):
                sp.dma_start(staged(n), loads[n].rearrange("(c p) n -> p c n", p=P)).then_inc(
                    w_loaded[n % 2], 16)

            sp.dma_start(xin[:], x[0:T, :].rearrange("(j p) n -> p j n", p=P)).then_inc(x_loaded, 16)
            load_weights(0)
            load_weights(1)
            sp.dma_start(bqk[:], bqk1).then_inc(bias_loaded, 16)
            sp.dma_start(bv[:], bv1).then_inc(bias_loaded, 16)
            sp.dma_start(bo[:], bo1.to_broadcast([P, D])).then_inc(bias_loaded, 16)
            sp.dma_start(gb[:], gate_b.to_broadcast([P, NE])).then_inc(bias_loaded, 16)
            sp.wait_ge(qkv0_split, 2)
            load_weights(2)
            for n in range(3, len(loads)):
                sp.wait_ge(split_end, n - 2)
                load_weights(n)

            def batch(b, more):
                x3_rows = x3_d[bass.ts(b, T), :].rearrange("(j p) n -> p j n", p=P)
                if more:
                    x_rows = x[bass.ts(b + 1, T), :].rearrange("(j p) n -> p j n", p=P)
                    sp.wait_ge(x1_ready, b * TJ + TJ)
                    sp.dma_start(xin[:], x_rows).then_inc(x_loaded, 16)
                sp.wait_ge(x3_ready, b * TJ + TJ)
                sp.dma_start(x3_rows, xres[:]).then_inc(x3_stored, 16)

            with sp.Fori(0, B - 1) as b:
                batch(b, True)
            batch(B - 1, False)
            sp.wait_ge(x3_stored, 16 * B)
            sp.wait_ge(kept, 32 * B)

        @block.gpsimd
        def _(pool):
            pool.memset(ident[:], 0.0).then_inc(const_zero, 1)
            pool.memset(identb[:], 0.0).then_inc(const_zero, 1)
            pool.memset(mask_q[:], 0.0).then_inc(const_zero, 1)
            pool.memset(mask_k[:], 0.0).then_inc(const_zero, 1)
            pool.memset(epsc[:], EPS).then_inc(consts, 1)
            pool.memset(halfc[:], -0.5).then_inc(consts, 1)
            pool.wait_ge(const_zero, 4)
            for m in (ident, identb):
                pool.affine_select(out=m[:], in_=m[:], compare_op=ALU.not_equal, fill=1.0, base=0,
                                   pattern=[[-1, P]], channel_multiplier=1).then_inc(consts, 1)
            pool.affine_select(out=mask_q[:], in_=mask_q[:], compare_op=ALU.is_ge, fill=NEG, base=0,
                               pattern=[[-1, P]], channel_multiplier=1).then_inc(consts, 1)
            pool.affine_select(out=mask_k[:], in_=mask_k[:], compare_op=ALU.is_ge, fill=NEG, base=0,
                               pattern=[[1, P]], channel_multiplier=-1).then_inc(consts, 1)
            pool.memset(vh[:, :, :, HD:HD + 1], 1.0).then_inc(consts, 1)
            pool.memset(vh[:, :, :, HD + 1:32], 0.0).then_inc(consts, 1)
            pool.wait_ge(consts, 8)
            pool.memset(ka[P // 2:P, :, :].bitcast(F32), 0.0).then_inc(consts, 1)
            pool.wait_ge(consts, 9)
            pool.memset(kb[0:P // 2, :, :].bitcast(F32), 0.0).then_inc(consts, 1)
            pool.wait_ge(consts, 10)
            pool.memset(score[:, :, NE:LOGIT_PAD], NEG).then_inc(consts, 1)
            pool.memset(top4[:, :, TOP_K:8], NEG).then_inc(consts, 1)
            pool.memset(probs[:].bitcast(F32), 0.0).then_inc(consts, 1)

            def rstd_of(count, k):
                pool.wait_ge(aggr_done[k], TJ * count)
                pool.tensor_tensor(vareps[:, k], mv[:, k, :, 1], epsc[:], ALU.add).then_inc(vareps_done[k], 1)
                pool.wait_ge(vareps_done[k], count)
                pool.tensor_tensor(rstd[:, k], vareps[:, k], halfc[:], ALU.pow).then_inc(rstd_done[k], 1)

            def prepare_weights():
                parts = {1: wo0s, 2: wq1, 3: wo1s, 4: gws}
                for n, w in parts.items():
                    loaded(pool, n)
                    pool.tensor_copy(w[:, 0], staged(n)).then_inc(split, 1)
                    pool.wait_ge(split, n)
                    pool.tensor_tensor(w[:, 1], staged(n), w[:, 0].bitcast(F32), ALU.subtract).then_inc(split_end, 1)
                for k, w in enumerate((tup, tgate, tdown)):
                    pool.wait_ge(abs_summed, k + 1)
                    pool.partition_all_reduce(abstot[:, k:k + 1], abssum[:, k:k + 1], P,
                                              bass.bass_isa.ReduceOp.add).then_inc(scale_step, 1)
                    pool.wait_ge(scale_step, 4 * k + 1)
                    pool.tensor_scalar(tscale[:, k:k + 1], abstot[:, k:k + 1], 1.0 / (FF * D), TEPS,
                                       ALU.mult, ALU.add).then_inc(scale_step, 1)
                    pool.wait_ge(scale_step, 4 * k + 2)
                    pool.tensor_scalar(thalf[:, k:k + 1], tscale[:, k:k + 1], 0.5, 0.0,
                                       ALU.mult, ALU.add).then_inc(scale_step, 1)
                    pool.tensor_scalar(tnhalf[:, k:k + 1], tscale[:, k:k + 1], -0.5, 0.0,
                                       ALU.mult, ALU.add).then_inc(scale_step, 1)
                    pool.wait_ge(scale_step, 4 * k + 4)
                    flat = w[:, :, :].rearrange("p c n -> p (c n)")
                    for h in range(2):
                        part = slice(1024 * h, 1024 * h + 1024)
                        src = stage[:, (UP + k) % 2, part]
                        steps = 5 * k + 3 * h
                        pool.tensor_scalar(below[:], src, tnhalf[:, k:k + 1], 1.0, ALU.is_lt, ALU.mult)\
                            .then_inc(tern_step, 1)
                        pool.wait_ge(tern_step, steps + 1)
                        pool.tensor_scalar(src, src, thalf[:, k:k + 1], 1.0, ALU.is_gt, ALU.mult)\
                            .then_inc(tern_step, 1)
                        pool.wait_ge(tern_step, steps + 2)
                        pool.tensor_tensor(flat[:, part], src, below[:], ALU.subtract)\
                            .then_inc(tern_step if h == 0 else split_end, 1)
                        if h == 0:
                            pool.wait_ge(tern_step, steps + 3)
                        else:
                            pool.wait_ge(split_end, 5 + k)
                pool.tensor_tensor(tsgd[:], tscale[:, 1:2], tscale[:, 2:3], ALU.mult).then_inc(ternary, 1)

            def pads():
                pool.memset(qkt[:, :, 0:NH, AUX:HS].bitcast(F32), 0.0).then_inc(pads_ready, 1)
                pool.memset(qkt[:, :, NH:2 * NH, AUX:AUX + 2].bitcast(F32), 1.0).then_inc(pads_ready, 1)
                pool.memset(qkt[:, :, NH:2 * NH, AUX + 2:HS].bitcast(F32), 0.0).then_inc(pads_ready, 1)

            def rest(b, more):
                rstd_of(b * 3 + 1, 1)
                for m in range(FM):
                    pool.wait_ge(hid_done, b * FM + m + 1)
                    pool.wait_ge(h_hi, b * FM + m + 1)
                    pool.tensor_tensor(hs[:, 1, m], hid[:, m % 2], hs[:, 0, m].bitcast(F32), ALU.subtract)\
                        .then_inc(h_lo, 1)
                    if m == LN0_AGGR and more:
                        rstd_of(b + 2, 0)
                rstd_of(b * 3 + 2, 1)
                pool.wait_ge(xn_ready[1], b * 12 + 2 * TJ)
                pool.tensor_tensor(xres[:], xres[:], bo[:].rearrange("p (a n) -> p a n", a=1).to_broadcast([P, TJ, D]),
                                   ALU.add).then_inc(bias_added, 1)
                if more:
                    pool.wait_ge(xt_psum, b * 2 * NXT + 2 * XT_CTX + 2)
                    pool.tensor_tensor(pfence[:], epsc[:, 0:1], epsc[:, 0:1], ALU.add)
                    pads()
                rstd_of(b * 3 + 3, 1)

            pads()
            rstd_of(1, 0)
            prepare_weights()
            pool.wait_ge(bias_loaded, 64)
            with pool.Fori(0, B - 1) as b:
                rest(b, True)
            rest(B - 1, False)

        @block.vector
        def _(dve):
            def statistics(k, j, src):
                dve.bn_stats(stats[:, k, j], src[:, j]).then_inc(stats_done[k], 1)

            def aggregate(count, k):
                dve.wait_ge(stats_done[k], TJ * count)
                dve.memset(fence[:], 0.0)
                for j in range(TJ):
                    dve.bn_aggr(mv[:, k, j], stats[:, k, j]).then_inc(aggr_done[k], 1)

            def normalised(count, k, src):
                dve.wait_ge(rstd_done[k], count)
                for j in range(TJ):
                    dve.tensor_scalar(xn[:, j], src[:, j], mv[:, k, j, 0:1], rstd[:, k, j:j + 1],
                                      ALU.subtract, ALU.mult).then_inc(xn_ready[k], 1)

            def low_half(b, t, kh, bias=None):
                bank = ps[:, XT_BANK[t] + kh]
                dve.wait_ge(xt_hi, b * 2 * NXT + 2 * t + kh + 1)
                if bias is None:
                    dve.tensor_tensor(xt[:, 1, kh], bank, xt[:, 0, kh].bitcast(F32), ALU.subtract)\
                        .then_inc(xt_lo, 1)
                else:
                    dve.scalar_tensor_tensor(xt[:, 1, kh], bank, bias, xt[:, 0, kh].bitcast(F32),
                                             ALU.add, ALU.subtract).then_inc(xt_lo, 1)

            def low_halves0(b):
                for kh in range(KH):
                    dve.wait_ge(xt0_hi, b * 2 + kh + 1)
                    dve.tensor_tensor(xt0[:, 1, kh], ps[:, XT0_BANK + kh], xt0[:, 0, kh].bitcast(F32), ALU.subtract)\
                        .then_inc(xt0_lo, 1)

            def low_heads(b, j):
                dve.wait_ge(qk_hi, b * 8 + 2 * j + 2)
                bank = ps[:, 2 * (j % 2)].rearrange("p (h c) -> p h c", h=2 * NH)
                dve.tensor_tensor(qkt[:, j, 0:NH, Q_LO:Q_LO + HD], bank[:, 0:NH],
                                  qkt[:, j, 0:NH, 0:HD].bitcast(F32), ALU.subtract).then_inc(qk_lo, 1)
                dve.tensor_tensor(qkt[:, j, NH:2 * NH, K_LO:K_LO + HD], bank[:, NH:2 * NH],
                                  qkt[:, j, NH:2 * NH, 0:HD].bitcast(F32), ALU.subtract).then_inc(qk_lo, 1)

            def attention(b, first):
                for event in ORDER:
                    kind, p, u = event
                    if kind == "turn_k":
                        dve.wait_ge(turned, b * len(TURNS) + TURNS.index(event) + 1)
                        if p >= 4:
                            dve.wait_ge(scored_t, b * 32 + TJ * (p - 3))
                        dve.tensor_copy(kb[P // 2:P, p % 4], ps[P // 2:P, T_BANK]).then_inc(turn_read, 1)
                    elif kind == "score":
                        n = TJ * p + u
                        s = unit_slot(event)
                        dve.wait_ge(scored, b * 32 + n + 1)
                        dve.tensor_reduce(negm[:, p % 2, u], ps[:, 2 * s:2 * s + 2, 0:P * (u + 1)], X, ALU.max,
                                          negate=True).then_inc(max_done, 1)
                        if u == TJ - 1:
                            dve.wait_ge(max_done, b * 32 + n + 1)
                            aux = qkt[:, :, 2 * p:2 * p + 2, AUX]
                            dve.tensor_copy(aux, negm[:, p % 2]).then_inc(m_part, 1)
                            dve.wait_ge(m_part, b * NP + p + 1)
                            dve.tensor_tensor(qkt[:, :, 2 * p:2 * p + 2, AUX + 1], negm[:, p % 2],
                                              aux.bitcast(F32), ALU.subtract).then_inc(m_ready, 1)
                        if not first and p >= ROUTER_PAIR and TJ * (p - ROUTER_PAIR) + u < ROUTER_PARTS:
                            router(b - 1, TJ * (p - ROUTER_PAIR) + u)
                    elif kind == "turn_out":
                        g = p
                        dve.wait_ge(turned, b * len(TURNS) + TURNS.index(event) + 1)
                        rows = ps[:, T_BANK].rearrange("p (j h c) -> p j h c", j=TJ, h=4)
                        dve.reciprocal(zinv[:], rows[:, :, :, HD]).then_inc(zinv_done, 1)
                        dve.wait_ge(zinv_done, b * 4 + g + 1)
                        dve.tensor_tensor(xn[:, :, 4 * HD * g:4 * HD * (g + 1)].rearrange("p j (h c) -> p j h c", h=4),
                                          rows[:, :, :, 0:HD],
                                          zinv[:].rearrange("p j (h a) -> p j h a", a=1).to_broadcast([P, TJ, 4, HD]),
                                          ALU.mult).then_inc(turn_read, 1)
                for kh in range(KH):
                    low_half(b, XT_Z, kh)
                if not first:
                    dve.wait_ge(x3_stored, b * 16)
                for j in range(TJ):
                    dve.wait_ge(attn_psum, b * TJ + j + 1)
                    dve.tensor_tensor(xres[:, j], ps[:, 2 + j, 0:D], xin[:, j], ALU.add).then_inc(x1_ready, 1)

            def feed_forward(b, more):
                for m in range(FM):
                    r = m % 2
                    dve.wait_ge(up_psum, b * 2 * FM + 2 * m + 2)
                    dve.wait_ge(silu_done, b * FM + m + 1)
                    if m >= 2:
                        dve.wait_ge(h_lo, b * FM + m - 1)
                    dve.tensor_tensor(hid[:, r], ps[:, 2 * r + 1], gated[:, r], ALU.mult).then_inc(hid_done, 1)
                    if more and m == LN0_AGGR - 1:
                        dve.wait_ge(x_loaded, b * 16 + 32)
                        for j in range(TJ):
                            statistics(0, j, xin)
                    elif more and m == LN0_AGGR:
                        aggregate(b + 2, 0)
                    elif more and m == LN0_AGGR + 2:
                        normalised(b + 2, 0, xin)
                for j in range(TJ):
                    dve.wait_ge(down_psum, b * TJ + j + 1)
                    if j == 0:
                        dve.wait_ge(ternary, 1)
                    dve.scalar_tensor_tensor(xres[:, j], ps[:, 4 + j, 0:D], tsgd[:, 0:1], xres[:, j],
                                             ALU.mult, ALU.add).then_inc(x2_ready, 1)

            def second_attention(b):
                for m in range(4):
                    dve.wait_ge(qk1_hi, b * 4 + m + 1)
                    dve.scalar_tensor_tensor(qk1[:, 1, m], ps[:, m], bqk[:, m:m + 1], qk1[:, 0, m].bitcast(F32),
                                             ALU.add, ALU.subtract).then_inc(qk1_lo, 1)
                for j in range(TJ):
                    dve.wait_ge(v1_hi, b * TJ + j + 1)
                    dve.tensor_tensor(v1[:, 1, j], ps[:, 4 + j, 0:D], v1[:, 0, j].bitcast(F32), ALU.subtract)\
                        .then_inc(v1_lo, 1)

                def maximum(j):
                    dve.wait_ge(s1_psum, b * TJ + j + 1)
                    dve.tensor_reduce(nm1[:, j:j + 1], ps[:, j], X, ALU.max, negate=True).then_inc(nm1_part, 1)
                    dve.wait_ge(nm1_part, b * TJ + j + 1)
                    dve.tensor_scalar(nm1s[:, j:j + 1], nm1[:, j:j + 1], 1.0 / 16, None, ALU.mult)\
                        .then_inc(nm1_ready, 1)

                def normalise(j):
                    dve.wait_ge(exp1_done, b * TJ + j + 1)
                    dve.reciprocal(ri1[:, j:j + 1], rs1[:, j:j + 1]).then_inc(ri1_done, 1)
                    dve.wait_ge(ri1_done, b * TJ + j + 1)
                    dve.tensor_scalar(p1[:, j], p1[:, j], ri1[:, j:j + 1], None, ALU.mult).then_inc(p1_ready, 1)

                for j in range(TJ):
                    maximum(j)
                    if j:
                        normalise(j - 1)
                normalise(TJ - 1)
                for i in range(TJ):
                    dve.wait_ge(pt1_hi, b * TJ + i + 1)
                    dve.tensor_tensor(ptr[:, 1, i], ps[:, 4 + i], ptr[:, 0, i].bitcast(F32), ALU.subtract)\
                        .then_inc(pt1_lo, 1)
                for kh in range(KH):
                    low_half(b, XT_CTX, kh, bv[:, kh:kh + 1])
                for j in range(TJ):
                    dve.wait_ge(out1_psum, b * TJ + j + 1)
                    if j == 0:
                        dve.wait_ge(bias_added, b + 1)
                    dve.tensor_tensor(xres[:, j], ps[:, 4 + j, 0:D], xres[:, j], ALU.add).then_inc(x3_ready, 1)

            def router(b, part):
                at = b * N_ROUTE
                s = score[:, :, 0:NE]
                if part == 0:
                    dve.wait_ge(elog_done, b + 1)
                    dve.tensor_scalar(prob[:], elog[:], 1.0, None, ALU.add).then_inc(route, 1)
                    dve.wait_ge(route, at + 1)
                    dve.reciprocal(elog[:], prob[:]).then_inc(route, 1)
                elif part == 1:
                    dve.wait_ge(route, at + 2)
                    dve.tensor_tensor(s, elog[:], gb[:].rearrange("p (a e) -> p a e", a=1).to_broadcast(
                        [P, TJ, NE]), ALU.add).then_inc(route, 1)
                elif part == 2:
                    dve.wait_ge(route, at + 3)
                    dve.memset(fence[:], 0.0)
                    for j in range(TJ):
                        dve.max(top8[:, j], score[:, j]).then_inc(route, 1)
                elif part == 3:
                    dve.wait_ge(route, at + 3 + TJ)
                    dve.tensor_reduce(topsum[:], top8[:, :, 0:TOP_K], X, ALU.add).then_inc(route, 1)
                    dve.tensor_copy(top4[:, :, 0:TOP_K], top8[:, :, 0:TOP_K]).then_inc(route, 1)
                elif part == 4:
                    dve.wait_ge(route, at + 5 + TJ)
                    dve.reciprocal(topinv[:], topsum[:]).then_inc(route, 1)
                    for j in range(TJ):
                        dve.match_replace(others[:, j], top4[:, j], score[:, j], -3.0e38).then_inc(route, 1)
                elif part == 5:
                    dve.wait_ge(route, at + 6 + 2 * TJ)
                    dve.tensor_tensor(prob[:], others[:, :, 0:NE], s, ALU.not_equal).then_inc(route, 1)
                    dve.wait_ge(route, at + 7 + 2 * TJ)
                    dve.tensor_tensor(prob[:], prob[:], s, ALU.mult).then_inc(route, 1)
                elif part == 6:
                    dve.wait_ge(route, at + 8 + 2 * TJ)
                    dve.tensor_tensor(elog[:], prob[:], topinv[:].rearrange(
                        "p (j a) -> p j a", a=1).to_broadcast([P, TJ, NE]), ALU.mult).then_inc(route, 1)
                else:
                    dve.wait_ge(route, at + N_ROUTE)
                    dve.tensor_copy(probs[:, :, 0:NE], elog[:]).then_inc(probs_ready, 1)
                    dve.wait_ge(probs_ready, b * 2 + 1)
                    dve.tensor_tensor(probs[:, :, NE:2 * NE], elog[:], probs[:, :, 0:NE].bitcast(F32), ALU.subtract)\
                        .then_inc(probs_ready, 1)

            dve.wait_ge(qkv0_split, 1)
            dve.tensor_tensor(wq0[:, 1], staged(0), wq0[:, 0].bitcast(F32), ALU.subtract).then_inc(qkv0_split, 1)
            dve.wait_ge(bias_loaded, 64)

            def rest(b, more):
                for j in range(TJ):
                    dve.wait_ge(x1_ready, b * TJ + j + 1)
                    statistics(1, j, xres)
                aggregate(b * 3 + 1, 1)
                normalised(b * 3 + 1, 1, xres)
                for kh in range(KH):
                    low_half(b, XT_LN1, kh)
                feed_forward(b, more)
                for j in range(TJ):
                    dve.wait_ge(x2_ready, b * TJ + j + 1)
                    statistics(1, j, xres)
                aggregate(b * 3 + 2, 1)
                if more:
                    low_halves0(b + 1)
                normalised(b * 3 + 2, 1, xres)
                for kh in range(KH):
                    low_half(b, XT_LN2, kh)
                second_attention(b)
                for j in range(TJ):
                    dve.wait_ge(x3_ready, b * TJ + j + 1)
                    statistics(1, j, xres)
                aggregate(b * 3 + 3, 1)
                if more:
                    low_heads(b + 1, 0)
                normalised(b * 3 + 3, 1, xres)
                if more:
                    for j in range(1, TJ):
                        low_heads(b + 1, j)
                for kh in range(KH):
                    low_half(b, XT_LN3, kh)

            dve.wait_ge(x_loaded, 16)
            for j in range(TJ):
                statistics(0, j, xin)
            aggregate(1, 0)
            normalised(1, 0, xin)
            low_halves0(0)
            for j in range(TJ):
                low_heads(0, j)
            attention(0, True)
            with dve.Fori(0, B - 1) as b:
                rest(b, True)
                attention(b + 1, False)
            rest(B - 1, False)
            for part in range(ROUTER_PARTS):
                router(B - 1, part)

        @block.scalar
        def _(act):
            def high_half(b, t, kh, bias=None):
                bank = ps[:, XT_BANK[t] + kh]
                act.wait_ge(xt_psum, b * 2 * NXT + 2 * t + kh + 1)
                if bias is None:
                    act.activation(xt[:, 0, kh], bank, ACT.Copy).then_inc(xt_hi, 1)
                else:
                    act.activation(xt[:, 0, kh], bank, ACT.Identity, bias=bias).then_inc(xt_hi, 1)

            def high_halves0(b):
                for kh in range(KH):
                    act.wait_ge(xt0_psum, b * 2 + kh + 1)
                    act.activation(xt0[:, 0, kh], ps[:, XT0_BANK + kh], ACT.Copy).then_inc(xt0_hi, 1)

            def high_heads(b):
                for j in range(TJ):
                    act.wait_ge(qkv_psum, b * TJ + j + 1)
                    bank = ps[:, 2 * (j % 2)].rearrange("p (h a c) -> p h a c", h=2 * NH, a=1)
                    act.activation(qkt[:, j, 0:NH, 0:AUX].rearrange("p h (a c) -> p h a c", c=HD)[:, :, 0:3:2],
                                   bank[:, 0:NH].to_broadcast([P, NH, 2, HD]), ACT.Copy).then_inc(qk_hi, 1)
                    act.activation(qkt[:, j, NH:2 * NH, 0:AUX].rearrange("p h (a c) -> p h a c", c=HD)[:, :, 0:2],
                                   bank[:, NH:2 * NH].to_broadcast([P, NH, 2, HD]), ACT.Copy).then_inc(qk_hi, 1)
                    act.activation(vh[:, j, :, 0:HD], ps[:, 2 * (j % 2) + 1, 0:D].rearrange("p (h c) -> p h c", h=NH),
                                   ACT.Copy).then_inc(v_ready, 1)

            def keep_routing(b):
                act.wait_ge(probt_psum, b + 1)
                act.activation(probt[:], ps[:, T_BANK], ACT.Copy).then_inc(probt_ready, 1)
                act.wait_ge(probt_ready, b + 1)
                act.dma_start(probs_d[:, bass.ts(b, T)], probt[:].bitcast(F32)).then_inc(kept, 16)

            def attention(b, first):
                for event in ORDER:
                    kind, p, u = event
                    if kind in ("turn_k", "turn_q", "turn_shifted_q"):
                        if kind == "turn_k":
                            to = ka[0:P // 2, p % 4]
                            if p >= 4:
                                act.wait_ge(scored_t, b * 32 + TJ * (p - 3))
                        elif kind == "turn_q":
                            to = q1[:, p % 2]
                            if p >= 2:
                                act.wait_ge(scored, b * 32 + TJ * (p - 1))
                        else:
                            to = q2[:, p % 2]
                            if p >= 2:
                                act.wait_ge(scored_t, b * 32 + TJ * (p - 1))
                        act.wait_ge(turned, b * len(TURNS) + TURNS.index(event) + 1)
                        rows = P // 2 if kind == "turn_k" else P
                        act.activation(to, ps[0:rows, T_BANK], ACT.Copy).then_inc(turn_read, 1)
                    elif kind == "scoreT":
                        n = TJ * p + u
                        s = unit_slot(event)
                        w = T - P * u
                        act.wait_ge(scored_t, b * 32 + n + 1)
                        if n >= 3:
                            act.wait_ge(pv_done, b * 32 + n - 2)
                        act.activation(pt[:, n % 3, :, 0:w], ps[:, 2 * s:2 * s + 2, 0:w], ACT.Exp,
                                       scale=0.25).then_inc(exp_done, 1)
                    elif kind == "copy_out":
                        act.wait_ge(pv_done, b * 32 + 8 * (p + 1))
                        if p >= 2:
                            act.wait_ge(turned, b * len(TURNS) + TURNS.index(("turn_out", p - 2, 0)) + 1)
                        act.activation(ot[:, p % 2], ps[:, PO_BANK], ACT.Copy).then_inc(out_copied, 1)
                    if first and event in (("scoreT", 1, 0), ("scoreT", 3, 0), ("scoreT", 5, 0)):
                        k = p // 2
                        loaded(act, UP + k)
                        act.activation(absout[:], stage[:, (UP + k) % 2, :], ACT.Abs,
                                       accum_out=abssum[:, k:k + 1]).then_inc(abs_summed, 1)
                if not first:
                    act.wait_ge(kept, b * 32 - 16)
                for kh in range(KH):
                    high_half(b, XT_Z, kh)
                if not first:
                    keep_routing(b - 1)

            def feed_forward(b):
                def high(m):
                    act.wait_ge(hid_done, b * FM + m + 1)
                    act.activation(hs[:, 0, m], hid[:, m % 2], ACT.Copy).then_inc(h_hi, 1)

                for m in range(FM):
                    r = m % 2
                    act.wait_ge(up_psum, b * 2 * FM + 2 * m + 1)
                    if m >= 2:
                        act.wait_ge(hid_done, b * FM + m - 1)
                    act.activation(gated[:, r], ps[:, 2 * r], ACT.Silu, scale=tscale[:, 0:1]).then_inc(silu_done, 1)
                    if m:
                        high(m - 1)
                high(FM - 1)

            def second_attention(b):
                for m in range(4):
                    act.wait_ge(qk1_psum, b * 4 + m + 1)
                    act.activation(qk1[:, 0, m], ps[:, m], ACT.Identity, bias=bqk[:, m:m + 1]).then_inc(qk1_hi, 1)
                for j in range(TJ):
                    act.wait_ge(v1_psum, b * TJ + j + 1)
                    act.activation(v1[:, 0, j], ps[:, 4 + j, 0:D], ACT.Copy).then_inc(v1_hi, 1)
                for j in range(TJ):
                    act.wait_ge(nm1_ready, b * TJ + j + 1)
                    act.activation(p1[:, j], ps[:, j], ACT.Exp, bias=nm1s[:, j:j + 1], scale=1.0 / 16,
                                   accum_out=rs1[:, j:j + 1]).then_inc(exp1_done, 1)
                act.wait_ge(pt1_psum, b * TJ + TJ)
                for i in range(TJ):
                    act.activation(ptr[:, 0, i], ps[:, 4 + i], ACT.Copy).then_inc(pt1_hi, 1)
                for kh in range(KH):
                    high_half(b, XT_CTX, kh, bv[:, kh:kh + 1])

            def rest(b, more):
                for kh in range(KH):
                    high_half(b, XT_LN1, kh)
                feed_forward(b)
                if more:
                    high_halves0(b + 1)
                for kh in range(KH):
                    high_half(b, XT_LN2, kh)
                second_attention(b)
                if more:
                    high_heads(b + 1)
                for kh in range(KH):
                    high_half(b, XT_LN3, kh)
                act.wait_ge(xt_lo, b * 2 * NXT + 2 * NXT)
                act.dma_start(xt4_d[:, :, :, bass.ts(b, T)], xt[:].bitcast(F32)).then_inc(kept, 16)
                act.wait_ge(logits_psum, b + 1)
                act.activation(elog[:], ps[:, LOGIT_BANK, 0:TJ * NE].rearrange("p (j e) -> p j e", j=TJ), ACT.Exp,
                               scale=-1.0).then_inc(elog_done, 1)

            loaded(act, 0)
            act.activation(wq0[:, 0], staged(0), ACT.Copy).then_inc(qkv0_split, 1)
            act.wait_ge(bias_loaded, 64)
            high_halves0(0)
            high_heads(0)
            attention(0, True)
            with act.Fori(0, B - 1) as b:
                rest(b, True)
                attention(b + 1, False)
            rest(B - 1, False)
            act.wait_ge(kept, 32 * B - 16)
            keep_routing(B - 1)

        @block.tensor
        def _(pe):
            def turn_halves(bank, src, done, ready):
                for kh in range(KH):
                    for j in range(TJ):
                        if kh == 0:
                            ready(j)
                        mm = pe.transpose(ps[:, bank + kh, P * j:P * (j + 1)], src[:, j, P * kh:P * (kh + 1)], ident[:])
                    mm.then_inc(done, 1)

            def turn_norm(b, t, n):
                turn_halves(XT_BANK[t], xn, xt_psum, lambda j: pe.wait_ge(xn_ready[1], b * 12 + TJ * (n - 1) + j + 1))

            def halves_ready(b, t):
                for kh in range(KH):
                    pe.wait_ge(xt_lo, b * 2 * NXT + 2 * t + kh + 1)

            def product(out, left, right, start=True, stop=True):
                terms = [(l, r, kh) for kh in range(KH) for l, r in ((0, 0), (1, 0), (0, 1))]
                for n, (l, r, kh) in enumerate(terms):
                    mm = pe.matmul(out, left(l, kh), right(r, kh), start=start and n == 0,
                                   stop=stop and n == len(terms) - 1)
                return mm

            def x_tile(j):
                return lambda part, kh: xt[:, part, kh, P * j:P * (j + 1)]

            def turn_norm0(b):
                turn_halves(XT0_BANK, xn, xt0_psum, lambda j: pe.wait_ge(xn_ready[0], b * TJ + j + 1))

            def project(b):
                for kh in range(KH):
                    pe.wait_ge(xt0_lo, b * 2 + kh + 1)
                for j in range(TJ):
                    r = j % 2
                    if j >= 2:
                        pe.wait_ge(qk_lo, b * 8 + 2 * (j - 1))
                        pe.wait_ge(v_ready, b * TJ + j - 1)

                    def tokens(part, kh):
                        return xt0[:, part, kh, P * j:P * (j + 1)]

                    product(ps[:, 2 * r], tokens, lambda part, kh: wq0[:, part, kh, 0:2 * D])
                    product(ps[:, 2 * r + 1, 0:D], tokens, lambda part, kh: wq0[:, part, kh, 2 * D:3 * D])\
                        .then_inc(qkv_psum, 1)

            def turn_probs(b):
                pe.wait_ge(probs_ready, b * 2 + 2)
                for j in range(TJ):
                    mm = pe.transpose(ps[:, T_BANK, P * j:P * (j + 1)], probs[:, j].bitcast(F32), ident[:])
                mm.then_inc(probt_psum, 1)

            def attention(b, first):
                pe.wait_ge(qk_lo, b * 8 + 8)
                pe.wait_ge(pads_ready, b * 3 + 3)
                for event in ORDER:
                    kind, p, u = event
                    if kind.startswith("turn"):
                        n = TURNS.index(event)
                        if n:
                            pe.wait_ge(turn_read, b * N_TURN_READS + turn_reads(TURNS[n - 1]))
                        if kind == "turn_shifted_q":
                            pe.wait_ge(m_ready, b * NP + p + 1)
                        if kind == "turn_out":
                            pe.wait_ge(out_copied, b * 4 + p + 1)
                        for j in range(TJ):
                            if kind == "turn_out":
                                src = ot[:, p % 2, P * j:P * (j + 1)]
                            else:
                                h = 2 * p + (NH if kind == "turn_k" else 0)
                                src = qkt[:, j, h:h + 2].rearrange("p h c -> p (h c)").bitcast(F32)
                            mm = pe.transpose(ps[:, T_BANK, P * j:P * (j + 1)], src, ident[:])
                        mm.then_inc(turned, 1)
                    elif kind in ("score", "scoreT"):
                        n = UNITS.index(event)
                        s = unit_slot(event)
                        if n >= 3:
                            before, bp, bu = UNITS[n - 3]
                            pe.wait_ge(max_done if before == "score" else exp_done, b * 32 + TJ * bp + bu + 1)
                        if event == UNITS[0]:
                            pe.wait_ge(v_ready, b * TJ + TJ)
                        if u == 0:
                            q = ("turn_q" if kind == "score" else "turn_shifted_q", p, 0)
                            pe.wait_ge(turn_read, b * N_TURN_READS + turn_reads(q))
                        for h, keys in enumerate((ka, kb)):
                            if kind == "score":
                                w, d = P * (u + 1), P * u
                                pe.matmul(ps[:, 2 * s + h, 0:w], q1[:, p % 2, P * u:P * (u + 1)],
                                          keys[:, p % 4, 0:w], start=True, stop=False)
                                mm = pe.matmul(ps[:, 2 * s + h, d:d + P], identb[:], mask_q[:],
                                               start=False, stop=True)
                            else:
                                w = T - P * u
                                pe.matmul(ps[:, 2 * s + h, 0:w], keys[:, p % 4, P * u:P * (u + 1)],
                                          q2[:, p % 2, P * u:T], start=True, stop=False)
                                mm = pe.matmul(ps[:, 2 * s + h, 0:P], identb[:], mask_k[:],
                                               start=False, stop=True)
                        mm.then_inc(scored if kind == "score" else scored_t, 1)
                    elif kind == "value":
                        n = TJ * p + u
                        w = T - P * u
                        pe.wait_ge(exp_done, b * 32 + n + 1)
                        if n == 0 and not first:
                            pe.wait_ge(elog_done, b)
                        if p % 2 == 0 and u == 0 and p:
                            pe.wait_ge(out_copied, b * 4 + p // 2)
                        for h in range(2):
                            at = 32 * (2 * (p % 2) + h)
                            mm = pe.matmul(ps[at:at + 32, PO_BANK, P * u:T], vh[:, u, 2 * p + h],
                                           pt[:, n % 3, h, 0:w], start=u == 0, stop=u == TJ - 1)
                        mm.then_inc(pv_done, 1)
                turn_halves(XT_BANK[XT_Z], xn, xt_psum,
                            lambda j: pe.wait_ge(turn_read, b * N_TURN_READS + N_TURN_READS))
                if not first:
                    turn_probs(b - 1)
                halves_ready(b, XT_Z)
                pe.wait_ge(split_end, 1)
                for j in range(TJ):
                    product(ps[:, 2 + j, 0:D], x_tile(j), lambda part, kh: wo0s[:, part, kh]).then_inc(attn_psum, 1)
                if not first:
                    pe.wait_ge(probt_ready, b)

            def feed_forward(b):
                halves_ready(b, XT_LN1)
                pe.wait_ge(ternary, 1)

                def down(m):
                    pe.wait_ge(h_lo, b * FM + m + 1)
                    for j in range(TJ):
                        for part in range(2):
                            mm = pe.matmul(ps[:, 4 + j, 0:D], hs[:, part, m, P * j:P * (j + 1)], tdown[:, m],
                                           start=m == 0 and part == 0, stop=m == FM - 1 and part == 1)
                        if m == FM - 1:
                            mm.then_inc(down_psum, 1)

                for m in range(FM + 2):
                    if m < FM:
                        r = m % 2
                        if m >= 2:
                            pe.wait_ge(hid_done, b * FM + m - 1)
                        for w, bank in ((tup, 2 * r), (tgate, 2 * r + 1)):
                            for kh in range(KH):
                                for part in range(2):
                                    mm = pe.matmul(ps[:, bank], w[:, kh, P * m:P * (m + 1)], xt[:, part, kh],
                                                   start=kh == 0 and part == 0, stop=kh == 1 and part == 1)
                            mm.then_inc(up_psum, 1)
                    if m >= 2:
                        down(m - 2)

            def second_attention(b, more):
                halves_ready(b, XT_LN2)
                pe.wait_ge(split_end, 2)
                for m in range(4):
                    if more and m == XT0_BANK:
                        pe.wait_ge(xt0_lo, b * 2 + 4)
                    product(ps[:, m], lambda part, kh: wq1[:, part, kh, P * m:P * (m + 1)],
                            lambda part, kh: xt[:, part, kh]).then_inc(qk1_psum, 1)
                for j in range(TJ):
                    product(ps[:, 4 + j, 0:D], x_tile(j), lambda part, kh: wq1[:, part, kh, 2 * D:3 * D])\
                        .then_inc(v1_psum, 1)
                pe.wait_ge(qk1_lo, b * 4 + 4)
                for j in range(TJ):
                    product(ps[:, j], lambda part, kh: qk1[:, part, kh, P * j:P * (j + 1)],
                            lambda part, kh: qk1[:, part, 2 + kh]).then_inc(s1_psum, 1)
                pe.wait_ge(v1_lo, b * TJ + TJ)
                for j in range(TJ):
                    pe.wait_ge(p1_ready, b * TJ + j + 1)
                    for i in range(TJ):
                        mm = pe.transpose(ps[:, 4 + i, P * j:P * (j + 1)], p1[:, j, P * i:P * (i + 1)], ident[:])
                    mm.then_inc(pt1_psum, 1)
                for hh in range(KH):
                    for i in range(TJ):
                        if hh == 0:
                            pe.wait_ge(pt1_lo, b * TJ + i + 1)
                        for l, r in ((0, 0), (1, 0), (0, 1)):
                            mm = pe.matmul(ps[:, hh], v1[:, l, i, P * hh:P * (hh + 1)], ptr[:, r, i],
                                           start=i == 0 and l == 0 and r == 0, stop=i == TJ - 1 and r == 1)
                    mm.then_inc(xt_psum, 1)
                halves_ready(b, XT_CTX)
                pe.wait_ge(split_end, 3)
                for j in range(TJ):
                    product(ps[:, 4 + j, 0:D], x_tile(j), lambda part, kh: wo1s[:, part, kh]).then_inc(out1_psum, 1)

            def router(b):
                halves_ready(b, XT_LN3)
                pe.wait_ge(split_end, 4)
                for j in range(TJ):
                    mm = product(ps[:, LOGIT_BANK, NE * j:NE * (j + 1)], x_tile(j), lambda part, kh: gws[:, part, kh])
                mm.then_inc(logits_psum, 1)

            def rest(b, more):
                turn_norm(b, XT_LN1, 1)
                feed_forward(b)
                if more:
                    turn_norm0(b + 1)
                turn_norm(b, XT_LN2, 2)
                second_attention(b, more)
                if more:
                    project(b + 1)
                turn_norm(b, XT_LN3, 3)
                router(b)

            pe.wait_ge(consts, N_CONSTS)
            turn_norm0(0)
            pe.wait_ge(qkv0_split, 2)
            project(0)
            attention(0, True)
            with pe.Fori(0, B - 1) as b:
                rest(b, True)
                attention(b + 1, False)
            rest(B - 1, False)
            turn_probs(B - 1)


def experts(nc, w1, w3, w2, sel, x3_d, xt4_d, probs_d, out):
    with ExitStack() as ctx:
        def sb(name, shape, dt=F32):
            return ctx.enter_context(nc.sbuf_tensor(name, shape, dt))

        def sem(name):
            return ctx.enter_context(nc.semaphore(name))

        ps = ctx.enter_context(nc.psum_tensor("eps", [P, 8, 512], F32))
        xt4 = sb("xt4", [P, 2, KH, NTOK], F32R)
        prt = sb("prt", [P, NTOK], F32R)
        x3 = sb("x3", [P, NTOK // P, D])
        acc = sb("acc", [P, KH, NTOK])
        ident = sb("eident", [P, P])
        st13 = sb("st13", [P, 2, 2, KH, PAIR])
        st2 = sb("st2", [P, 2, 2, D])
        stsel = sb("stsel", [P, 2, PAIR])
        w13s = sb("w13s", [P, 2, 2, 2, KH, PAIR], F32R)
        w2s = sb("w2s", [P, 2, 2, 2, D], F32R)
        sels = sb("sels", [P, 2, PAIR], F32R)
        h1 = sb("h1", [P, 2, T])
        gate = sb("gate", [P, 2, T])
        act_h = sb("act_h", [P, 2, T])
        y = sb("y", [P, 2, T])
        ys = sb("ys", [P, 4, 2, T], F32R)

        zeroed = sem("e_zeroed")
        ident_ready = sem("e_ident_ready")
        xt4_loaded = sem("xt4_loaded")
        prt_loaded = sem("prt_loaded")
        x3_loaded = sem("x3_loaded")
        w_loaded = [sem("e_w_loaded_even"), sem("e_w_loaded_odd")]
        w_hi = sem("e_w_hi")
        w_lo = sem("e_w_lo")
        up_psum = sem("e_up_psum")
        spread_psum = sem("e_spread_psum")
        h1_copied = sem("h1_copied")
        gate_done = sem("gate_done")
        silu_done = sem("e_silu_done")
        y_ready = sem("y_ready")
        y_hi = sem("y_hi")
        y_lo = sem("y_lo")
        y_used = sem("y_used")
        half_psum = sem("half_psum")
        acc_zeroed = sem("acc_zeroed")
        acc_done = sem("acc_done")
        acc_turned = sem("acc_turned")
        summed = sem("summed")
        stored = sem("stored")

        block = ctx.enter_context(nc.Block())
        NU = 2 * B
        LOOPS = (NPAIRS - 2) // 2

        def steps(eng, step):
            step(0, 0)
            with eng.Fori(0, LOOPS) as k:
                step(2 * k + 1, 1)
                step(2 * k + 2, 0)
            step(NPAIRS - 1, 1)

        @block.sync
        def _(sp):
            def load(u, slot):
                cols = bass.ts(u, PAIR)
                w1_at = w1[:, cols].rearrange("(c p) n -> p c n", p=P)
                w3_at = w3[:, cols].rearrange("(c p) n -> p c n", p=P)
                w2_at = w2[cols, :].rearrange("(c p) n -> p c n", p=P)
                sel_at = sel[:, cols]
                if not isinstance(u, int):
                    sp.wait_ge(w_lo, 2 * (u - 1))
                sp.dma_start(st13[:, slot, 0], w1_at).then_inc(w_loaded[slot], 16)
                sp.dma_start(st13[:, slot, 1], w3_at).then_inc(w_loaded[slot], 16)
                sp.dma_start(st2[:, slot], w2_at).then_inc(w_loaded[slot], 16)
                sp.dma_start(stsel[:, slot], sel_at).then_inc(w_loaded[slot], 16)

            load(0, 0)
            for c in range(B):
                sp.dma_start(xt4[:, :, :, bass.ts(c, T)].bitcast(F32), xt4_d[:, :, :, bass.ts(c, T)]).then_inc(xt4_loaded, 16)
            load(1, 1)
            sp.dma_start(prt[:].bitcast(F32), probs_d).then_inc(prt_loaded, 16)
            sp.dma_start(x3[:], x3_d.rearrange("(j p) n -> p j n", p=P)).then_inc(x3_loaded, 16)
            with sp.Fori(1, LOOPS + 1) as k:
                load(2 * k, 0)
                load(2 * k + 1, 1)
            for c in range(B):
                sp.wait_ge(summed, c + 1)
                sp.dma_start(out[bass.ts(c, T), :].rearrange("(j p) n -> p j n", p=P),
                             x3[:, TJ * c:TJ * (c + 1)]).then_inc(stored, 16)
            sp.wait_ge(stored, 16 * B)

        @block.gpsimd
        def _(pool):
            pool.memset(ident[:], 0.0).then_inc(zeroed, 1)
            pool.wait_ge(zeroed, 1)
            pool.affine_select(out=ident[:], in_=ident[:], compare_op=ALU.not_equal, fill=1.0, base=0,
                               pattern=[[-1, P]], channel_multiplier=1).then_inc(ident_ready, 1)

            def split_low(u, slot):
                pool.wait_ge(w_hi, 3 * u + 3)
                pool.tensor_tensor(w13s[:, slot, 1], st13[:, slot], w13s[:, slot, 0].bitcast(F32), ALU.subtract)\
                    .then_inc(w_lo, 1)
                pool.tensor_tensor(w2s[:, slot, 1], st2[:, slot], w2s[:, slot, 0].bitcast(F32), ALU.subtract)\
                    .then_inc(w_lo, 1)

            def step(u, slot):
                for n in range(NU):
                    pool.wait_ge(y_hi, NU * u + n + 1)
                    pool.tensor_tensor(ys[:, n % 4, 1], y[:, n % 2], ys[:, n % 4, 0].bitcast(F32), ALU.subtract)\
                        .then_inc(y_lo, 1)
                    if n == 3 and not (isinstance(u, int) and u == NPAIRS - 1):
                        split_low(u + 1, 1 - slot)

            pool.memset(acc[:], 0.0).then_inc(acc_zeroed, 1)
            split_low(0, 0)
            steps(pool, step)

        @block.scalar
        def _(act):
            def split(u, slot, round_):
                act.wait_ge(w_loaded[slot], 64 * round_ + 64)
                act.activation(w13s[:, slot, 0], st13[:, slot], ACT.Copy).then_inc(w_hi, 1)
                act.activation(w2s[:, slot, 0], st2[:, slot], ACT.Copy).then_inc(w_hi, 1)
                act.activation(sels[:, slot], stsel[:, slot], ACT.Copy).then_inc(w_hi, 1)

            def step(u, slot, next_round, shared=False, last=False):
                for n in range(NU):
                    r = n % 2
                    act.wait_ge(up_psum, NU * u + n + 1)
                    if shared:
                        if n >= 2:
                            act.wait_ge(y_ready, n - 1)
                        act.activation(h1[:, r], ps[:, 3 * r], ACT.Silu).then_inc(h1_copied, 1)
                    else:
                        act.activation(h1[:, r], ps[:, 3 * r], ACT.Copy).then_inc(h1_copied, 1)
                        act.wait_ge(gate_done, NU * (u - 1) + n + 1)
                        act.activation(act_h[:, r], gate[:, r], ACT.Silu).then_inc(silu_done, 1)
                    act.wait_ge(y_ready, NU * u + n + 1)
                    if not (shared and n < 4):
                        act.wait_ge(y_used, NU * u + n - 3)
                    act.activation(ys[:, n % 4, 0], y[:, r], ACT.Copy).then_inc(y_hi, 1)
                    if n == 3 and not last:
                        if not shared:
                            act.wait_ge(y_used, NU * u)
                        split(u + 1, 1 - slot, next_round)

            split(0, 0, 0)
            step(0, 0, 0, shared=True)
            with act.Fori(0, LOOPS) as k:
                step(2 * k + 1, 1, k + 1)
                step(2 * k + 2, 0, k + 1)
            step(NPAIRS - 1, 1, 0, last=True)

        @block.vector
        def _(dve):
            def accumulate(c, chunk):
                dve.wait_ge(half_psum, c + 1)
                dve.tensor_tensor(acc[:, 0, bass.ts(chunk, T)], ps[:, 6], acc[:, 0, bass.ts(chunk, T)], ALU.add)\
                    .then_inc(acc_done, 1)
                dve.wait_ge(y_used, 2 * c + 2)
                dve.tensor_tensor(acc[:, 1, bass.ts(chunk, T)], ps[:, 7], acc[:, 1, bass.ts(chunk, T)], ALU.add)\
                    .then_inc(acc_done, 1)

            def step(u, slot):
                shared = isinstance(u, int) and u == 0
                for n in range(NU):
                    r = n % 2
                    dve.wait_ge(h1_copied, NU * u + n + 1)
                    if shared:
                        if n >= 2:
                            dve.wait_ge(y_lo, n - 1)
                        dve.tensor_tensor(y[:, r], ps[:, 3 * r + 1], h1[:, r], ALU.mult).then_inc(y_ready, 1)
                    else:
                        dve.tensor_tensor(gate[:, r], ps[:, 3 * r + 1], h1[:, r], ALU.mult).then_inc(gate_done, 1)
                        dve.wait_ge(spread_psum, NU * (u - 1) + n + 1)
                        dve.wait_ge(y_lo, NU * u + n - 1)
                        dve.wait_ge(silu_done, NU * (u - 1) + n + 1)
                        dve.tensor_tensor(y[:, r], ps[:, 3 * r + 2], act_h[:, r], ALU.mult).then_inc(y_ready, 1)
                    if n % 2 and not (shared and n == 1):
                        c = n // 2 - 1
                        if c < 0:
                            accumulate(B * u - 1, B - 1)
                        else:
                            accumulate(B * u + c, c)

            dve.wait_ge(acc_zeroed, 1)
            steps(dve, step)
            accumulate(B * NPAIRS - 1, B - 1)
            dve.wait_ge(x3_loaded, 16)
            for c in range(B):
                dve.wait_ge(acc_turned, c + 1)
                rows = x3[:, TJ * c:TJ * (c + 1)]
                at = 4 * (c % 2)
                dve.tensor_tensor(rows, ps[:, at:at + 2].rearrange("p a (j n) -> p (a j) n", j=2), rows, ALU.add)\
                    .then_inc(summed, 1)

        @block.tensor
        def _(pe):
            def up(u, slot, n):
                r, c, s = n % 2, n // 2, n % 2
                shared = isinstance(u, int) and u == 0
                if not (shared and n < 2):
                    pe.wait_ge(y_ready, NU * u + n - 1)
                if shared and s == 0:
                    pe.wait_ge(xt4_loaded, 64)
                if n == 0:
                    pe.wait_ge(w_hi, 3 * u + 3)
                    pe.wait_ge(w_lo, 2 * u + 2)
                for k in range(2):
                    terms = [(l, q, kh) for kh in range(KH) for l, q in ((0, 0), (1, 0), (0, 1))]
                    for i, (l, q, kh) in enumerate(terms):
                        mm = pe.matmul(ps[:, 3 * r + k], w13s[:, slot, l, k, kh, P * s:P * (s + 1)],
                                       xt4[:, q, kh, T * c:T * (c + 1)], start=i == 0, stop=i == len(terms) - 1)
                mm.then_inc(up_psum, 1)
                if not shared:
                    if n == 0:
                        pe.wait_ge(prt_loaded, 16)
                    pe.matmul(ps[:, 3 * r + 2], sels[:, slot, P * s:P * (s + 1)], prt[:, T * c:T * (c + 1)],
                              start=True, stop=True).then_inc(spread_psum, 1)

            def down(u, slot, n):
                c, s = n // 2, n % 2
                shared = isinstance(u, int) and u == 0
                if s == 0 and not (shared and n == 0):
                    pe.wait_ge(acc_done, 2 * (B * u + c))
                pe.wait_ge(y_lo, NU * u + n + 1)
                for half in range(KH):
                    for l, q in ((0, 0), (1, 0), (0, 1)):
                        mm = pe.matmul(ps[:, 6 + half], w2s[:, slot, l, s, P * half:P * (half + 1)], ys[:, n % 4, q],
                                       start=s == 0 and l == 0 and q == 0, stop=s == 1 and q == 1)
                    if s == 1 and half == 0:
                        mm.then_inc(half_psum, 1)
                mm.then_inc(y_used, 1)

            def step(u, slot):
                shared = isinstance(u, int) and u == 0
                for n in range(NU):
                    up(u, slot, n)
                    if n >= 2:
                        down(u, slot, n - 2)
                    elif not shared:
                        down(u - 1, 1 - slot, NU - 2 + n)

            steps(pe, step)
            down(NPAIRS - 1, 1, NU - 2)
            down(NPAIRS - 1, 1, NU - 1)
            pe.wait_ge(ident_ready, 1)
            for c in range(B):
                pe.wait_ge(acc_done, 2 * (B * (NPAIRS - 1) + c + 1))
                if c == 0:
                    pe.wait_ge(y_ready, NU * NPAIRS)
                if c >= 2:
                    pe.wait_ge(summed, c - 1)
                for j in range(TJ):
                    for half in range(KH):
                        at = D * (j % 2) + P * half
                        first = T * c + P * j
                        mm = pe.transpose(ps[:, 4 * (c % 2) + j // 2, at:at + P], acc[:, half, first:first + P],
                                          ident[:])
                mm.then_inc(acc_turned, 1)


def program(nc, t, out):
    x3_d = nc.dram_tensor("x3_kept", [NTOK, D], F32).ap()
    xt4_d = nc.dram_tensor("xt4_kept", [P, 2, KH, NTOK], F32).ap()
    probs_d = nc.dram_tensor("probs_kept", [P, NTOK], F32).ap()
    layers(nc, t["x"], t["wqkv0"], t["wo0"], t["w_up"], t["w_gate"], t["w_down"], t["wqkv1"], t["bqk1"], t["bv1"],
           t["wo1"], t["bo1"], t["gate_w"], t["gate_b"], x3_d, xt4_d, probs_d)
    experts(nc, t["w1"], t["w3"], t["w2"], t["sel"], x3_d, xt4_d, probs_d, out)


def kernel(**inputs):
    import numpy as np
    import concourse.bacc as bacc
    from concourse.bass_utils import run_bass_kernel_spmd as run

    a = {k: np.asarray(v) for k, v in inputs.items()}

    def padded(shared, axis):
        fill = [(0, 0), (0, 0)]
        fill[axis] = (0, PAIR - EH)
        return np.pad(shared, fill)

    def by_input(routed):
        return routed.transpose(1, 0, 2).reshape(D, HID)

    sel = np.zeros((P, PAIR + HID), np.float32)
    for e in range(NE):
        sel[e, PAIR + EH * e:PAIR + EH * (e + 1)] = 1.0
        sel[NE + e, PAIR + EH * e:PAIR + EH * (e + 1)] = 1.0

    wqkv1, bqkv1 = a["L1_attn_w_qkv"], a["L1_attn_b_qkv"]
    arrays = {
        "x": a["L0_attn_x"].reshape(NTOK, D),
        "wqkv0": np.concatenate([a["L0_attn_Wq"].T, a["L0_attn_Wk"].T, a["L0_attn_Wv"].T], 1),
        "wo0": a["L0_attn_Wo"].T,
        "w_up": a["L0_ffn_W_up"].T,
        "w_gate": a["L0_ffn_W_gate"].T,
        "w_down": a["L0_ffn_W_down"].T,
        "wqkv1": wqkv1.T,
        "bqk1": bqkv1[0:2 * D].reshape(4, P).T,
        "bv1": bqkv1[2 * D:3 * D].reshape(2, P).T,
        "wo1": a["L1_attn_w_out"].T,
        "bo1": a["L1_attn_b_out"].reshape(1, D),
        "gate_w": a["L1_ffn_gate_w"].T,
        "gate_b": a["L1_ffn_gate_b"].reshape(1, NE),
        "w1": np.concatenate([padded(a["L1_ffn_w1_shared"], 1), by_input(a["L1_ffn_w1_routed"])], 1),
        "w3": np.concatenate([padded(a["L1_ffn_w3_shared"], 1), by_input(a["L1_ffn_w3_routed"])], 1),
        "w2": np.concatenate([padded(a["L1_ffn_w2_shared"], 0), a["L1_ffn_w2_routed"].reshape(HID, D)], 0),
        "sel": sel,
    }
    arrays = {k: np.ascontiguousarray(v) for k, v in arrays.items()}
    nc = bacc.Bacc("TRN2", target_bir_lowering=False, num_devices=1)
    t = {k: nc.dram_tensor(k + "_in", v.shape, F32, kind="ExternalInput").ap() for k, v in arrays.items()}
    out = nc.dram_tensor("out", [NTOK, D], F32, kind="ExternalOutput").ap()
    program(nc, t, out)
    r = run(nc, [{k + "_in": v for k, v in arrays.items()}], core_ids=[0])
    return r.results[0]["out"].reshape(B, T, D)
```

```python
from contextlib import ExitStack

import concourse.bass as bass
from concourse import mybir

ALU = mybir.AluOpType
ACT = mybir.ActivationFunctionType
F32 = mybir.dt.float32
F32R = mybir.dt.float32r
BF16 = mybir.dt.bfloat16
X = mybir.AxisListType.X

P = 128
D = 256
KH = D // P
B, T = 4, 512
TJ = T // P
NTOK = B * T
NH, HD = 16, 16
NP = NH // 2
HS = 64
Q_LO, K_LO, AUX = 16, 32, 48
FF = 1024
FM = FF // P
NE, EH = 16, 176
HID = NE * EH
TOP_K = 4
PAIR = 2 * P
NPAIRS = 1 + HID // PAIR
GROUP = 16
NEG = -1.0e30
EPS = 1e-5
TEPS = 1e-8
LOGIT_PAD = 20

XT_Z, XT_LN1, XT_LN2, XT_LN3 = range(4)
NXT = 4
XT_BANK = {XT_Z: 2, XT_LN1: 0, XT_LN2: 0, XT_LN3: 4}
XT0_BANK = 0
V_BANK = 2
WO_BANK = (4, 5, 0, 1)
HALF = T // 2
ROUTER_PARTS = 7
ROUTER_PAIR = 1
LN0_AGGR = 3
LAG = 2
T_BANK, PO_BANK = 6, 7
LOGIT_BANK = PO_BANK


TURN_AT = ((0, 0), (1, 1), (2, 1), (3, 1))


def attention_order():
    order = []
    for s in range(-1, NP + LAG + 1):
        done = s - LAG - 1
        turns = [("turn_k", s + 1, TURN_AT[0]), ("turn_q", s + 1, TURN_AT[1]), ("turn_shifted_q", s - 1, TURN_AT[2])]
        if done >= 0 and done % 2:
            order.append(("copy_out", done // 2, 0))
            turns.append(("turn_out", done // 2, TURN_AT[3]))
        for u in range(TJ):
            for place in range(3):
                for kind, p, at in turns:
                    if at == (u, place) and (kind == "turn_out" or 0 <= p < NP):
                        order.append((kind, p, 0))
                if place == 0 and 0 <= s < NP:
                    order.append(("score", s, u))
                if place == 1 and 0 <= s - LAG < NP:
                    order.append(("scoreT", s - LAG, u))
                if place == 0 and u >= 2 and 0 <= s - LAG < NP:
                    order.append(("value", s - LAG, u - 2))
        if 0 <= s - LAG < NP:
            order.append(("value", s - LAG, TJ - 2))
        if 0 <= s - LAG < NP:
            order.append(("value", s - LAG, TJ - 1))
    return order


ORDER = attention_order()
UNITS = [x for x in ORDER if x[0] in ("score", "scoreT")]
TURNS = [x for x in ORDER if x[0].startswith("turn")]
TURN_READS = {"turn_k": 2, "turn_q": 1, "turn_shifted_q": 1, "turn_out": 1}
N_TURN_READS = sum(TURN_READS[k] for k, _, _ in TURNS)


TERNARY_AT = ((4, 0), (5, 3), (7, 3))
ABS_AT = (("scoreT", 0, 0), ("scoreT", 1, 0), ("scoreT", 3, 0))
NORM3_AT = ORDER[0]
LOGITS_AT = ("score", 0, 1)
Z_AT = ("value", NP - 1, TJ - 2)
assert NORM3_AT[0] == "turn_k"


def turn_reads(event):
    n = TURNS.index(event)
    return sum(TURN_READS[k] for k, _, _ in TURNS[: n + 1])


def unit_slot(unit):
    return UNITS.index(unit) % 3


def load_expert_step(sp, wstage, u, slot, w1, w3, w2, done):
    ats = [w1[:, bass.ts(u, PAIR)], w3[:, bass.ts(u, PAIR)], w2[bass.ts(u, PAIR), :]]
    for k in range(3):
        sp.dma_start(wstage[:, slot, k], ats[k].rearrange("(c p) n -> p c n", p=P)).then_inc(done, 16)


def layers(nc, x, wqkv0, wo0, w_up, w_gate, w_down, wqkv1, bqk1, bv1, wo1, bo1, gate_w, gate_b,
           w1, w3, w2, x3_d, routing_d, stage, below, absout, xt4, big, wstage, kept):
    with ExitStack() as ctx:
        def sb(name, shape, dt=F32):
            return ctx.enter_context(nc.sbuf_tensor(name, shape, dt))

        def sem(name):
            return ctx.enter_context(nc.semaphore(name))

        ps = ctx.enter_context(nc.psum_tensor("ps", [P, 8, 512], F32))

        wq0 = sb("wq0", [P, 2, KH, 3 * D], F32R)
        wo0s = sb("wo0s", [P, 2, KH, D], F32R)
        wq1 = sb("wq1", [P, 2, KH, 3 * D], F32R)
        wo1s = sb("wo1s", [P, 2, KH, D], F32R)
        gws = sb("gws", [P, 2, KH, NE], F32R)
        tup = sb("tup", [P, KH, FF], F32R)
        tgate = sb("tgate", [P, KH, FF], F32R)
        tdown = sb("tdown", [P, FM, D], F32R)
        abssum = sb("abssum", [P, 3])
        abstot = sb("abstot", [P, 3])
        meaneps = sb("meaneps", [P, 3])
        tscale = sb("tscale", [P, 3])
        thalf = sb("thalf", [P, 3])
        tnhalf = sb("tnhalf", [P, 3])
        tsgd = sb("tsgd", [P, 1])
        bqk = sb("bqk", [P, 4])
        bv = sb("bv", [P, 2])
        bo = sb("bo", [P, D])
        gb = sb("gb", [P, NE])

        ident = sb("ident", [P, P])
        identb = sb("identb", [P, P], BF16)
        mask_q = sb("mask_q", [P, P], BF16)
        mask_k = sb("mask_k", [P, P], BF16)
        epsc = sb("epsc", [P, TJ])
        halfc = sb("halfc", [P, TJ])

        xin = sb("xin", [P, TJ, D])
        xres = sb("xres", [P, TJ, D])
        xn = sb("xn", [P, TJ, D])
        xt = sb("xt", [P, 2, KH, T], F32R)
        xt0 = sb("xt0", [P, 2, KH, T], F32R)
        vh = sb("vh", [P, TJ, NH, 32])
        ka = sb("ka", [P, 4, T], F32R)
        kb = sb("kb", [P, 4, T], F32R)
        qv = sb("qv", [P, 4 * T], F32R)
        pt = sb("pt", [P, 3, 2, T])
        ot = sb("ot", [P, 2, T])

        fence = sb("fence", [P, 1])
        pfence = sb("pfence", [P, 1])
        stats = sb("stats", [P, 2, TJ, 6])
        mv = sb("mv", [P, 2, TJ, 2])
        vareps = sb("vareps", [P, 2, TJ])
        rstd = sb("rstd", [P, 2, TJ])
        negm = sb("negm", [P, 2, TJ, 2])
        zinv = sb("zinv", [P, TJ, 4])
        nm1 = sb("nm1", [P, TJ])
        nm1s = sb("nm1s", [P, TJ])
        rs1 = sb("rs1", [P, TJ])
        ri1 = sb("ri1", [P, TJ])
        elog = sb("elog", [P, TJ, NE])
        score = sb("score", [P, TJ, LOGIT_PAD])
        top8 = sb("top8", [P, TJ, 8])
        top4 = sb("top4", [P, TJ, 8])
        topsum = sb("topsum", [P, TJ])
        topinv = sb("topinv", [P, TJ])
        others = sb("others", [P, TJ, LOGIT_PAD])
        prob = sb("prob", [P, TJ, NE])
        probs = sb("probs", [P, TJ, NE])
        probt = sb("probt", [NE, T])

        qkt = big[:, :].rearrange("p (j h c) -> p j h c", j=TJ, h=2 * NH)
        hs = big[:, :].rearrange("p (l m t) -> p l m t", l=2, m=FM)
        qk1 = big[:, 0:4096].rearrange("p (l m t) -> p l m t", l=2, m=4)
        ptr = big[:, 4096:8192].rearrange("p (l m t) -> p l m t", l=2, m=TJ)
        q1 = qv[:, 0:2 * T].rearrange("p (a t) -> p a t", a=2)
        q2 = qv[:, 2 * T:4 * T].rearrange("p (a t) -> p a t", a=2)
        v1 = qv[:, :].rearrange("p (l j n) -> p l j n", l=2, j=TJ)
        gated = pt[:, 0]
        hid = pt[:, 1]
        p1 = pt[:, 0:2].rearrange("p a h t -> p (a h) t")

        def by_tokens(bank):
            return ps[:, bank].rearrange("p (k t) -> p k t", k=KH)

        w_loaded = [sem("w_loaded_even"), sem("w_loaded_odd")]
        bias_loaded = sem("bias_loaded")
        qkv0_split = sem("qkv0_split")
        split = sem("split")
        split_end = sem("split_end")
        abs_summed = sem("abs_summed")
        scale_step = sem("scale_step")
        below_done = sem("below_done")
        ternary = sem("ternary")
        const_zero = sem("const_zero")
        consts = sem("consts")
        x_loaded = sem("x_loaded")
        stats_done = [sem("stats0_done"), sem("stats_done")]
        aggr_done = [sem("aggr0_done"), sem("aggr_done")]
        vareps_done = [sem("vareps0_done"), sem("vareps_done")]
        rstd_done = [sem("rstd0_done"), sem("rstd_done")]
        xn_ready = [sem("xn0_ready"), sem("xn_ready")]
        xt0_psum = sem("xt0_psum")
        xt0_hi = sem("xt0_hi")
        xt0_lo = sem("xt0_lo")
        xt_psum = sem("xt_psum")
        xt_hi = sem("xt_hi")
        xt_lo = sem("xt_lo")
        pads_ready = sem("pads_ready")
        qk_psum = sem("qk_psum")
        qk_hi = sem("qk_hi")
        qk_lo = sem("qk_lo")
        v_psum = sem("v_psum")
        v_ready = sem("v_ready")
        turned = sem("turned")
        turn_read = sem("turn_read")
        scored = sem("scored")
        max_done = sem("max_done")
        m_part = sem("m_part")
        m_ready = sem("m_ready")
        scored_t = sem("scored_t")
        exp_done = sem("exp_done")
        pv_done = sem("pv_done")
        out_copied = sem("out_copied")
        zinv_done = sem("zinv_done")
        attn_psum = sem("attn_psum")
        x1_ready = sem("x1_ready")
        up_psum = sem("up_psum")
        silu_done = sem("silu_done")
        hid_done = sem("hid_done")
        h_hi = sem("h_hi")
        h_lo = sem("h_lo")
        down_psum = sem("down_psum")
        x2_ready = sem("x2_ready")
        qk1_psum = sem("qk1_psum")
        qk1_hi = sem("qk1_hi")
        qk1_lo = sem("qk1_lo")
        v1_psum = sem("v1_psum")
        v1_hi = sem("v1_hi")
        v1_lo = sem("v1_lo")
        ctx_psum = sem("ctx_psum")
        ctx_hi = sem("ctx_hi")
        ctx_lo = sem("ctx_lo")
        s1_psum = sem("s1_psum")
        nm1_part = sem("nm1_part")
        nm1_ready = sem("nm1_ready")
        exp1_done = sem("exp1_done")
        ri1_done = sem("ri1_done")
        p1_ready = sem("p1_ready")
        pt1_psum = sem("pt1_psum")
        pt1_hi = sem("pt1_hi")
        pt1_lo = sem("pt1_lo")
        out1_psum = sem("out1_psum")
        bias_added = sem("bias_added")
        x3_ready = sem("x3_ready")
        x3_stored = sem("x3_stored")
        first_loaded = sem("first_loaded")
        logits_psum = sem("logits_psum")
        elog_done = sem("elog_done")
        route = sem("route")
        probs_ready = sem("probs_ready")
        probt_psum = sem("probt_psum")
        probt_ready = sem("probt_ready")

        N_CONSTS = 12
        N_ROUTE = 8 + 2 * TJ

        block = ctx.enter_context(nc.Block())

        loads = [wqkv0, wo0, wqkv1, wo1, gate_w, w_up, w_gate, w_down]
        UP, DOWN = 5, 7

        def staged(n):
            rows, cols = loads[n].shape
            c = rows // P
            return stage[:, n % 2, 0:c * cols].rearrange("p (c n) -> p c n", c=c)

        def loaded(eng, n):
            eng.wait_ge(w_loaded[n % 2], 16 * (n // 2 + 1))

        @block.sync
        def _(sp):
            def load_weights(n):
                sp.dma_start(staged(n), loads[n].rearrange("(c p) n -> p c n", p=P)).then_inc(
                    w_loaded[n % 2], 16)

            sp.dma_start(xin[:], x[0:T, :].rearrange("(j p) n -> p j n", p=P)).then_inc(x_loaded, 16)
            load_weights(0)
            load_weights(1)
            sp.dma_start(bqk[:], bqk1).then_inc(bias_loaded, 16)
            sp.dma_start(bv[:], bv1).then_inc(bias_loaded, 16)
            sp.dma_start(bo[:], bo1.to_broadcast([P, D])).then_inc(bias_loaded, 16)
            sp.dma_start(gb[:], gate_b.to_broadcast([P, NE])).then_inc(bias_loaded, 16)
            sp.wait_ge(qkv0_split, 2)
            load_weights(2)
            for n in range(3, len(loads)):
                sp.wait_ge(split_end, n - 2)
                load_weights(n)

            def batch(b, more):
                x3_rows = x3_d[bass.ts(b, T), :].rearrange("(j p) n -> p j n", p=P)
                if more:
                    x_rows = x[bass.ts(b + 1, T), :].rearrange("(j p) n -> p j n", p=P)
                    sp.wait_ge(x1_ready, b * TJ + TJ)
                    sp.dma_start(xin[:], x_rows).then_inc(x_loaded, 16)
                sp.wait_ge(x3_ready, b * TJ + TJ)
                sp.dma_start(x3_rows, xres[:]).then_inc(x3_stored, 16)

            with sp.Fori(0, B - 1) as b:
                batch(b, True)
            batch(B - 1, False)
            sp.wait_ge(ctx_psum, 2 * B)
            load_expert_step(sp, wstage, 0, 0, w1, w3, w2, first_loaded)
            load_expert_step(sp, wstage, 1, 1, w1, w3, w2, first_loaded)
            sp.wait_ge(first_loaded, 96)
            sp.wait_ge(x3_stored, 16 * B)

        @block.gpsimd
        def _(pool):
            def rstd_of(count, k):
                for g in range(2):
                    tiles = slice(2 * g, 2 * g + 2)
                    pool.wait_ge(aggr_done[k], TJ * count - 2 + 2 * g)
                    pool.tensor_tensor(vareps[:, k, tiles], mv[:, k, tiles, 1], epsc[:, tiles], ALU.add)\
                        .then_inc(vareps_done[k], 1)
                    pool.wait_ge(vareps_done[k], 2 * count - 1 + g)
                    pool.tensor_tensor(rstd[:, k, tiles], vareps[:, k, tiles], halfc[:, tiles], ALU.pow)\
                        .then_inc(rstd_done[k], 1)

            pool.memset(ident[:], 0.0).then_inc(const_zero, 1)
            pool.memset(identb[:], 0.0).then_inc(const_zero, 1)
            pool.memset(mask_q[:], 0.0).then_inc(const_zero, 1)
            pool.memset(mask_k[:], 0.0).then_inc(const_zero, 1)
            pool.memset(epsc[:], EPS).then_inc(consts, 1)
            pool.memset(halfc[:], -0.5).then_inc(consts, 1)
            pool.wait_ge(const_zero, 4)
            for m in (ident, identb):
                pool.affine_select(out=m[:], in_=m[:], compare_op=ALU.not_equal, fill=1.0, base=0,
                                   pattern=[[-1, P]], channel_multiplier=1).then_inc(consts, 1)
            pool.affine_select(out=mask_q[:], in_=mask_q[:], compare_op=ALU.is_ge, fill=NEG, base=0,
                               pattern=[[-1, P]], channel_multiplier=1).then_inc(consts, 1)
            pool.affine_select(out=mask_k[:], in_=mask_k[:], compare_op=ALU.is_ge, fill=NEG, base=0,
                               pattern=[[1, P]], channel_multiplier=-1).then_inc(consts, 1)
            pool.wait_ge(consts, 2)
            rstd_of(1, 0)
            pool.memset(vh[:, :, :, HD:HD + 1], 1.0).then_inc(consts, 1)
            pool.memset(vh[:, :, :, HD + 1:32], 0.0).then_inc(consts, 1)
            pool.wait_ge(consts, 8)
            pool.memset(ka[P // 2:P, :, :].bitcast(F32), 0.0).then_inc(consts, 1)
            pool.wait_ge(consts, 9)
            pool.memset(kb[0:P // 2, :, :].bitcast(F32), 0.0).then_inc(consts, 1)
            pool.wait_ge(consts, 10)
            pool.memset(score[:, :, NE:LOGIT_PAD], NEG).then_inc(consts, 1)
            pool.memset(top4[:, :, TOP_K:8], NEG).then_inc(consts, 1)

            def prepare_weights():
                parts = {1: wo0s, 2: wq1, 3: wo1s, 4: gws}
                for n, w in parts.items():
                    loaded(pool, n)
                    pool.tensor_copy(w[:, 0], staged(n)).then_inc(split, 1)
                    pool.wait_ge(split, n)
                    pool.tensor_tensor(w[:, 1], staged(n), w[:, 0].bitcast(F32), ALU.subtract).then_inc(split_end, 1)
                for k in range(3):
                    pool.wait_ge(abs_summed, k + 1)
                    pool.partition_all_reduce(abstot[:, k:k + 1], abssum[:, k:k + 1], P,
                                              bass.bass_isa.ReduceOp.add).then_inc(scale_step, 1)
                    pool.wait_ge(scale_step, 4 * k + 1)
                    pool.tensor_scalar(tscale[:, k:k + 1], abstot[:, k:k + 1], 1.0 / (FF * D), TEPS,
                                       ALU.mult, ALU.add).then_inc(scale_step, 1)
                    pool.wait_ge(scale_step, 4 * k + 2)
                    pool.tensor_scalar(thalf[:, k:k + 1], tscale[:, k:k + 1], 0.5, 0.0,
                                       ALU.mult, ALU.add).then_inc(scale_step, 1)
                    pool.tensor_scalar(tnhalf[:, k:k + 1], tscale[:, k:k + 1], -0.5, 0.0,
                                       ALU.mult, ALU.add).then_inc(scale_step, 1)
                    pool.wait_ge(scale_step, 4 * k + 4)
                    if k == 2:
                        pool.wait_ge(split_end, 5)
                    pool.tensor_scalar(below[:, k % 2], stage[:, (UP + k) % 2], tnhalf[:, k:k + 1], 1.0,
                                       ALU.is_lt, ALU.mult).then_inc(below_done, 1)
                pool.tensor_tensor(tsgd[:], tscale[:, 1:2], tscale[:, 2:3], ALU.mult).then_inc(ternary, 1)

            def pads():
                pool.memset(qkt[:, :, 0:NH, AUX:HS].bitcast(F32), 0.0).then_inc(pads_ready, 1)
                pool.memset(qkt[:, :, NH:2 * NH, AUX:AUX + 2].bitcast(F32), 1.0).then_inc(pads_ready, 1)
                pool.memset(qkt[:, :, NH:2 * NH, AUX + 2:HS].bitcast(F32), 0.0).then_inc(pads_ready, 1)

            def rest(b, more):
                rstd_of(b * 3 + 1, 1)
                for m in range(FM):
                    pool.wait_ge(hid_done, b * FM + m + 1)
                    pool.wait_ge(h_hi, b * FM + m + 1)
                    pool.tensor_tensor(hs[:, 1, m], hid[:, m % 2], hs[:, 0, m].bitcast(F32), ALU.subtract)\
                        .then_inc(h_lo, 1)
                    if m == LN0_AGGR and more:
                        rstd_of(b + 2, 0)
                rstd_of(b * 3 + 2, 1)
                pool.wait_ge(xn_ready[1], b * 12 + 2 * TJ)
                pool.tensor_tensor(xres[:], xres[:], bo[:].rearrange("p (a n) -> p a n", a=1).to_broadcast([P, TJ, D]),
                                   ALU.add).then_inc(bias_added, 1)
                if more:
                    pool.wait_ge(ctx_psum, b * 2 + 2)
                    pool.tensor_tensor(pfence[:], epsc[:, 0:1], epsc[:, 0:1], ALU.add)
                    pads()
                rstd_of(b * 3 + 3, 1)

            pads()
            prepare_weights()
            pool.wait_ge(bias_loaded, 64)
            with pool.Fori(0, B - 1) as b:
                rest(b, True)
            rest(B - 1, False)

        @block.vector
        def _(dve):
            def statistics(k, j, src):
                dve.bn_stats(stats[:, k, j], src[:, j]).then_inc(stats_done[k], 1)

            def aggregate(count, k, tiles):
                dve.wait_ge(stats_done[k], TJ * count - TJ + tiles[-1] + 1)
                dve.memset(fence[:], 0.0)
                for j in tiles:
                    dve.bn_aggr(mv[:, k, j], stats[:, k, j]).then_inc(aggr_done[k], 1)

            def normalised(count, k, src):
                for j in range(TJ):
                    if j % 2 == 0:
                        dve.wait_ge(rstd_done[k], 2 * count - 1 + j // 2)
                    dve.tensor_scalar(xn[:, j], src[:, j], mv[:, k, j, 0:1], rstd[:, k, j:j + 1],
                                      ALU.subtract, ALU.mult).then_inc(xn_ready[k], 1)

            def tile_statistics(b, n, j, ready):
                dve.wait_ge(ready, b * TJ + j + 1)
                statistics(1, j, xres)
                if j % 2:
                    aggregate(b * 3 + n, 1, (j - 1, j))

            def low_half(b, t, kh):
                dve.wait_ge(xt_hi, b * 2 * NXT + 2 * t + kh + 1)
                dve.tensor_tensor(xt[:, 1, kh], ps[:, XT_BANK[t] + kh], xt[:, 0, kh].bitcast(F32), ALU.subtract)\
                    .then_inc(xt_lo, 1)

            def low_tokens(b, t, g):
                at = slice(HALF * g, HALF * (g + 1))
                dve.wait_ge(xt_hi, b * 2 * NXT + 2 * t + g + 1)
                dve.tensor_tensor(xt[:, 1, :, at], by_tokens(XT_BANK[t] + g), xt[:, 0, :, at].bitcast(F32),
                                  ALU.subtract).then_inc(xt_lo, 1)

            def low_halves0(b):
                for g in range(2):
                    at = slice(HALF * g, HALF * (g + 1))
                    dve.wait_ge(xt0_hi, b * 2 + g + 1)
                    dve.tensor_tensor(xt0[:, 1, :, at], by_tokens(XT0_BANK + g),
                                      xt0[:, 0, :, at].bitcast(F32), ALU.subtract).then_inc(xt0_lo, 1)

            def low_heads(b, j):
                dve.wait_ge(qk_hi, b * 8 + 2 * j + 2)
                bank = ps[:, j].rearrange("p (h c) -> p h c", h=2 * NH)
                dve.tensor_tensor(qkt[:, j, 0:NH, Q_LO:Q_LO + HD], bank[:, 0:NH],
                                  qkt[:, j, 0:NH, 0:HD].bitcast(F32), ALU.subtract).then_inc(qk_lo, 1)
                dve.tensor_tensor(qkt[:, j, NH:2 * NH, K_LO:K_LO + HD], bank[:, NH:2 * NH],
                                  qkt[:, j, NH:2 * NH, 0:HD].bitcast(F32), ALU.subtract).then_inc(qk_lo, 1)

            def attention(b, first):
                for event in ORDER:
                    kind, p, u = event
                    if kind == "turn_k":
                        dve.wait_ge(turned, b * len(TURNS) + TURNS.index(event) + 1)
                        if p >= 4:
                            dve.wait_ge(scored_t, b * 32 + TJ * (p - 3))
                        dve.tensor_copy(kb[P // 2:P, p % 4], ps[P // 2:P, T_BANK]).then_inc(turn_read, 1)
                        if event == NORM3_AT and not first:
                            low_norm3(b - 1)
                    elif kind == "score":
                        n = TJ * p + u
                        s = unit_slot(event)
                        dve.wait_ge(scored, b * 32 + n + 1)
                        dve.tensor_reduce(negm[:, p % 2, u], ps[:, 2 * s:2 * s + 2, 0:P * (u + 1)], X, ALU.max,
                                          negate=True).then_inc(max_done, 1)
                        if u == TJ - 1:
                            dve.wait_ge(max_done, b * 32 + n + 1)
                            aux = qkt[:, :, 2 * p:2 * p + 2, AUX]
                            dve.tensor_copy(aux, negm[:, p % 2]).then_inc(m_part, 1)
                            dve.wait_ge(m_part, b * NP + p + 1)
                            dve.tensor_tensor(qkt[:, :, 2 * p:2 * p + 2, AUX + 1], negm[:, p % 2],
                                              aux.bitcast(F32), ALU.subtract).then_inc(m_ready, 1)
                        if first and (p, u) in TERNARY_AT:
                            k = TERNARY_AT.index((p, u))
                            w = (tup, tgate, tdown)[k]
                            dve.wait_ge(below_done, k + 1)
                            dve.scalar_tensor_tensor(w[:, :, :].rearrange("p c n -> p (c n)"), stage[:, (UP + k) % 2],
                                                     thalf[:, k:k + 1], below[:, k % 2], ALU.is_gt, ALU.subtract)\
                                .then_inc(split_end, 1)
                        if not first and p >= ROUTER_PAIR and TJ * (p - ROUTER_PAIR) + u < ROUTER_PARTS:
                            router(b - 1, TJ * (p - ROUTER_PAIR) + u)
                    elif kind == "turn_out":
                        g = p
                        dve.wait_ge(turned, b * len(TURNS) + TURNS.index(event) + 1)
                        rows = ps[:, T_BANK].rearrange("p (j h c) -> p j h c", j=TJ, h=4)
                        dve.reciprocal(zinv[:], rows[:, :, :, HD]).then_inc(zinv_done, 1)
                        dve.wait_ge(zinv_done, b * 4 + g + 1)
                        dve.tensor_tensor(xn[:, :, 4 * HD * g:4 * HD * (g + 1)].rearrange("p j (h c) -> p j h c", h=4),
                                          rows[:, :, :, 0:HD],
                                          zinv[:].rearrange("p j (h a) -> p j h a", a=1).to_broadcast([P, TJ, 4, HD]),
                                          ALU.mult).then_inc(turn_read, 1)
                    if event == Z_AT:
                        low_half(b, XT_Z, 0)
                low_half(b, XT_Z, 1)
                if not first:
                    dve.wait_ge(x3_stored, b * 16)
                for j in range(TJ):
                    dve.wait_ge(attn_psum, b * TJ + j + 1)
                    dve.tensor_tensor(xres[:, j], ps[:, WO_BANK[j], 0:D], xin[:, j], ALU.add).then_inc(x1_ready, 1)
                    if j:
                        tile_statistics(b, 1, j - 1, x1_ready)

            def feed_forward(b, more):
                for m in range(FM):
                    r = m % 2
                    dve.wait_ge(up_psum, b * 2 * FM + 2 * m + 2)
                    dve.wait_ge(silu_done, b * FM + m + 1)
                    if m >= 2:
                        dve.wait_ge(h_lo, b * FM + m - 1)
                    dve.tensor_tensor(hid[:, r], ps[:, 2 * r + 1], gated[:, r], ALU.mult).then_inc(hid_done, 1)
                    if more and m == LN0_AGGR - 1:
                        dve.wait_ge(x_loaded, b * 16 + 32)
                        for j in range(TJ):
                            statistics(0, j, xin)
                    elif more and m == LN0_AGGR:
                        aggregate(b + 2, 0, (0, 1, 2, 3))
                    elif more and m == LN0_AGGR + 2:
                        normalised(b + 2, 0, xin)
                if more:
                    low_halves0(b + 1)
                for j in range(TJ):
                    dve.wait_ge(down_psum, b * TJ + j + 1)
                    if j == 0:
                        dve.wait_ge(ternary, 1)
                    dve.scalar_tensor_tensor(xres[:, j], ps[:, 4 + j, 0:D], tsgd[:, 0:1], xres[:, j],
                                             ALU.mult, ALU.add).then_inc(x2_ready, 1)
                    if j:
                        tile_statistics(b, 2, j - 1, x2_ready)

            def second_attention(b):
                for m in range(4):
                    dve.wait_ge(qk1_hi, b * 4 + m + 1)
                    dve.scalar_tensor_tensor(qk1[:, 1, m], ps[:, m], bqk[:, m:m + 1], qk1[:, 0, m].bitcast(F32),
                                             ALU.add, ALU.subtract).then_inc(qk1_lo, 1)

                def low_values(j):
                    dve.wait_ge(v1_hi, b * TJ + j + 1)
                    dve.tensor_tensor(v1[:, 1, j], ps[:, 4 + j, 0:D], v1[:, 0, j].bitcast(F32), ALU.subtract)\
                        .then_inc(v1_lo, 1)

                low_values(0)
                low_values(1)

                def maximum(j):
                    dve.wait_ge(s1_psum, b * TJ + j + 1)
                    dve.tensor_reduce(nm1[:, j:j + 1], ps[:, j], X, ALU.max, negate=True).then_inc(nm1_part, 1)
                    dve.wait_ge(nm1_part, b * TJ + j + 1)
                    dve.tensor_scalar(nm1s[:, j:j + 1], nm1[:, j:j + 1], 1.0 / 16, None, ALU.mult)\
                        .then_inc(nm1_ready, 1)

                def normalise(j):
                    dve.wait_ge(exp1_done, b * TJ + j + 1)
                    dve.reciprocal(ri1[:, j:j + 1], rs1[:, j:j + 1]).then_inc(ri1_done, 1)
                    dve.wait_ge(ri1_done, b * TJ + j + 1)
                    dve.tensor_scalar(p1[:, j], p1[:, j], ri1[:, j:j + 1], None, ALU.mult).then_inc(p1_ready, 1)

                for j in range(TJ):
                    maximum(j)
                    if j:
                        normalise(j - 1)
                low_values(2)
                normalise(TJ - 1)
                low_values(3)
                for g in range(2):
                    for c in range(2):
                        dve.wait_ge(pt1_hi, b * 4 + 2 * g + c + 1)
                        at = (slice(None), slice(2 * c, 2 * c + 2), slice(HALF * g, HALF * (g + 1)))
                        dve.tensor_tensor(ptr[:, 1][at], by_tokens(4 + 2 * g + c), ptr[:, 0][at].bitcast(F32),
                                          ALU.subtract).then_inc(pt1_lo, 1)
                for g in range(2):
                    dve.wait_ge(ctx_hi, b * 4 + 2 * g + 2)
                    for kh in range(KH):
                        dve.scalar_tensor_tensor(xt[:, 1, kh, HALF * g:HALF * (g + 1)], by_tokens(g)[:, kh],
                                                 bv[:, kh:kh + 1], xt[:, 0, kh, HALF * g:HALF * (g + 1)].bitcast(F32),
                                                 ALU.add, ALU.subtract).then_inc(ctx_lo, 1)
                for j in range(TJ):
                    dve.wait_ge(out1_psum, b * TJ + j + 1)
                    if j == 0:
                        dve.wait_ge(bias_added, b + 1)
                    dve.tensor_tensor(xres[:, j], ps[:, 4 + j, 0:D], xres[:, j], ALU.add).then_inc(x3_ready, 1)
                    if j:
                        tile_statistics(b, 3, j - 1, x3_ready)

            def low_norm3(b):
                for g in range(2):
                    low_tokens(b, XT_LN3, g)

            def router(b, part):
                at = b * N_ROUTE
                s = score[:, :, 0:NE]
                if part == 0:
                    dve.wait_ge(elog_done, b + 1)
                    dve.tensor_scalar(prob[:], elog[:], 1.0, None, ALU.add).then_inc(route, 1)
                    dve.wait_ge(route, at + 1)
                    dve.reciprocal(elog[:], prob[:]).then_inc(route, 1)
                elif part == 1:
                    dve.wait_ge(route, at + 2)
                    dve.tensor_tensor(s, elog[:], gb[:].rearrange("p (a e) -> p a e", a=1).to_broadcast(
                        [P, TJ, NE]), ALU.add).then_inc(route, 1)
                elif part == 2:
                    dve.wait_ge(route, at + 3)
                    dve.memset(fence[:], 0.0)
                    for j in range(TJ):
                        dve.max(top8[:, j], score[:, j]).then_inc(route, 1)
                elif part == 3:
                    dve.wait_ge(route, at + 3 + TJ)
                    dve.tensor_reduce(topsum[:], top8[:, :, 0:TOP_K], X, ALU.add).then_inc(route, 1)
                    dve.tensor_copy(top4[:, :, 0:TOP_K], top8[:, :, 0:TOP_K]).then_inc(route, 1)
                elif part == 4:
                    dve.wait_ge(route, at + 5 + TJ)
                    dve.reciprocal(topinv[:], topsum[:]).then_inc(route, 1)
                    for j in range(TJ):
                        dve.match_replace(others[:, j], top4[:, j], score[:, j], -3.0e38).then_inc(route, 1)
                elif part == 5:
                    dve.wait_ge(route, at + 6 + 2 * TJ)
                    dve.tensor_tensor(prob[:], others[:, :, 0:NE], s, ALU.not_equal).then_inc(route, 1)
                    dve.wait_ge(route, at + 7 + 2 * TJ)
                    dve.tensor_tensor(prob[:], prob[:], s, ALU.mult).then_inc(route, 1)
                else:
                    dve.wait_ge(route, at + 8 + 2 * TJ)
                    dve.tensor_tensor(probs[:], prob[:], topinv[:].rearrange(
                        "p (j a) -> p j a", a=1).to_broadcast([P, TJ, NE]), ALU.mult).then_inc(probs_ready, 1)

            def rest(b, more):
                tile_statistics(b, 1, TJ - 1, x1_ready)
                normalised(b * 3 + 1, 1, xres)
                for g in range(2):
                    low_tokens(b, XT_LN1, g)
                feed_forward(b, more)
                tile_statistics(b, 2, TJ - 1, x2_ready)
                normalised(b * 3 + 2, 1, xres)
                for g in range(2):
                    low_tokens(b, XT_LN2, g)
                second_attention(b)
                tile_statistics(b, 3, TJ - 1, x3_ready)
                if more:
                    low_heads(b + 1, 0)
                normalised(b * 3 + 3, 1, xres)
                if more:
                    for j in range(1, TJ):
                        low_heads(b + 1, j)
                else:
                    low_norm3(b)

            dve.wait_ge(x_loaded, 16)
            for j in range(TJ):
                statistics(0, j, xin)
                if j % 2:
                    aggregate(1, 0, (j - 1, j))
            normalised(1, 0, xin)
            dve.wait_ge(qkv0_split, 1)
            dve.tensor_tensor(wq0[:, 1], staged(0), wq0[:, 0].bitcast(F32), ALU.subtract).then_inc(qkv0_split, 1)
            low_halves0(0)
            for j in range(TJ):
                low_heads(0, j)
            attention(0, True)
            dve.wait_ge(bias_loaded, 64)
            with dve.Fori(0, B - 1) as b:
                rest(b, True)
                attention(b + 1, False)
            rest(B - 1, False)
            for part in range(ROUTER_PARTS):
                router(B - 1, part)

        @block.scalar
        def _(act):
            def high_half(b, t, kh):
                act.wait_ge(xt_psum, b * 2 * NXT + 2 * t + kh + 1)
                act.activation(xt[:, 0, kh], ps[:, XT_BANK[t] + kh], ACT.Copy).then_inc(xt_hi, 1)

            def high_tokens(b, t, g):
                at = slice(HALF * g, HALF * (g + 1))
                act.wait_ge(xt_psum, b * 2 * NXT + 2 * t + g + 1)
                act.activation(xt[:, 0, :, at], by_tokens(XT_BANK[t] + g), ACT.Copy).then_inc(xt_hi, 1)

            def high_halves0(b):
                for g in range(2):
                    at = slice(HALF * g, HALF * (g + 1))
                    act.wait_ge(xt0_psum, b * 2 + g + 1)
                    act.activation(xt0[:, 0, :, at], by_tokens(XT0_BANK + g), ACT.Copy).then_inc(xt0_hi, 1)

            def high_heads(b):
                for j in range(TJ):
                    act.wait_ge(qk_psum, b * TJ + j + 1)
                    bank = ps[:, j].rearrange("p (h a c) -> p h a c", h=2 * NH, a=1)
                    act.activation(qkt[:, j, 0:NH, 0:AUX].rearrange("p h (a c) -> p h a c", c=HD)[:, :, 0:3:2],
                                   bank[:, 0:NH].to_broadcast([P, NH, 2, HD]), ACT.Copy).then_inc(qk_hi, 1)
                    act.activation(qkt[:, j, NH:2 * NH, 0:AUX].rearrange("p h (a c) -> p h a c", c=HD)[:, :, 0:2],
                                   bank[:, NH:2 * NH].to_broadcast([P, NH, 2, HD]), ACT.Copy).then_inc(qk_hi, 1)

            def copy_values0(b):
                for g in range(2):
                    act.wait_ge(v_psum, b * 2 + g + 1)
                    act.activation(vh[:, 2 * g:2 * g + 2, :, 0:HD],
                                   ps[:, V_BANK + g].rearrange("p (j h c) -> p j h c", j=2, h=NH),
                                   ACT.Copy).then_inc(v_ready, 1)

            def keep_routing(b):
                rows = routing_d[:, bass.ts(b, T)].rearrange("(e g) n -> e g n", e=NE)
                act.wait_ge(probt_psum, b + 1)
                act.activation(probt[:], ps[0:NE, T_BANK], ACT.Copy).then_inc(probt_ready, 1)
                act.wait_ge(probt_ready, b + 1)
                act.dma_start(rows, probt[:].rearrange("e (g n) -> e g n", g=1).to_broadcast([NE, EH // GROUP, T]))\
                    .then_inc(kept, 16)

            def attention(b, first):
                if not first:
                    high_norm3(b - 1)
                for event in ORDER:
                    kind, p, u = event
                    if kind in ("turn_k", "turn_q", "turn_shifted_q"):
                        if kind == "turn_k":
                            to = ka[0:P // 2, p % 4]
                            if p >= 4:
                                act.wait_ge(scored_t, b * 32 + TJ * (p - 3))
                        elif kind == "turn_q":
                            to = q1[:, p % 2]
                            if p >= 2:
                                act.wait_ge(scored, b * 32 + TJ * (p - 1))
                        else:
                            to = q2[:, p % 2]
                            if p >= 2:
                                act.wait_ge(scored_t, b * 32 + TJ * (p - 1))
                        act.wait_ge(turned, b * len(TURNS) + TURNS.index(event) + 1)
                        rows = P // 2 if kind == "turn_k" else P
                        act.activation(to, ps[0:rows, T_BANK], ACT.Copy).then_inc(turn_read, 1)
                    elif kind == "scoreT":
                        n = TJ * p + u
                        s = unit_slot(event)
                        w = T - P * u
                        act.wait_ge(scored_t, b * 32 + n + 1)
                        if n >= 3:
                            act.wait_ge(pv_done, b * 32 + n - 2)
                        act.activation(pt[:, n % 3, :, 0:w], ps[:, 2 * s:2 * s + 2, 0:w], ACT.Exp,
                                       scale=0.25).then_inc(exp_done, 1)
                    elif kind == "copy_out":
                        act.wait_ge(pv_done, b * 32 + 8 * (p + 1))
                        if p >= 2:
                            act.wait_ge(turned, b * len(TURNS) + TURNS.index(("turn_out", p - 2, 0)) + 1)
                        act.activation(ot[:, p % 2], ps[:, PO_BANK], ACT.Copy).then_inc(out_copied, 1)
                    if first and event in ABS_AT:
                        k = ABS_AT.index(event)
                        loaded(act, UP + k)
                        act.activation(absout[:], stage[:, (UP + k) % 2, :], ACT.Abs,
                                       accum_out=abssum[:, k:k + 1]).then_inc(abs_summed, 1)
                    if event == LOGITS_AT and not first:
                        keep_norm3(b - 1)
                    if event == Z_AT:
                        if not first:
                            act.wait_ge(kept, b * 32 - 16)
                        high_half(b, XT_Z, 0)
                high_half(b, XT_Z, 1)
                if not first:
                    keep_routing(b - 1)

            def feed_forward(b):
                def high(m):
                    act.wait_ge(hid_done, b * FM + m + 1)
                    act.activation(hs[:, 0, m], hid[:, m % 2], ACT.Copy).then_inc(h_hi, 1)

                for m in range(FM):
                    r = m % 2
                    act.wait_ge(up_psum, b * 2 * FM + 2 * m + 1)
                    if m >= 2:
                        act.wait_ge(hid_done, b * FM + m - 1)
                    act.activation(gated[:, r], ps[:, 2 * r], ACT.Silu, scale=tscale[:, 0:1]).then_inc(silu_done, 1)
                    if m:
                        high(m - 1)
                high(FM - 1)

            def second_attention(b):
                for m in range(4):
                    act.wait_ge(qk1_psum, b * 4 + m + 1)
                    act.activation(qk1[:, 0, m], ps[:, m], ACT.Identity, bias=bqk[:, m:m + 1]).then_inc(qk1_hi, 1)

                def high_values(j):
                    act.wait_ge(v1_psum, b * TJ + j + 1)
                    act.activation(v1[:, 0, j], ps[:, 4 + j, 0:D], ACT.Copy).then_inc(v1_hi, 1)

                high_values(0)
                high_values(1)
                for j in range(TJ):
                    if j >= 2:
                        high_values(j)
                    act.wait_ge(nm1_ready, b * TJ + j + 1)
                    act.activation(p1[:, j], ps[:, j], ACT.Exp, bias=nm1s[:, j:j + 1], scale=1.0 / 16,
                                   accum_out=rs1[:, j:j + 1]).then_inc(exp1_done, 1)
                for g in range(2):
                    act.wait_ge(pt1_psum, b * TJ + 2 * g + 2)
                    for c in range(2):
                        act.activation(ptr[:, 0, 2 * c:2 * c + 2, HALF * g:HALF * (g + 1)], by_tokens(4 + 2 * g + c),
                                       ACT.Copy).then_inc(pt1_hi, 1)
                for g in range(2):
                    act.wait_ge(ctx_psum, b * 2 + g + 1)
                    for kh in range(KH):
                        act.activation(xt[:, 0, kh, HALF * g:HALF * (g + 1)], by_tokens(g)[:, kh], ACT.Identity,
                                       bias=bv[:, kh:kh + 1]).then_inc(ctx_hi, 1)

            def rest(b, more):
                for g in range(2):
                    high_tokens(b, XT_LN1, g)
                feed_forward(b)
                if more:
                    high_halves0(b + 1)
                    copy_values0(b + 1)
                for g in range(2):
                    high_tokens(b, XT_LN2, g)
                second_attention(b)
                if more:
                    high_heads(b + 1)
                else:
                    high_norm3(b)
                    keep_norm3(b)

            def high_norm3(b):
                for g in range(2):
                    high_tokens(b, XT_LN3, g)

            def keep_norm3(b):
                act.wait_ge(xt_lo, b * 2 * NXT + 2 * NXT)
                act.dma_start(xt4[:, bass.ts(b, 2 * KH)].bitcast(F32), xt[:].rearrange("p l k t -> p (l k) t").bitcast(F32))\
                    .then_inc(kept, 16)
                act.wait_ge(logits_psum, b + 1)
                act.activation(elog[:], ps[:, LOGIT_BANK, 0:TJ * NE].rearrange("p (j e) -> p j e", j=TJ), ACT.Exp,
                               scale=-1.0).then_inc(elog_done, 1)

            loaded(act, 0)
            act.activation(wq0[:, 0], staged(0), ACT.Copy).then_inc(qkv0_split, 1)
            high_halves0(0)
            copy_values0(0)
            high_heads(0)
            attention(0, True)
            act.wait_ge(bias_loaded, 64)
            with act.Fori(0, B - 1) as b:
                rest(b, True)
                attention(b + 1, False)
            rest(B - 1, False)
            act.wait_ge(kept, 32 * B - 16)
            keep_routing(B - 1)

        @block.tensor
        def _(pe):
            def turn_half(bank, kh, src):
                for j in range(TJ):
                    mm = pe.transpose(ps[:, bank + kh, P * j:P * (j + 1)], src[:, j, P * kh:P * (kh + 1)], ident[:])
                mm.then_inc(xt_psum, 1)

            def turn_norm(bank, done, ready, count):
                for j in range(TJ):
                    pe.wait_ge(ready, count + j + 1)
                    for kh in range(KH):
                        mm = pe.transpose(by_tokens(bank + j // 2)[:, kh, P * (j % 2):P * (j % 2 + 1)],
                                          xn[:, j, P * kh:P * (kh + 1)], ident[:])
                    if j % 2:
                        mm.then_inc(done, 1)

            def halves_ready(b, t):
                for kh in range(KH):
                    pe.wait_ge(xt_lo, b * 2 * NXT + 2 * t + kh + 1)

            def product(out, left, right, start=True, stop=True):
                terms = [(l, r, kh) for kh in range(KH) for l, r in ((0, 0), (1, 0), (0, 1))]
                for n, (l, r, kh) in enumerate(terms):
                    mm = pe.matmul(out, left(l, kh), right(r, kh), start=start and n == 0,
                                   stop=stop and n == len(terms) - 1)
                return mm

            def x_tile(j):
                return lambda part, kh: xt[:, part, kh, P * j:P * (j + 1)]

            def turn_norm0(b):
                turn_norm(XT0_BANK, xt0_psum, xn_ready[0], b * TJ)

            def tokens0(j):
                return lambda part, kh: xt0[:, part, kh, P * j:P * (j + 1)]

            def values0(b):
                for g in range(2):
                    pe.wait_ge(xt0_lo, b * 2 + g + 1)
                    for j in (2 * g, 2 * g + 1):
                        mm = product(by_tokens(V_BANK + g)[:, j % 2], tokens0(j),
                                     lambda part, kh: wq0[:, part, kh, 2 * D:3 * D])
                    mm.then_inc(v_psum, 1)

            def project(b):
                for j in range(TJ):
                    product(ps[:, j], tokens0(j), lambda part, kh: wq0[:, part, kh, 0:2 * D]).then_inc(qk_psum, 1)

            def turn_probs(b):
                pe.wait_ge(probs_ready, b + 1)
                for j in range(TJ):
                    mm = pe.transpose(ps[0:NE, T_BANK, P * j:P * (j + 1)], probs[:, j], ident[:])
                mm.then_inc(probt_psum, 1)

            def turn_norm3(b):
                turn_norm(XT_BANK[XT_LN3], xt_psum, xn_ready[1], b * 12 + 2 * TJ)

            def attention(b, first):
                if not first:
                    turn_norm3(b - 1)
                pe.wait_ge(qk_lo, b * 8 + 8)
                pe.wait_ge(pads_ready, b * 3 + 3)
                for event in ORDER:
                    kind, p, u = event
                    if kind.startswith("turn"):
                        n = TURNS.index(event)
                        if n:
                            pe.wait_ge(turn_read, b * N_TURN_READS + turn_reads(TURNS[n - 1]))
                        if kind == "turn_shifted_q":
                            pe.wait_ge(m_ready, b * NP + p + 1)
                        if kind == "turn_out":
                            pe.wait_ge(out_copied, b * 4 + p + 1)
                        for j in range(TJ):
                            if kind == "turn_out":
                                src = ot[:, p % 2, P * j:P * (j + 1)]
                            else:
                                h = 2 * p + (NH if kind == "turn_k" else 0)
                                src = qkt[:, j, h:h + 2].rearrange("p h c -> p (h c)").bitcast(F32)
                            mm = pe.transpose(ps[:, T_BANK, P * j:P * (j + 1)], src, ident[:])
                        mm.then_inc(turned, 1)
                    elif kind in ("score", "scoreT"):
                        n = UNITS.index(event)
                        s = unit_slot(event)
                        if n >= 3:
                            before, bp, bu = UNITS[n - 3]
                            pe.wait_ge(max_done if before == "score" else exp_done, b * 32 + TJ * bp + bu + 1)
                        if event == UNITS[0]:
                            pe.wait_ge(v_ready, b * 2 + 2)
                        if u == 0:
                            q = ("turn_q" if kind == "score" else "turn_shifted_q", p, 0)
                            pe.wait_ge(turn_read, b * N_TURN_READS + turn_reads(q))
                        for h, keys in enumerate((ka, kb)):
                            if kind == "score":
                                w, d = P * (u + 1), P * u
                                pe.matmul(ps[:, 2 * s + h, 0:w], q1[:, p % 2, P * u:P * (u + 1)],
                                          keys[:, p % 4, 0:w], start=True, stop=False)
                                mm = pe.matmul(ps[:, 2 * s + h, d:d + P], identb[:], mask_q[:],
                                               start=False, stop=True)
                            else:
                                w = T - P * u
                                pe.matmul(ps[:, 2 * s + h, 0:w], keys[:, p % 4, P * u:P * (u + 1)],
                                          q2[:, p % 2, P * u:T], start=True, stop=False)
                                mm = pe.matmul(ps[:, 2 * s + h, 0:P], identb[:], mask_k[:],
                                               start=False, stop=True)
                        mm.then_inc(scored if kind == "score" else scored_t, 1)
                    elif kind == "value":
                        n = TJ * p + u
                        w = T - P * u
                        pe.wait_ge(exp_done, b * 32 + n + 1)
                        if n == 0 and not first:
                            pe.wait_ge(elog_done, b)
                        if p % 2 == 0 and u == 0 and p:
                            pe.wait_ge(out_copied, b * 4 + p // 2)
                        for h in range(2):
                            at = 32 * (2 * (p % 2) + h)
                            mm = pe.matmul(ps[at:at + 32, PO_BANK, P * u:T], vh[:, u, 2 * p + h],
                                           pt[:, n % 3, h, 0:w], start=u == 0, stop=u == TJ - 1)
                        mm.then_inc(pv_done, 1)
                    if not first and event == LOGITS_AT:
                        logits(b - 1)
                    if event == Z_AT:
                        pe.wait_ge(turn_read, b * N_TURN_READS + turn_reads(("turn_out", 1, 0)))
                        turn_half(XT_BANK[XT_Z], 0, xn)
                pe.wait_ge(turn_read, b * N_TURN_READS + N_TURN_READS)
                turn_half(XT_BANK[XT_Z], 1, xn)
                if not first:
                    turn_probs(b - 1)
                pe.wait_ge(split_end, 1)
                for kh in range(KH):
                    pe.wait_ge(xt_lo, b * 2 * NXT + 2 * XT_Z + kh + 1)
                    for j in range(TJ):
                        for l, r in ((0, 0), (1, 0), (0, 1)):
                            mm = pe.matmul(ps[:, WO_BANK[j], 0:D], x_tile(j)(l, kh), wo0s[:, r, kh],
                                           start=kh == 0 and l == 0 and r == 0, stop=kh == 1 and r == 1)
                        if kh == 1:
                            mm.then_inc(attn_psum, 1)
                if not first:
                    pe.wait_ge(probt_ready, b)

            def feed_forward(b, more):
                halves_ready(b, XT_LN1)
                pe.wait_ge(split_end, 7)

                def down(m):
                    pe.wait_ge(h_lo, b * FM + m + 1)
                    for j in range(TJ):
                        for part in range(2):
                            mm = pe.matmul(ps[:, 4 + j, 0:D], hs[:, part, m, P * j:P * (j + 1)], tdown[:, m],
                                           start=m == 0 and part == 0, stop=m == FM - 1 and part == 1)
                        if m == FM - 1:
                            mm.then_inc(down_psum, 1)

                for m in range(FM + 2):
                    if m == FM and more:
                        pe.wait_ge(hid_done, b * FM + FM - 1)
                        turn_norm0(b + 1)
                    if m < FM:
                        r = m % 2
                        if m >= 2:
                            pe.wait_ge(hid_done, b * FM + m - 1)
                        for w, bank in ((tup, 2 * r), (tgate, 2 * r + 1)):
                            for kh in range(KH):
                                for part in range(2):
                                    mm = pe.matmul(ps[:, bank], w[:, kh, P * m:P * (m + 1)], xt[:, part, kh],
                                                   start=kh == 0 and part == 0, stop=kh == 1 and part == 1)
                            mm.then_inc(up_psum, 1)
                    if m >= 2:
                        down(m - 2)

            def second_attention(b, more):
                halves_ready(b, XT_LN2)
                pe.wait_ge(split_end, 2)
                for m in range(4):
                    if more and m == V_BANK:
                        pe.wait_ge(v_ready, b * 2 + 4)
                    product(ps[:, m], lambda part, kh: wq1[:, part, kh, P * m:P * (m + 1)],
                            lambda part, kh: xt[:, part, kh]).then_inc(qk1_psum, 1)

                def values(j):
                    product(ps[:, 4 + j, 0:D], x_tile(j), lambda part, kh: wq1[:, part, kh, 2 * D:3 * D])\
                        .then_inc(v1_psum, 1)

                values(0)
                values(1)
                pe.wait_ge(qk1_lo, b * 4 + 4)
                for j in range(TJ):
                    product(ps[:, j], lambda part, kh: qk1[:, part, kh, P * j:P * (j + 1)],
                            lambda part, kh: qk1[:, part, 2 + kh]).then_inc(s1_psum, 1)
                values(2)
                values(3)
                for j in range(TJ):
                    if j % 2 == 0:
                        pe.wait_ge(v1_lo, b * TJ + j + 2)
                    pe.wait_ge(p1_ready, b * TJ + j + 1)
                    for i in range(TJ):
                        mm = pe.transpose(by_tokens(4 + 2 * (j // 2) + i // 2)[:, i % 2, P * (j % 2):P * (j % 2 + 1)],
                                          p1[:, j, P * i:P * (i + 1)], ident[:])
                    mm.then_inc(pt1_psum, 1)
                for g in range(2):
                    pe.wait_ge(pt1_lo, b * TJ + 2 * g + 2)
                    for hh in range(KH):
                        at = slice(HALF * g, HALF * (g + 1))
                        for i in range(TJ):
                            for l, r in ((0, 0), (1, 0), (0, 1)):
                                mm = pe.matmul(by_tokens(g)[:, hh], v1[:, l, i, P * hh:P * (hh + 1)], ptr[:, r, i, at],
                                               start=i == 0 and l == 0 and r == 0, stop=i == TJ - 1 and r == 1)
                        if hh == KH - 1:
                            mm.then_inc(ctx_psum, 1)
                pe.wait_ge(split_end, 3)
                for j in range(TJ):
                    if j % 2 == 0:
                        pe.wait_ge(ctx_lo, b * 4 + j + 2)
                    product(ps[:, 4 + j, 0:D], x_tile(j), lambda part, kh: wo1s[:, part, kh]).then_inc(out1_psum, 1)

            def logits(b):
                halves_ready(b, XT_LN3)
                pe.wait_ge(split_end, 4)
                for j in range(TJ):
                    mm = product(ps[:, LOGIT_BANK, NE * j:NE * (j + 1)], x_tile(j), lambda part, kh: gws[:, part, kh])
                mm.then_inc(logits_psum, 1)

            def rest(b, more):
                turn_norm(XT_BANK[XT_LN1], xt_psum, xn_ready[1], b * 12 + 0)
                feed_forward(b, more)
                if more:
                    values0(b + 1)
                turn_norm(XT_BANK[XT_LN2], xt_psum, xn_ready[1], b * 12 + 4)
                second_attention(b, more)
                if more:
                    project(b + 1)
                else:
                    turn_norm3(b)
                    logits(b)

            pe.wait_ge(consts, 4)
            turn_norm0(0)
            pe.wait_ge(qkv0_split, 2)
            values0(0)
            pe.wait_ge(v_ready, 2)
            project(0)
            pe.wait_ge(consts, N_CONSTS)
            attention(0, True)
            with pe.Fori(0, B - 1) as b:
                rest(b, True)
                attention(b + 1, False)
            rest(B - 1, False)
            turn_probs(B - 1)


def experts(nc, w1, w3, w2, x3_d, routing_d, xt4, wstage, kept, out):
    with ExitStack() as ctx:
        def sb(name, shape, dt=F32):
            return ctx.enter_context(nc.sbuf_tensor(name, shape, dt))

        def sem(name):
            return ctx.enter_context(nc.semaphore(name))

        ps = ctx.enter_context(nc.psum_tensor("eps", [P, 8, 512], F32))
        routing = sb("routing", [P, 2, 2, NTOK])
        x3 = sb("x3", [P, NTOK // P, D])
        acc = sb("acc", [P, KH, NTOK])
        ident = sb("eident", [P, P])
        w13s = sb("w13s", [P, 2, 2, 2, KH, PAIR], F32R)
        w2s = sb("w2s", [P, 2, 2, 2, D], F32R)
        h1 = sb("h1", [P, 2, T])
        gate = sb("gate", [P, 2, T])
        act_h = sb("act_h", [P, 2, T])
        y = sb("y", [P, 2, T])
        ys = sb("ys", [P, 4, 2, T], F32R)

        zeroed = sem("e_zeroed")
        ident_ready = sem("e_ident_ready")
        routing_loaded = [sem("routing_loaded_even"), sem("routing_loaded_odd")]
        x3_loaded = sem("x3_loaded")
        w_loaded = [sem("e_w_loaded_even"), sem("e_w_loaded_odd")]
        w_hi = sem("e_w_hi")
        w_lo = sem("e_w_lo")
        up_psum = sem("e_up_psum")
        h1_copied = sem("h1_copied")
        gate_done = sem("gate_done")
        silu_done = sem("e_silu_done")
        y_ready = sem("y_ready")
        y_hi = sem("y_hi")
        y_lo = sem("y_lo")
        y_used = sem("y_used")
        half_psum = sem("half_psum")
        acc_zeroed = sem("acc_zeroed")
        acc_done = sem("acc_done")
        acc_turned = sem("acc_turned")
        summed = sem("summed")
        stored = sem("stored")

        block = ctx.enter_context(nc.Block())
        SUM_BANKS = ((6, 7), (2, 5))
        NU = 2 * B
        LOOPS = (NPAIRS - 2) // 2

        def steps(eng, step):
            step(0, 0)
            with eng.Fori(0, LOOPS) as k:
                step(2 * k + 1, 1)
                step(2 * k + 2, 0)
            step(NPAIRS - 1, 1)

        @block.sync
        def _(sp):
            def load_routing(u, slot):
                for s in range(2):
                    at = (2 * u + s - 2) * (P // GROUP)
                    rows = routing_d[bass.ds(at, P // GROUP), :].rearrange("(g a) n -> g a n", a=1)
                    sp.dma_start(routing[:, slot, s], rows.to_broadcast([P // GROUP, GROUP, NTOK]))\
                        .then_inc(routing_loaded[slot], 16)

            def load(u, slot):
                sp.wait_ge(y_ready, NU * (u - 1))
                load_expert_step(sp, wstage, u, slot, w1, w3, w2, w_loaded[slot])
                load_routing(u, slot)

            sp.wait_ge(kept, 32 * B)
            load_routing(1, 1)
            sp.dma_start(x3[:], x3_d.rearrange("(j p) n -> p j n", p=P)).then_inc(x3_loaded, 16)
            with sp.Fori(1, LOOPS + 1) as k:
                load(2 * k, 0)
                load(2 * k + 1, 1)
            for c in range(B):
                sp.wait_ge(summed, c + 1)
                sp.dma_start(out[bass.ts(c, T), :].rearrange("(j p) n -> p j n", p=P),
                             x3[:, TJ * c:TJ * (c + 1)]).then_inc(stored, 16)
            sp.wait_ge(stored, 16 * B)

        @block.gpsimd
        def _(pool):
            pool.memset(ident[:], 0.0).then_inc(zeroed, 1)
            pool.wait_ge(zeroed, 1)
            pool.affine_select(out=ident[:], in_=ident[:], compare_op=ALU.not_equal, fill=1.0, base=0,
                               pattern=[[-1, P]], channel_multiplier=1).then_inc(ident_ready, 1)

            def split_low(u, slot):
                pool.wait_ge(w_hi, 2 * u + 2)
                pool.tensor_tensor(w13s[:, slot, 1], wstage[:, slot, 0:2], w13s[:, slot, 0].bitcast(F32),
                                   ALU.subtract).then_inc(w_lo, 1)
                pool.tensor_tensor(w2s[:, slot, 1], wstage[:, slot, 2], w2s[:, slot, 0].bitcast(F32), ALU.subtract)\
                    .then_inc(w_lo, 1)

            def step(u, slot):
                for n in range(NU):
                    pool.wait_ge(y_hi, NU * u + n + 1)
                    pool.tensor_tensor(ys[:, n % 4, 1], y[:, n % 2], ys[:, n % 4, 0].bitcast(F32), ALU.subtract)\
                        .then_inc(y_lo, 1)
                    if n == 3 and not (isinstance(u, int) and u == NPAIRS - 1):
                        split_low(u + 1, 1 - slot)

            split_low(0, 0)
            steps(pool, step)

        @block.scalar
        def _(act):
            def split(slot, round_):
                if round_ is not None:
                    act.wait_ge(w_loaded[slot], 48 * round_)
                act.activation(w13s[:, slot, 0], wstage[:, slot, 0:2], ACT.Copy).then_inc(w_hi, 1)
                act.activation(w2s[:, slot, 0], wstage[:, slot, 2], ACT.Copy).then_inc(w_hi, 1)

            def step(u, slot, next_round, shared=False, last=False):
                for n in range(NU):
                    r = n % 2
                    act.wait_ge(up_psum, NU * u + n + 1)
                    if shared:
                        if n >= 2:
                            act.wait_ge(y_ready, n - 1)
                        act.activation(h1[:, r], ps[:, 3 * r], ACT.Silu).then_inc(h1_copied, 1)
                    else:
                        act.activation(h1[:, r], ps[:, 3 * r], ACT.Copy).then_inc(h1_copied, 1)
                        act.wait_ge(gate_done, NU * (u - 1) + n + 1)
                        act.activation(act_h[:, r], gate[:, r], ACT.Silu).then_inc(silu_done, 1)
                    act.wait_ge(y_ready, NU * u + n + 1)
                    if not (shared and n < 4):
                        act.wait_ge(y_used, NU * u + n - 3)
                    act.activation(ys[:, n % 4, 0], y[:, r], ACT.Copy).then_inc(y_hi, 1)
                    if n == 3 and not last:
                        if not shared:
                            act.wait_ge(y_used, NU * u)
                        split(1 - slot, next_round)

            split(0, None)
            step(0, 0, None, shared=True)
            with act.Fori(0, LOOPS) as k:
                step(2 * k + 1, 1, k + 1)
                step(2 * k + 2, 0, k + 1)
            step(NPAIRS - 1, 1, None, last=True)

        @block.vector
        def _(dve):
            def accumulate(c, chunk):
                dve.wait_ge(half_psum, c + 1)
                dve.tensor_tensor(acc[:, 0, bass.ts(chunk, T)], ps[:, SUM_BANKS[chunk % 2][0]], acc[:, 0, bass.ts(chunk, T)], ALU.add)\
                    .then_inc(acc_done, 1)
                dve.wait_ge(y_used, 2 * c + 2)
                dve.tensor_tensor(acc[:, 1, bass.ts(chunk, T)], ps[:, SUM_BANKS[chunk % 2][1]], acc[:, 1, bass.ts(chunk, T)], ALU.add)\
                    .then_inc(acc_done, 1)

            def step(u, slot, routed_round):
                shared = isinstance(u, int) and u == 0
                for n in range(NU):
                    r = n % 2
                    dve.wait_ge(h1_copied, NU * u + n + 1)
                    if shared:
                        if n >= 2:
                            dve.wait_ge(y_lo, n - 1)
                        dve.tensor_tensor(y[:, r], ps[:, 3 * r + 1], h1[:, r], ALU.mult).then_inc(y_ready, 1)
                    else:
                        dve.tensor_tensor(gate[:, r], ps[:, 3 * r + 1], h1[:, r], ALU.mult).then_inc(gate_done, 1)
                        if n == 0:
                            dve.wait_ge(routing_loaded[slot], 32 * routed_round)
                        dve.wait_ge(y_lo, NU * u + n - 1)
                        dve.wait_ge(silu_done, NU * (u - 1) + n + 1)
                        tokens = bass.ts(n // 2, T)
                        dve.tensor_tensor(y[:, r], routing[:, slot, n % 2, tokens], act_h[:, r], ALU.mult)\
                            .then_inc(y_ready, 1)
                    if n % 2 and not (shared and n == 1):
                        c = n // 2 - 1
                        if c < 0:
                            accumulate(B * u - 1, B - 1)
                        else:
                            accumulate(B * u + c, c)

            dve.memset(acc[:], 0.0).then_inc(acc_zeroed, 1)
            dve.wait_ge(acc_zeroed, 1)
            step(0, 0, None)
            with dve.Fori(0, LOOPS) as k:
                step(2 * k + 1, 1, k + 1)
                step(2 * k + 2, 0, k + 1)
            step(NPAIRS - 1, 1, LOOPS + 1)
            accumulate(B * NPAIRS - 1, B - 1)
            dve.wait_ge(x3_loaded, 16)
            for c in range(B):
                dve.wait_ge(acc_turned, c + 1)
                rows = x3[:, TJ * c:TJ * (c + 1)]
                at = 3 * (c % 2)
                dve.tensor_tensor(rows, ps[:, at:at + 2].rearrange("p a (j n) -> p (a j) n", j=2), rows, ALU.add)\
                    .then_inc(summed, 1)

        @block.tensor
        def _(pe):
            def up(u, slot, n):
                r, c, s = n % 2, n // 2, n % 2
                shared = isinstance(u, int) and u == 0
                if not (shared and n < 2):
                    pe.wait_ge(y_ready, NU * u + n - 1)
                if n == 0:
                    pe.wait_ge(w_hi, 2 * u + 2)
                    pe.wait_ge(w_lo, 2 * u + 2)
                for k in range(2):
                    terms = [(l, q, kh) for kh in range(KH) for l, q in ((0, 0), (1, 0), (0, 1))]
                    for i, (l, q, kh) in enumerate(terms):
                        mm = pe.matmul(ps[:, 3 * r + k], w13s[:, slot, l, k, kh, P * s:P * (s + 1)],
                                       xt4[:, 2 * KH * c + KH * q + kh], start=i == 0, stop=i == len(terms) - 1)
                mm.then_inc(up_psum, 1)

            def down(u, slot, n):
                c, s = n // 2, n % 2
                shared = isinstance(u, int) and u == 0
                if s == 0 and not (shared and c < 2):
                    pe.wait_ge(acc_done, 2 * (B * u + c - 1))
                pe.wait_ge(y_lo, NU * u + n + 1)
                for half in range(KH):
                    for l, q in ((0, 0), (1, 0), (0, 1)):
                        mm = pe.matmul(ps[:, SUM_BANKS[c % 2][half]], w2s[:, slot, l, s, P * half:P * (half + 1)], ys[:, n % 4, q],
                                       start=s == 0 and l == 0 and q == 0, stop=s == 1 and q == 1)
                    if s == 1 and half == 0:
                        mm.then_inc(half_psum, 1)
                mm.then_inc(y_used, 1)

            def step(u, slot):
                shared = isinstance(u, int) and u == 0
                for n in range(NU):
                    up(u, slot, n)
                    if n >= 2:
                        down(u, slot, n - 2)
                    elif not shared:
                        down(u - 1, 1 - slot, NU - 2 + n)

            steps(pe, step)
            down(NPAIRS - 1, 1, NU - 2)
            down(NPAIRS - 1, 1, NU - 1)
            pe.wait_ge(ident_ready, 1)
            for c in range(B):
                pe.wait_ge(acc_done, 2 * (B * (NPAIRS - 1) + c + 1))
                if c == 0:
                    pe.wait_ge(y_ready, NU * NPAIRS)
                if c >= 2:
                    pe.wait_ge(summed, c - 1)
                for j in range(TJ):
                    for half in range(KH):
                        at = D * (j % 2) + P * half
                        first = T * c + P * j
                        mm = pe.transpose(ps[:, 3 * (c % 2) + j // 2, at:at + P], acc[:, half, first:first + P],
                                          ident[:])
                mm.then_inc(acc_turned, 1)


def program(nc, t, out):
    x3_d = nc.dram_tensor("x3_kept", [NTOK, D], F32).ap()
    routing_d = nc.dram_tensor("routing_kept", [HID // GROUP, NTOK], F32).ap()
    with ExitStack() as ctx:
        with nc.sbuf_tensor("stage", [P, 2, 2048], F32) as stage, nc.sbuf_tensor("below", [P, 2, 2048], BF16) as below, \
                nc.sbuf_tensor("absout", [P, 2048], BF16) as absout:
            pass
        xt4 = ctx.enter_context(nc.sbuf_tensor("xt4", [P, B * 2 * KH, T], F32R))
        with nc.sbuf_tensor("wstage", [P, 2, 3, 2, PAIR], F32) as wstage:
            pass
        big = ctx.enter_context(nc.sbuf_tensor("big", [P, 8192], F32R))
        kept = ctx.enter_context(nc.semaphore("kept"))
        layers(nc, t["x"], t["wqkv0"], t["wo0"], t["w_up"], t["w_gate"], t["w_down"], t["wqkv1"], t["bqk1"], t["bv1"],
               t["wo1"], t["bo1"], t["gate_w"], t["gate_b"], t["w1"], t["w3"], t["w2"], x3_d, routing_d,
               stage, below, absout, xt4, big, wstage, kept)
        experts(nc, t["w1"], t["w3"], t["w2"], x3_d, routing_d, xt4, wstage, kept, out)


def kernel(**inputs):
    import numpy as np
    import concourse.bacc as bacc
    from concourse.bass_utils import run_bass_kernel_spmd as run

    a = {k: np.asarray(v) for k, v in inputs.items()}

    def padded(shared, axis):
        fill = [(0, 0), (0, 0)]
        fill[axis] = (0, PAIR - EH)
        return np.pad(shared, fill)

    def by_input(routed):
        return routed.transpose(1, 0, 2).reshape(D, HID)

    wqkv1, bqkv1 = a["L1_attn_w_qkv"], a["L1_attn_b_qkv"]
    arrays = {
        "x": a["L0_attn_x"].reshape(NTOK, D),
        "wqkv0": np.concatenate([a["L0_attn_Wq"].T, a["L0_attn_Wk"].T, a["L0_attn_Wv"].T], 1),
        "wo0": a["L0_attn_Wo"].T,
        "w_up": a["L0_ffn_W_up"].T,
        "w_gate": a["L0_ffn_W_gate"].T,
        "w_down": a["L0_ffn_W_down"].T,
        "wqkv1": wqkv1.T,
        "bqk1": bqkv1[0:2 * D].reshape(4, P).T,
        "bv1": bqkv1[2 * D:3 * D].reshape(2, P).T,
        "wo1": a["L1_attn_w_out"].T,
        "bo1": a["L1_attn_b_out"].reshape(1, D),
        "gate_w": a["L1_ffn_gate_w"].T,
        "gate_b": a["L1_ffn_gate_b"].reshape(1, NE),
        "w1": np.concatenate([padded(a["L1_ffn_w1_shared"], 1), by_input(a["L1_ffn_w1_routed"])], 1),
        "w3": np.concatenate([padded(a["L1_ffn_w3_shared"], 1), by_input(a["L1_ffn_w3_routed"])], 1),
        "w2": np.concatenate([padded(a["L1_ffn_w2_shared"], 0), a["L1_ffn_w2_routed"].reshape(HID, D)], 0),
    }
    arrays = {k: np.ascontiguousarray(v) for k, v in arrays.items()}
    nc = bacc.Bacc("TRN2", target_bir_lowering=False, num_devices=1)
    t = {k: nc.dram_tensor(k + "_in", v.shape, F32, kind="ExternalInput").ap() for k, v in arrays.items()}
    out = nc.dram_tensor("out", [NTOK, D], F32, kind="ExternalOutput").ap()
    program(nc, t, out)
    r = run(nc, [{k + "_in": v for k, v in arrays.items()}], core_ids=[0])
    return r.results[0]["out"].reshape(B, T, D)
```
